# Optimizing a Trainium2 kernel written in Bass

```python
import numpy as np
import jax
import jax.numpy as jnp

def _softmax(x, axis=-1):
    return jax.nn.softmax(x, axis=axis)

def _gelu(x):
    return jax.nn.gelu(x, approximate=True)

def _silu(x):
    return jax.nn.silu(x)

def _sigmoid(x):
    return jax.nn.sigmoid(x)

def _layernorm(x, axis=-1, eps=1e-05):
    m = jnp.mean(x, axis=axis, keepdims=True)
    v = jnp.var(x, axis=axis, keepdims=True)
    return (x - m) / jnp.sqrt(v + eps)

def _scatter_add(tgt, idx, src, axis=0):
    return tgt.at[idx].add(src)

def _segment_sum(src, seg, n):
    return jax.ops.segment_sum(src, seg, n)
kernel_name = 'mk_adaln_d2_jaxref_r8_ef5b47'

def setup_inputs(seed: int=0):
    np.random.seed(seed)
    _w = jnp.asarray

    def _L0_attn_setup():
        import jax, jax.numpy as jnp
        import numpy as np
        D_MODEL = 128
        N_HEADS = 16
        HEAD_DIM = D_MODEL // N_HEADS
        KV_LATENT = 32
        LN_EPS = 1e-05

        def apply_rope(x):
            b, h, t, d = x.shape
            half = d // 2
            pos = jnp.arange(t, dtype=x.dtype)[:, None]
            inv_freq = 1.0 / 10000.0 ** (jnp.arange(half, dtype=x.dtype) / half)
            angles = pos * inv_freq[None, :]
            sin = jnp.sin(angles)[None, None]
            cos = jnp.cos(angles)[None, None]
            x1, x2 = (x[..., :half], x[..., half:])
            return jnp.concatenate([x1 * cos - x2 * sin, x1 * sin + x2 * cos], axis=-1)
        key = jax.random.key(seed)
        ks = jax.random.split(key, 6)
        d, L = (D_MODEL, KV_LATENT)
        s = 1.0 / np.sqrt(d)
        sl = 1.0 / np.sqrt(L)
        return {'x': jax.random.normal(ks[0], (2, 256, d), dtype=jnp.float32), 'W_q': jax.random.uniform(ks[1], (d, d), jnp.float32, -s, s), 'W_dkv': jax.random.uniform(ks[2], (d, L), jnp.float32, -s, s), 'W_uk': jax.random.uniform(ks[3], (L, d), jnp.float32, -sl, sl), 'W_uv': jax.random.uniform(ks[4], (L, d), jnp.float32, -sl, sl), 'W_o': jax.random.uniform(ks[5], (d, d), jnp.float32, -s, s), 'ln_gamma': jnp.ones((L,), jnp.float32), 'ln_beta': jnp.zeros((L,), jnp.float32)}
    _L0_attn_in = _L0_attn_setup()

    def _L0_ffn_setup():
        import jax, jax.numpy as jnp
        import numpy as np
        HIDDEN = 128
        NUM_EXPERTS = 8
        TOP_K = 2
        B, S = (4, 128)
        key = jax.random.key(seed)
        ks = jax.random.split(key, 8)
        H, E = (HIDDEN, NUM_EXPERTS)
        sc = lambda fan_in: 1.0 / np.sqrt(fan_in)
        x = jax.random.normal(ks[0], (B, S, H), dtype=jnp.float32)
        Wr = jax.random.uniform(ks[1], (H, E), minval=-sc(H), maxval=sc(H), dtype=jnp.float32)
        br = jax.random.uniform(ks[2], (E,), minval=-sc(H), maxval=sc(H), dtype=jnp.float32)
        W1 = jax.random.uniform(ks[3], (E, H, 2 * H), minval=-sc(H), maxval=sc(H), dtype=jnp.float32)
        b1 = jax.random.uniform(ks[4], (E, 2 * H), minval=-sc(H), maxval=sc(H), dtype=jnp.float32)
        W2 = jax.random.uniform(ks[5], (E, 2 * H, H), minval=-sc(2 * H), maxval=sc(2 * H), dtype=jnp.float32)
        b2 = jax.random.uniform(ks[6], (E, H), minval=-sc(2 * H), maxval=sc(2 * H), dtype=jnp.float32)
        return {'x': x, 'Wr': Wr, 'br': br, 'W1': W1, 'b1': b1, 'W2': W2, 'b2': b2}
    _L0_ffn_in = _L0_ffn_setup()
    _L0_c = _w((lambda *s: np.random.randn(*s).astype(np.float32) * 0.05)(4, 128))
    _L0_wmod = _w((lambda *s: np.random.randn(*s).astype(np.float32) * 0.05)(128, 6 * 128) * 128 ** (-0.5))

    def _L1_attn_setup():
        import jax, jax.numpy as jnp
        import numpy as np
        B, T, C, H = (2, 256, 128, 16)
        R = 32
        LORA_SCALE = 0.5
        HD = C // H

        def lora_linear(x, w, b, la, lb):
            return x @ w.T + b + LORA_SCALE * (x @ la.T @ lb.T)
        key = jax.random.key(seed)
        ks = jax.random.split(key, 8)
        std = 0.02
        return {'x': jax.random.normal(ks[0], (B, T, C), jnp.float32), 'w_attn': jax.random.normal(ks[1], (3 * C, C), jnp.float32) * std, 'b_attn': jnp.zeros((3 * C,), jnp.float32), 'la_attn': jax.random.normal(ks[2], (R, C), jnp.float32) * std, 'lb_attn': jax.random.normal(ks[3], (3 * C, R), jnp.float32) * std, 'w_proj': jax.random.normal(ks[4], (C, C), jnp.float32) * std, 'b_proj': jnp.zeros((C,), jnp.float32), 'la_proj': jax.random.normal(ks[5], (R, C), jnp.float32) * std, 'lb_proj': jax.random.normal(ks[6], (C, R), jnp.float32) * std}
    _L1_attn_in = _L1_attn_setup()

    def _L1_ffn_setup():
        import jax, jax.numpy as jnp
        import numpy as np
        K = 2
        CAP_FACTOR = 1.25
        key = jax.random.key(seed)
        ks = jax.random.split(key, 6)
        B, T, C, H, E = (8, 256, 128, 512, 8)
        return {'x': jax.random.normal(ks[0], (B, T, C), dtype=jnp.float32), 'Wr': jax.random.normal(ks[1], (C, E), dtype=jnp.float32) * 0.02, 'W1': jax.random.normal(ks[2], (E, C, H), dtype=jnp.float32) * 0.02, 'b1': jax.random.normal(ks[3], (E, H), dtype=jnp.float32) * 0.02, 'W2': jax.random.normal(ks[4], (E, H, C), dtype=jnp.float32) * 0.02, 'b2': jax.random.normal(ks[5], (E, C), dtype=jnp.float32) * 0.02}
    _L1_ffn_in = _L1_ffn_setup()
    _L1_c = _w((lambda *s: np.random.randn(*s).astype(np.float32) * 0.05)(4, 128))
    _L1_wmod = _w((lambda *s: np.random.randn(*s).astype(np.float32) * 0.05)(128, 6 * 128) * 128 ** (-0.5))
    _d = {'L0_attn_x': _L0_attn_in['x'], 'L0_attn_W_q': _L0_attn_in['W_q'], 'L0_attn_W_dkv': _L0_attn_in['W_dkv'], 'L0_attn_W_uk': _L0_attn_in['W_uk'], 'L0_attn_W_uv': _L0_attn_in['W_uv'], 'L0_attn_W_o': _L0_attn_in['W_o'], 'L0_attn_ln_gamma': _L0_attn_in['ln_gamma'], 'L0_attn_ln_beta': _L0_attn_in['ln_beta'], 'L0_ffn_Wr': _L0_ffn_in['Wr'], 'L0_ffn_br': _L0_ffn_in['br'], 'L0_ffn_W1': _L0_ffn_in['W1'], 'L0_ffn_b1': _L0_ffn_in['b1'], 'L0_ffn_W2': _L0_ffn_in['W2'], 'L0_ffn_b2': _L0_ffn_in['b2'], 'L0_c': _L0_c, 'L0_wmod': _L0_wmod, 'L1_attn_w_attn': _L1_attn_in['w_attn'], 'L1_attn_b_attn': _L1_attn_in['b_attn'], 'L1_attn_la_attn': _L1_attn_in['la_attn'], 'L1_attn_lb_attn': _L1_attn_in['lb_attn'], 'L1_attn_w_proj': _L1_attn_in['w_proj'], 'L1_attn_b_proj': _L1_attn_in['b_proj'], 'L1_attn_la_proj': _L1_attn_in['la_proj'], 'L1_attn_lb_proj': _L1_attn_in['lb_proj'], 'L1_ffn_Wr': _L1_ffn_in['Wr'], 'L1_ffn_W1': _L1_ffn_in['W1'], 'L1_ffn_b1': _L1_ffn_in['b1'], 'L1_ffn_W2': _L1_ffn_in['W2'], 'L1_ffn_b2': _L1_ffn_in['b2'], 'L1_c': _L1_c, 'L1_wmod': _L1_wmod}
    _x0 = _d['L0_attn_x']
    _d['L0_attn_x'] = jax.random.normal(jax.random.fold_in(jax.random.key(seed), 1), (4, 512, 128), dtype=_x0.dtype)
    del _x0
    return _d

def reference(L0_attn_x, L0_attn_W_q, L0_attn_W_dkv, L0_attn_W_uk, L0_attn_W_uv, L0_attn_W_o, L0_attn_ln_gamma, L0_attn_ln_beta, L0_ffn_Wr, L0_ffn_br, L0_ffn_W1, L0_ffn_b1, L0_ffn_W2, L0_ffn_b2, L0_c, L0_wmod, L1_attn_w_attn, L1_attn_b_attn, L1_attn_la_attn, L1_attn_lb_attn, L1_attn_w_proj, L1_attn_b_proj, L1_attn_la_proj, L1_attn_lb_proj, L1_ffn_Wr, L1_ffn_W1, L1_ffn_b1, L1_ffn_W2, L1_ffn_b2, L1_c, L1_wmod):

    def _L0_attn_ref(x, W_q, W_dkv, W_uk, W_uv, W_o, ln_gamma, ln_beta):
        import jax, jax.numpy as jnp
        import numpy as np
        D_MODEL = 128
        N_HEADS = 16
        HEAD_DIM = D_MODEL // N_HEADS
        KV_LATENT = 32
        LN_EPS = 1e-05

        def apply_rope(x):
            b, h, t, d = x.shape
            half = d // 2
            pos = jnp.arange(t, dtype=x.dtype)[:, None]
            inv_freq = 1.0 / 10000.0 ** (jnp.arange(half, dtype=x.dtype) / half)
            angles = pos * inv_freq[None, :]
            sin = jnp.sin(angles)[None, None]
            cos = jnp.cos(angles)[None, None]
            x1, x2 = (x[..., :half], x[..., half:])
            return jnp.concatenate([x1 * cos - x2 * sin, x1 * sin + x2 * cos], axis=-1)
        b, t, _ = x.shape
        q = (x @ W_q).reshape(b, t, N_HEADS, HEAD_DIM).transpose(0, 2, 1, 3)
        lat = x @ W_dkv
        mu = jnp.mean(lat, axis=-1, keepdims=True)
        var = jnp.mean(jnp.square(lat - mu), axis=-1, keepdims=True)
        lat = (lat - mu) * jax.lax.rsqrt(var + LN_EPS) * ln_gamma + ln_beta
        k = (lat @ W_uk).reshape(b, t, N_HEADS, HEAD_DIM).transpose(0, 2, 1, 3)
        v = (lat @ W_uv).reshape(b, t, N_HEADS, HEAD_DIM).transpose(0, 2, 1, 3)
        q = apply_rope(q)
        k = apply_rope(k)
        scores = jnp.einsum('bhqd,bhkd->bhqk', q, k) / jnp.sqrt(jnp.float32(HEAD_DIM))
        causal = jnp.tril(jnp.ones((t, t), dtype=bool))
        scores = jnp.where(causal[None, None], scores, -jnp.inf)
        attn = jax.nn.softmax(scores, axis=-1)
        out = jnp.einsum('bhqk,bhkd->bhqd', attn, v)
        out = out.transpose(0, 2, 1, 3).reshape(b, t, D_MODEL)
        return out @ W_o

    def _L0_ffn_ref(x, Wr, br, W1, b1, W2, b2):
        import jax, jax.numpy as jnp
        import numpy as np
        HIDDEN = 128
        NUM_EXPERTS = 8
        TOP_K = 2
        B, S = (4, 128)
        B_, S_, H = x.shape
        xf = x.reshape(-1, H)
        logits = xf @ Wr + br
        topk_w, topk_idx = jax.lax.top_k(logits, TOP_K)
        topk_w = jax.nn.softmax(topk_w, axis=-1)
        gate = jnp.sum(jax.nn.one_hot(topk_idx, NUM_EXPERTS, dtype=xf.dtype) * topk_w[..., None], axis=1)
        h = jax.nn.relu(jnp.einsum('th,ehf->etf', xf, W1) + b1[:, None, :])
        y = jnp.einsum('etf,efh->eth', h, W2) + b2[:, None, :]
        out = jnp.einsum('te,eth->th', gate, y)
        return out.reshape(B_, S_, H)

    def _L1_attn_ref(x, w_attn, b_attn, la_attn, lb_attn, w_proj, b_proj, la_proj, lb_proj):
        import jax, jax.numpy as jnp
        import numpy as np
        B, T, C, H = (2, 256, 128, 16)
        R = 32
        LORA_SCALE = 0.5
        HD = C // H

        def lora_linear(x, w, b, la, lb):
            return x @ w.T + b + LORA_SCALE * (x @ la.T @ lb.T)
        Bsz, Tlen, Cdim = x.shape
        qkv = lora_linear(x, w_attn, b_attn, la_attn, lb_attn)
        q, k, v = jnp.split(qkv, 3, axis=2)
        rs = lambda t: t.reshape(Bsz, Tlen, H, HD).transpose(0, 2, 1, 3)
        q, k, v = (rs(q), rs(k), rs(v))
        att = jnp.einsum('bhqd,bhkd->bhqk', q, k) * (1.0 / np.sqrt(HD))
        causal = jnp.tril(jnp.ones((Tlen, Tlen), dtype=bool))
        att = jnp.where(causal[None, None], att, -jnp.inf)
        att = jax.nn.softmax(att, axis=-1)
        y = jnp.einsum('bhqk,bhkd->bhqd', att, v)
        y = y.transpose(0, 2, 1, 3).reshape(Bsz, Tlen, Cdim)
        return lora_linear(y, w_proj, b_proj, la_proj, lb_proj)

    def _L1_ffn_ref(x, Wr, W1, b1, W2, b2):
        import jax, jax.numpy as jnp
        import numpy as np
        K = 2
        CAP_FACTOR = 1.25
        B, T, C = x.shape
        E = Wr.shape[1]
        capacity = int(T / E * CAP_FACTOR)
        probs = jax.nn.softmax(x @ Wr, axis=-1)
        topk_probs, topk_experts = jax.lax.top_k(probs, K)
        S = T * K
        e_flat = topk_experts.reshape(B, S)
        p_flat = topk_probs.reshape(B, S)
        x_rep = jnp.repeat(x, K, axis=1)
        onehot = jax.nn.one_hot(e_flat, E, dtype=jnp.int32)
        pos_all = jnp.cumsum(onehot, axis=1) - onehot
        pos = jnp.take_along_axis(pos_all, e_flat[..., None], axis=-1)[..., 0]
        keep = pos < capacity
        pos_c = jnp.minimum(pos, capacity - 1)
        b_idx = jnp.broadcast_to(jnp.arange(B)[:, None], (B, S))
        buf = jnp.zeros((E, B, capacity, C), dtype=x.dtype)
        buf = buf.at[e_flat, b_idx, pos_c].add(x_rep * keep[..., None].astype(x.dtype))
        h = jax.nn.relu(jnp.einsum('ebnc,ech->ebnh', buf, W1) + b1[:, None, None, :])
        y = jnp.einsum('ebnh,ehc->ebnc', h, W2) + b2[:, None, None, :]
        y_tok = y[e_flat, b_idx, pos_c]
        y_tok = y_tok * keep[..., None].astype(x.dtype) * p_flat[..., None]
        out = y_tok.reshape(B, T, K, C).sum(axis=2)
        return out
    x = L0_attn_x
    mod = (_silu(L0_c) @ L0_wmod).reshape(L0_c.shape[0], 6, 1, -1)
    sa, ca, ga, sb, cb, gb = (mod[:, 0], mod[:, 1], mod[:, 2], mod[:, 3], mod[:, 4], mod[:, 5])
    ga = (2 * (ga >= 0) - 1) * jnp.maximum(jnp.abs(ga), 0.25)
    gb = (2 * (gb >= 0) - 1) * jnp.maximum(jnp.abs(gb), 0.25)
    h = _layernorm(x, axis=-1) * (1 + ca) + sa
    x = x + ga * _L0_attn_ref(h, L0_attn_W_q, L0_attn_W_dkv, L0_attn_W_uk, L0_attn_W_uv, L0_attn_W_o, L0_attn_ln_gamma, L0_attn_ln_beta)
    h = _layernorm(x, axis=-1) * (1 + cb) + sb
    x = x + gb * _L0_ffn_ref(h, L0_ffn_Wr, L0_ffn_br, L0_ffn_W1, L0_ffn_b1, L0_ffn_W2, L0_ffn_b2)
    mod = (_silu(L1_c) @ L1_wmod).reshape(L1_c.shape[0], 6, 1, -1)
    sa, ca, ga, sb, cb, gb = (mod[:, 0], mod[:, 1], mod[:, 2], mod[:, 3], mod[:, 4], mod[:, 5])
    ga = (2 * (ga >= 0) - 1) * jnp.maximum(jnp.abs(ga), 0.25)
    gb = (2 * (gb >= 0) - 1) * jnp.maximum(jnp.abs(gb), 0.25)
    h = _layernorm(x, axis=-1) * (1 + ca) + sa
    x = x + ga * _L1_attn_ref(h, L1_attn_w_attn, L1_attn_b_attn, L1_attn_la_attn, L1_attn_lb_attn, L1_attn_w_proj, L1_attn_b_proj, L1_attn_la_proj, L1_attn_lb_proj)
    h = _layernorm(x, axis=-1) * (1 + cb) + sb
    x = x + gb * _L1_ffn_ref(h, L1_ffn_Wr, L1_ffn_W1, L1_ffn_b1, L1_ffn_W2, L1_ffn_b2)
    return x

_drawn_inputs = setup_inputs


def setup_inputs(seed=0):
    import zlib

    import numpy as np

    out = dict(_drawn_inputs(seed))
    spreads = {'L0_attn_ln_gamma': (1.0, 0.6),
     'L0_attn_ln_beta': (0.0, 0.712),
     'L1_attn_b_attn': (0.0, 0.8),
     'L1_attn_b_proj': (0.0, 0.335)}
    factors = {'L0_attn_W_q': 8.0,
     'L0_attn_W_dkv': 4.953,
     'L0_attn_W_uk': 8.0,
     'L0_attn_W_uv': 3.601,
     'L0_attn_W_o': 3.604,
     'L0_ffn_br': 5.948,
     'L0_ffn_b1': 8.0,
     'L0_ffn_b2': 8.0,
     'L1_attn_w_attn': 8.0,
     'L1_attn_la_attn': 8.0,
     'L1_attn_lb_attn': 8.0,
     'L1_attn_w_proj': 8.0,
     'L1_attn_la_proj': 8.0,
     'L1_attn_lb_proj': 8.0,
     'L1_ffn_Wr': 8.0,
     'L1_ffn_W1': 8.0,
     'L1_ffn_b1': 27.636,
     'L1_ffn_W2': 8.0,
     'L1_ffn_b2': 64.0}
    for name, (base, spread) in spreads.items():
        noise = np.random.default_rng([zlib.crc32(name.encode()), seed]).standard_normal(out[name].shape)
        drawn = base * np.exp(spread * noise) if base else spread * noise
        out[name] = jnp.asarray(drawn.astype(out[name].dtype))
    for name, factor in factors.items():
        out[name] = (out[name] * factor).astype(out[name].dtype)
    return out
```

```python
from contextlib import ExitStack

import numpy as np
import concourse.bass as bass
from concourse import mybir

ALU = mybir.AluOpType
ACT = mybir.ActivationFunctionType
AX = mybir.AxisListType.X
F32 = mybir.dt.float32
BF16 = mybir.dt.bfloat16
U32 = mybir.dt.uint32

LAYERS = 2
B, T, C = 4, 512, 128
P = 128
NI = T // P
NT = B * NI
NH, HD = 16, 8
GH = 4
NG = NH // GH
STEPS = B * NG
LAT = 32
RANK = 32
NE = 8
FC = (2, 4)
CAPACITY = int(T / NE * 1.25)
EPS = 1e-5
SCALE = 1.0 / float(np.sqrt(HD))
MASKED = -1e30
VW = HD + 1
VROW = NH * VW + 32 - VW
Q_PARTS = (0, 1, 0, 1, 0, 2)
K_PARTS = (0, 1, 1, 0, 2, 0)
MAX_ROW = HD * len(Q_PARTS)
HALF = 64
P_SLOTS = 20
ST_UNITS = 10
PAIR_UNITS = (((0, 0, 0),), ((0, 1, 0), (0, 3, 384)), ((1, 0, 0),), ((1, 1, 0), (1, 3, 384)),
              ((0, 2, 0), (1, 2, 256)))


def build(nc, a, out):
    with ExitStack() as ctx:
        def sb(name, shape, dt=F32):
            return ctx.enter_context(nc.sbuf_tensor(name, shape, dt))

        def sem(name):
            return ctx.enter_context(nc.semaphore(name))

        x = sb("x", [P, NT, C])
        xn = sb("xn", [P, NT, C])
        acc = xn
        hT = sb("hT", [P, B * T])
        ident = sb("ident", [P, P])
        identb = sb("identb", [P, P], BF16)
        mask_q = sb("mask_q", [P, P], BF16)
        mask_k = sb("mask_k", [P, P], BF16)
        before = sb("before", [P, P], BF16)
        ones = sb("ones", [P, P], BF16)
        onesf = sb("onesf", [1, P])
        tail_q = sb("tail_q", [P, T], BF16)
        tail_k = sb("tail_k", [P, T], BF16)
        cosT = sb("cosT", [P, T])
        sinT = sb("sinT", [P, T])
        cT = sb("cT", [P, LAYERS * B])
        silu = sb("silu", [P, 3, LAYERS * B])
        modT = sb("modT", [P, LAYERS, 6, B])
        gates = sb("gates", [P, LAYERS * B, 2, C])
        wq = sb("wq", [P, 2, C])
        wuk = sb("wuk", [LAT, 2, C])
        wuv = sb("wuv", [LAT, C])
        wdkv = sb("wdkv", [P, LAT])
        lnlat = sb("lnlat", [LAT, 2])
        wqkv = sb("wqkv", [P, 3 * C])
        la_attn = sb("la_attn", [RANK, C])
        lb_attn = sb("lb_attn", [RANK, 3 * C])
        la_proj = sb("la_proj", [RANK, C])
        lb_proj = sb("lb_proj", [RANK, C])
        bqk = sb("bqk", [P, 2])
        bv = sb("bv", [P, C])
        bproj = sb("bproj", [1, C])
        wo = sb("wo", [P, LAYERS, C])
        wr = sb("wr", [P, LAYERS, NE])
        br = sb("br", [P, NE])
        w1 = sb("w1", [P, NE * FC[1] * P])
        w2 = sb("w2", [P, NE * FC[1] * C])
        b1 = [sb(f"b1_{L}", [P, NE, FC[L]]) for L in range(LAYERS)]
        b2 = sb("b2", [NE, LAYERS, C])
        negh = sb("negh", [P, NI])
        iota8 = sb("iota8", [P, NE])
        stats = sb("stats", [P, B, NI, 6])
        mv = sb("mv", [P, B, NI, 2])
        ve = sb("ve", [P, B, NI])
        rstd = sb("rstd", [P, B, NI])
        parts = sb("parts", [P, 2, 3, T], BF16)
        latn = sb("latn", [P, NI, LAT])
        vaug = sb("vaug", [P, NT, VROW])
        qop = sb("qop", [P, 2, NH // 2, T], BF16)
        kop = sb("kop", [P, 2, NH, T], BF16)
        negmax = sb("negmax", [P, 2, NI * 2, 2])
        mres = sb("mres", [P, NI * 2, 2])
        mparts = sb("mparts", [P, 2, NI * 2, 3, 2], BF16)
        mT = sb("mT", [48, 2, P], BF16)
        pw = sb("pw", [P, P_SLOTS, T])
        wmod = pw[:, 0:3, :].rearrange("p a (b n) -> p (a b n)", b=1).rearrange("p (l n) -> p l n", l=LAYERS)
        silu_bc = pw[:, 3:5, :].rearrange("p a (m n) -> p (a m) n", n=P)
        latT = pw[0:LAT, 5, :]
        rot, full = pw[:, 6:8, :], pw[:, 8:10, :]
        gsign, gabs = (t.rearrange("p a (m j c) -> p (a m) j c", m=2, j=2) for t in (rot, full))
        gT = pw[0:NE, P_SLOTS - 4:P_SLOTS, :].rearrange("p a n -> p (a n)")
        oT4 = sb("oT4", [P, 2, T])
        rec = sb("rec", [P, NI, GH])
        o_nat = sb("o_nat", [P, 2, NI, C])
        oT = sb("oT", [P, T])
        upd = sb("upd", [P, NI, C])
        lg = sb("lg", [P, NT, NE])
        lgs = sb("lgs", [P, NT, NE])
        ex = sb("ex", [P, NT, NE])
        top = sb("top", [P, NT, 8])
        topi = sb("topi", [P, NT, 8], U32)
        topf = sb("topf", [P, NT, 2])
        wk = sb("wk", [P, 4, NT])
        oh = sb("oh", [P, 2, NT, NE])
        gate = sb("gate", [P, NT, NE])
        sel = sb("sel", [P, NT, NE], BF16)

        bank = [ctx.enter_context(nc.psum_tensor(f"bank{i}", [P, 512], F32)) for i in range(3)]
        pair = [ctx.enter_context(nc.psum_tensor(f"pair{i}", [P, 2, 512], F32)) for i in range(2)]
        pvb = ctx.enter_context(nc.psum_tensor("pvb", [P, 512], F32))

        scr_q = nc.dram_tensor("scr_q", (B, NH, HALF, T), BF16, kind="Internal").ap()
        scr_k = nc.dram_tensor("scr_k", (B, NH, HALF, T), BF16, kind="Internal").ap()
        scr_m = nc.dram_tensor("scr_m", (B, NG, 48, P), BF16, kind="Internal").ap()

        ld_x = [sem(f"ld_x{b}") for b in range(B)]
        ld_small, ld_attn, ld_moe = sem("ld_small"), sem("ld_attn"), sem("ld_moe")
        tails, pool_init = sem("tails"), sem("pool_init")
        act_silu, dve_silu, setup = sem("act_silu"), sem("dve_silu"), sem("setup")
        pair_full = sem("pair_full")
        bank_full, bank_free = sem("bank_full"), sem("bank_free")
        ln_stat, ln_mv, ln_ve, ln_rstd = sem("ln_stat"), sem("ln_mv"), sem("ln_ve"), sem("ln_rstd")
        ln_xn, h_ready = sem("ln_xn"), sem("h_ready")
        lat_ready, rotated, biased = sem("lat_ready"), sem("rotated"), sem("biased")
        split, v_ready = sem("split"), sem("v_ready")
        scr_done = [[sem(f"scr_{n}{b}") for b in range(B)] for n in "qk"]
        op_loaded = [[sem(f"op_loaded{i}_{g}") for g in range(NG)] for i in range(2)]
        reduced, msplit, m_copied = sem("reduced"), sem("msplit"), sem("m_copied")
        m_out, m_in = [sem(f"m_out{g}") for g in range(NG)], [sem(f"m_in{g}") for g in range(NG)]
        pv_done, pv_copied = sem("pv_done"), sem("pv_copied")
        o_step, oT_ready, gated, x_done = sem("o_step"), sem("oT_ready"), sem("gated"), sem("x_done")
        logits_read, route, exp_in, exp_out = sem("logits_read"), sem("route"), sem("exp_in"), sem("exp_out")
        chosen, gate_ready, gT_ready, acc_step = sem("chosen"), sem("gate_ready"), sem("gT_ready"), sem("acc_step")
        stored = sem("stored")

        BANKS = [0, STEPS * ST_UNITS + NE * B * FC[0]]
        REDUCTIONS = (1, 3, 4, 6, 7)
        ACC = 2 + NE * NT

        SMALL = ["ident", "identb", "mask_q", "mask_k", "before", "ones", "tail_q", "tail_k", "cosT", "sinT",
                 "cT", "iota8"]
        smalls = dict(ident=ident, identb=identb, mask_q=mask_q, mask_k=mask_k, before=before, ones=ones,
                      tail_q=tail_q, tail_k=tail_k, cosT=cosT, sinT=sinT, cT=cT, iota8=iota8)
        n_small = 16 * (len(SMALL) + LAYERS)

        wq_in = a["L0_attn_W_q"]
        attn_loads = [
            (wq[:, 0, :], wq_in), (wuk[:, 0, :], a["L0_attn_W_uk"]), (wuv[:], a["L0_attn_W_uv"]),
            (wdkv[:], a["L0_attn_W_dkv"]), (lnlat[:], a["lnlat"]), (wqkv[:], a["w_attnT"]),
            (la_attn[:], a["L1_attn_la_attn"]), (lb_attn[:], a["lb_attnT"]), (la_proj[:], a["L1_attn_la_proj"]),
            (lb_proj[:], a["lb_projT"]), (bqk[:], a["bqk"]), (bv[:], a["bv"]), (bproj[:], a["bproj"]),
            (wo[:, 0, :], a["L0_attn_W_o"]), (wo[:, 1, :], a["w_projT"]), (wr[:, 0, :], a["L0_ffn_Wr"]),
            (wr[:, 1, :], a["L1_ffn_Wr"]), (br[:], a["br"]), (b1[0][:], a["b1_0"]), (b1[1][:], a["b1_1"]),
            (b2[:, 0, :], a["L0_ffn_b2"]), (b2[:, 1, :], a["L1_ffn_b2"]),
        ]
        n_attn = 16 * len(attn_loads)

        def w1_view(L):
            return w1[:, 0:NE * FC[L] * P].rearrange("p (e n) -> p e n", e=NE)

        def w2_view(L):
            return w2[:, 0:NE * FC[L] * C].rearrange("p (e k n) -> p e k n", e=NE, k=FC[L])

        block = ctx.enter_context(nc.Block())

        @block.sync
        def _(sp):
            xv = a["L0_attn_x"].rearrange("b (i p) c -> b p i c", p=P)
            sp.dma_start(x[:, 0:NI, :], xv[0]).then_inc(ld_x[0], 16)
            for n in SMALL:
                sp.dma_start(smalls[n][:], a[n]).then_inc(ld_small, 16)
            for L in range(LAYERS):
                sp.dma_start(wmod[:, L, :], a[f"L{L}_wmod"]).then_inc(ld_small, 16)
            for b in range(1, B):
                sp.dma_start(x[:, b * NI:(b + 1) * NI, :], xv[b]).then_inc(ld_x[b], 16)
            for dst, src in attn_loads:
                sp.dma_start(dst, src).then_inc(ld_attn, 16)
            sp.wait_ge(ld_small, n_small)
            for b in range(B):
                for tile_, scr in ((tail_q, scr_q), (tail_k, scr_k)):
                    for h0 in (0, NH // 2):
                        sp.dma_start(scr[b, h0:h0 + NH // 2, MAX_ROW:HALF, :], tile_[:]).then_inc(tails, 16)

            def load_experts(L):
                sp.dma_start(w1_view(L), a[f"L{L}_ffn_W1"].rearrange("e p n -> p e n")).then_inc(ld_moe, 16)
                for e in range(NE):
                    sp.dma_start(w2_view(L)[:, e], a[f"L{L}_ffn_W2"][e].rearrange("(k p) n -> p k n", p=P))\
                      .then_inc(ld_moe, 16)

            load_experts(0)

            def write_parts(L, b):
                for n, (scr, order) in enumerate(((scr_q, Q_PARTS), (scr_k, K_PARTS))):
                    sp.wait_ge(split, 8 * (L * B + b) + 4 * (n + 1))
                    for r, part in enumerate(order):
                        sp.dma_start(scr[b, :, r * HD:(r + 1) * HD, :], parts[:, n, part, :])\
                          .then_inc(scr_done[n][b], 16)

            def load_operands(L, s):
                b, g = divmod(s, NG)
                gs = L * STEPS + s
                if gs >= 2 * NG:
                    Lo, so = divmod(gs - 2 * NG, STEPS)
                    sp.wait_ge(bank_full, BANKS[Lo] + (so + 1) * ST_UNITS)
                if g == 0:
                    sp.wait_ge(scr_done[0][b], 96 * (L + 1))
                    sp.wait_ge(scr_done[1][b], 96 * (L + 1))
                for par in range(2):
                    heads = slice(g * GH + par, (g + 1) * GH, 2)
                    rows = slice(par * HALF, (par + 1) * HALF)
                    sp.dma_start(qop[rows, b % 2, 2 * g:2 * g + 2, :], scr_q[b, heads].rearrange("h r t -> r h t"))\
                      .then_inc(op_loaded[b % 2][g], 16)
                    sp.dma_start(kop[rows, b % 2, heads, :], scr_k[b, heads].rearrange("h r t -> r h t"))\
                      .then_inc(op_loaded[b % 2][g], 16)

            for L in range(LAYERS):
                for b in range(B):
                    write_parts(L, b)
                if L == 0:
                    sp.wait_ge(tails, 16 * 4 * B)
                    sp.wait_ge(pool_init, 4)
                for s in range(STEPS):
                    load_operands(L, s)
                if L == 0:
                    sp.wait_ge(acc_step, ACC)
                    load_experts(1)
            ov = out.rearrange("b (i p) c -> b p i c", p=P)
            for b in range(B):
                sp.wait_ge(x_done, (2 * LAYERS - 1) * B + b + 1)
                sp.dma_start(ov[b], x[:, b * NI:(b + 1) * NI, :]).then_inc(stored, 16)
            sp.wait_ge(stored, 16 * B)

        @block.gpsimd
        def _(pool):
            nc.gpsimd.memset(kop[:, 0, :, :], 0.0).then_inc(pool_init, 1)
            nc.gpsimd.memset(kop[:, 1, :, :], 0.0).then_inc(pool_init, 1)
            nc.gpsimd.memset(vaug[:], 1.0).then_inc(pool_init, 1)
            nc.gpsimd.memset(negh[:], -0.5).then_inc(pool_init, 1)
            nc.gpsimd.memset(onesf[:], 1.0).then_inc(pool_init, 1)
            pool.wait_ge(pool_init, 5)
            rs = [0]

            def inv_std(b):
                rs[0] += 1
                pool.wait_ge(ln_mv, NI * rs[0])
                nc.gpsimd.tensor_scalar(ve[:, b, :], mv[:, b, :, 1], EPS, None, ALU.add).then_inc(ln_ve, 1)
                pool.wait_ge(ln_ve, rs[0])
                nc.gpsimd.tensor_tensor(rstd[:, b, :], ve[:, b, :], negh[:], ALU.pow).then_inc(ln_rstd, 1)

            for L in range(LAYERS):
                for b in range(B):
                    inv_std(b)
                if L == 0:
                    for b in range(B):
                        inv_std(b)
                for s in range(STEPS):
                    b, g = divmod(s, NG)
                    gs = L * STEPS + s
                    pool.wait_ge(m_copied, gs + 1)
                    pool.dma_start(scr_m[b, g], mT[:, s % 2, :]).then_inc(m_out[g], 16)
                    pool.wait_ge(m_out[g], 16 * (L * B + b + 1))
                    src = scr_m[b, g].rearrange("(i r part j) q -> r part j i q", i=NI, r=2, part=3)
                    for par in range(2):
                        row = par * HALF + MAX_ROW
                        for j in range(2):
                            pool.dma_start(qop[row:row + 3, b % 2, 2 * g + j, :].rearrange("p (i q) -> p i q", i=NI),
                                           src[par][:, j]).then_inc(m_in[g], 16)
                for b in range(B):
                    inv_std(b)

        @block.scalar
        def _(act):
            act.wait_ge(ld_small, n_small)
            nc.scalar.activation(silu[:, 0, :], cT[:], ACT.Exp, scale=-1.0).then_inc(act_silu, 1)
            nb = [0]

            def next_bank():
                nb[0] += 1
                act.wait_ge(bank_full, nb[0])
                return bank[(nb[0] - 1) % 3]

            for L in range(LAYERS):
                def pv_copy(s):
                    gs = L * STEPS + s
                    act.wait_ge(pv_done, gs + 1)
                    if gs >= 2:
                        act.wait_ge(o_step, 2 * (gs - 1))
                    nc.scalar.activation(oT4[:, gs % 2, :], pvb[:], ACT.Copy).then_inc(pv_copied, 1)

                for s in range(STEPS):
                    gs = L * STEPS + s
                    for u in range(ST_UNITS):
                        src = next_bank()
                        if u == 0 and gs >= 2:
                            act.wait_ge(pv_done, gs - 1)
                        slot = (s % 2) * ST_UNITS + u
                        nc.scalar.activation(pw[:, slot, :], src[:], ACT.Exp, scale=SCALE).then_inc(bank_free, 1)
                        if u == 6 and s:
                            pv_copy(s - 1)
                pv_copy(STEPS - 1)

                act.wait_ge(exp_in, L + 1)
                if L == 0:
                    nc.scalar.activation(wk[:, 1, :], wk[:, 0, :], ACT.Exp).then_inc(exp_out, 1)
                else:
                    nc.scalar.activation(ex[:], lgs[:], ACT.Exp).then_inc(exp_out, 1)

                act.wait_ge(ld_attn, n_attn)
                for n in range(NE * B):
                    e, b = divmod(n, B)
                    for f in range(FC[L]):
                        src = next_bank()
                        if n >= 4 and f == 0:
                            act.wait_ge(acc_step, L * ACC + 2 + NI * (n - 3))
                        dst = pw[:, (n % 4) * FC[L] + f, :]
                        nc.scalar.activation(dst, src[:], ACT.Relu, bias=b1[L][:, e, f:f + 1]).then_inc(bank_free, 1)

        @block.tensor
        def _(pe):
            np_, nb = [0], [0]

            readers = [None, None]

            def next_pair(*reader):
                n = np_[0]
                np_[0] += 1
                if readers[n % 2]:
                    pe.wait_ge(*readers[n % 2])
                readers[n % 2] = reader
                return pair[n % 2]

            def next_bank():
                n = nb[0]
                nb[0] += 1
                if n >= 3:
                    pe.wait_ge(bank_free, n - 2)
                return bank[n % 3]

            mm = nc.tensor.matmul

            pe.wait_ge(ld_small, n_small)
            pe.wait_ge(dve_silu, 4)
            u = next_pair(setup, 1)
            for L in range(LAYERS):
                for j in range(6):
                    last = mm(u[:, 0, L * 24 + j * B:L * 24 + (j + 1) * B], wmod[:, L, j * C:(j + 1) * C],
                              silu[:, 2, L * B:(L + 1) * B], start=True, stop=True)
            last.then_inc(pair_full, 1)
            for L in range(LAYERS):
                u = next_pair(setup, 4 + 4 * L)
                gw = wmod[:, L, :].rearrange("p (j k c) -> p k j c", j=2, k=3)[:, 2]
                for b in range(B):
                    last = mm(u[:, b // 2, (b % 2) * 256:(b % 2 + 1) * 256], silu_bc[:, L * B + b, :], gw,
                              start=True, stop=True)
                last.then_inc(pair_full, 1)
            pe.wait_ge(ld_attn, n_attn)
            u = next_pair(setup, 12)
            mm(u[:, 0, 0:3 * C], la_attn[:], lb_attn[:], start=True, stop=True)
            mm(u[:, 1, 0:C], la_proj[:], lb_proj[:], start=True, stop=True).then_inc(pair_full, 1)

            def turn_rows(n, b):
                u = next_pair(h_ready, n + 1)
                pe.wait_ge(ln_xn, NI * (n + 1))
                for i in range(NI):
                    last = nc.tensor.transpose(u[:, 0, i * P:(i + 1) * P], xn[:, b * NI + i, :], ident[:])
                last.then_inc(pair_full, 1)

            for L in range(LAYERS):
                for b in range(B):
                    turn_rows(2 * L * B + b, b)

                if L == 0:
                    pe.wait_ge(setup, SETUP)
                for b in range(B):
                    pe.wait_ge(h_ready, 2 * L * B + b + 1)
                    hb = hT[:, b * T:(b + 1) * T]
                    if L == 0:
                        u = next_pair(rotated, 6 * b + 2)
                        for v in range(2):
                            last = mm(u[:, v, :], wq[:, v, :], hb, start=True, stop=True)
                        last.then_inc(pair_full, 1)
                        u = next_pair(lat_ready, (NI + 1) * b + NI)
                        for i in range(NI):
                            last = mm(u[:, 0, i * LAT:(i + 1) * LAT], hb[:, i * P:(i + 1) * P], wdkv[:],
                                      start=True, stop=True)
                        last.then_inc(pair_full, 1)
                        u = next_pair(lat_ready, (NI + 1) * (b + 1))
                        pe.wait_ge(lat_ready, (NI + 1) * b + NI)
                        for i in range(NI):
                            last = nc.tensor.transpose(u[0:LAT, 0, i * P:(i + 1) * P], latn[:, i, :], ident[:])
                        last.then_inc(pair_full, 1)
                        u = next_pair(rotated, 6 * b + 5)
                        pe.wait_ge(lat_ready, (NI + 1) * (b + 1))
                        for v in range(2):
                            last = mm(u[:, v, :], wuk[:, v, :], latT[:], start=True, stop=True)
                        last.then_inc(pair_full, 1)
                        u = next_pair(v_ready, NI * (b + 1))
                        for i in range(NI):
                            last = mm(u[:, 0, i * C:(i + 1) * C], latT[:, i * P:(i + 1) * P], wuv[:],
                                      start=True, stop=True)
                        last.then_inc(pair_full, 1)
                    else:
                        u = next_pair(biased, 2 * (b + 1))
                        for v in range(2):
                            last = mm(u[:, v, :], wqkv[:, v * C:(v + 1) * C], hb, start=True, stop=True)
                        last.then_inc(pair_full, 1)
                        u = next_pair(v_ready, NI * (B + b + 1))
                        for i in range(NI):
                            last = mm(u[:, 0, i * C:(i + 1) * C], hb[:, i * P:(i + 1) * P], wqkv[:, 2 * C:3 * C],
                                      start=True, stop=True)
                        last.then_inc(pair_full, 1)

                def scores_q(s, k):
                    b, g = divmod(s, NG)
                    if k == 0:
                        pe.wait_ge(op_loaded[b % 2][g], 64 * (L * 2 + b // 2 + 1))
                    u = next_pair(reduced, 7 * (L * STEPS + s) + REDUCTIONS[k])
                    if k < 4:
                        pr, tiles = k // 2, ((3, 0),) if k % 2 == 0 else ((2, 0), (0, 384))
                        jobs = [(2 * pr + v, v, i, c0) for v in range(2) for i, c0 in tiles]
                    else:
                        jobs = [(h, h // 2, 1, (h % 2) * 256) for h in range(GH)]
                    for h, v, i, c0 in jobs:
                        head = g * GH + h
                        n = (i + 1) * P
                        mm(u[:, v, c0:c0 + n], qop[:, b % 2, head // 2, i * P:(i + 1) * P],
                           kop[:, b % 2, head, 0:n], start=True, stop=False)
                        last = mm(u[:, v, c0 + i * P:c0 + n], identb[:], mask_q[:], start=False, stop=True)
                    last.then_inc(pair_full, 1)

                def scores_k(s, k):
                    b, g = divmod(s, NG)
                    if k == 0:
                        pe.wait_ge(m_in[g], 64 * (L * B + b + 1))
                    dst = next_bank()
                    pr, k2 = divmod(k, 5)
                    for hh, j, c0 in PAIR_UNITS[k2]:
                        head = g * GH + 2 * pr + hh
                        n = T - j * P
                        mm(dst[:, c0:c0 + n], kop[:, b % 2, head, j * P:(j + 1) * P],
                           qop[:, b % 2, head // 2, j * P:T], start=True, stop=False)
                        last = mm(dst[:, c0:c0 + P], identb[:], mask_k[:], start=False, stop=True)
                    last.then_inc(bank_full, 1)

                def turn_max(s):
                    u = next_pair(m_copied, L * STEPS + s + 1)
                    pe.wait_ge(msplit, 4 * (L * STEPS + s + 1))
                    tb = u[0:48, 0, :].bitcast(BF16)[:, 0:P]
                    nc.tensor.transpose(tb, mparts[:, s % 2].rearrange("p a b c -> p (a b c)"), identb[:])\
                        .then_inc(pair_full, 1)

                def weighted_values(s):
                    b, g = divmod(s, NG)
                    gs = L * STEPS + s
                    if gs >= 1:
                        pe.wait_ge(pv_copied, gs)
                    pe.wait_ge(bank_free, unit_base + (s + 1) * ST_UNITS)
                    where = {}
                    for pr in range(2):
                        for k2, unit in enumerate(PAIR_UNITS):
                            for hh, j, c0 in unit:
                                where[2 * pr + hh, j] = ((s % 2) * ST_UNITS + 5 * pr + k2, c0)
                    for j in range(NI):
                        for h in range(GH):
                            slot, c0 = where[h, j]
                            col = (g * GH + h) * VW
                            last = mm(pvb[32 * h:32 * h + 32, j * P:T], vaug[:, b * NI + j, col:col + 32],
                                      pw[:, slot, c0:c0 + T - j * P], start=(j == 0), stop=(j == NI - 1))
                    last.then_inc(pv_done, 1)

                def turn_group(s):
                    gs = L * STEPS + s
                    u = next_pair(o_step, 2 * (gs + 1))
                    pe.wait_ge(pv_copied, gs + 1)
                    for i in range(NI):
                        last = nc.tensor.transpose(u[:, 0, i * P:(i + 1) * P], oT4[:, gs % 2, i * P:(i + 1) * P],
                                                   ident[:])
                    last.then_inc(pair_full, 1)

                def turn_output(b):
                    u = next_pair(oT_ready, L * B + b + 1)
                    pe.wait_ge(o_step, 2 * (L * STEPS + (b + 1) * NG))
                    for i in range(NI):
                        last = nc.tensor.transpose(u[:, 0, i * P:(i + 1) * P], o_nat[:, b % 2, i, :], ident[:])
                    last.then_inc(pair_full, 1)

                def project(b):
                    u = next_pair(gated, 2 * L * B + b + 1)
                    pe.wait_ge(oT_ready, L * B + b + 1)
                    for i in range(NI):
                        dst = u[:, 0, i * C:(i + 1) * C]
                        last = mm(dst, oT[:, i * P:(i + 1) * P], wo[:, L, :], start=True, stop=(L == 0))
                        if L == 1:
                            last = mm(dst, onesf[:], bproj[:], start=False, stop=True)
                    last.then_inc(pair_full, 1)

                unit_base = nb[0]
                if L == 0:
                    pe.wait_ge(pool_init, 5)
                pe.wait_ge(v_ready, NI * (L + 1) * B)
                for s in range(NG):
                    for k in range(5):
                        scores_q(s, k)
                    if s:
                        turn_max(s - 1)
                for s in range(STEPS):
                    for k in range(ST_UNITS):
                        scores_k(s, k)
                        if k % 2 and s + NG < STEPS:
                            scores_q(s + NG, k // 2)
                        if k == 4 and s:
                            weighted_values(s - 1)
                    if s + NG - 1 < STEPS:
                        turn_max(s + NG - 1)
                    if s:
                        turn_group(s - 1)
                    if s % NG == 1 and s > NG:
                        turn_output(s // NG - 1)
                    if s % NG == 2 and s > NG:
                        project(s // NG - 1)
                weighted_values(STEPS - 1)
                turn_group(STEPS - 1)
                turn_output(B - 1)
                project(B - 1)

                for b in range(B):
                    turn_rows((2 * L + 1) * B + b, b)

                u = next_pair(logits_read, L + 1)
                pe.wait_ge(h_ready, (2 * L + 2) * B)
                for t in range(NT):
                    last = mm(u[:, 0, t * NE:(t + 1) * NE], hT[:, t * P:(t + 1) * P], wr[:, L, :],
                              start=True, stop=True)
                last.then_inc(pair_full, 1)
                if L == 1:
                    u = next_pair(gate_ready, 2)
                    pe.wait_ge(chosen, 1)
                    for t in range(NT):
                        b, i = divmod(t, NI)
                        dst = u[:, 0, t * NE:(t + 1) * NE]
                        last = mm(dst, before[:], sel[:, t, :], start=True, stop=(i == 0))
                        for k in range(i):
                            last = mm(dst, ones[:], sel[:, b * NI + k, :], start=False, stop=(k == i - 1))
                    last.then_inc(pair_full, 1)
                for half in range(2):
                    u = next_pair(gT_ready, 2 * L + half + 1)
                    pe.wait_ge(gate_ready, L + 1)
                    for k in range(NT // 2):
                        last = nc.tensor.transpose(u[0:NE, k // 4, (k % 4) * P:(k % 4 + 1) * P],
                                                   gate[:, half * NT // 2 + k, :], ident[:])
                    last.then_inc(pair_full, 1)
                for half in range(2):
                    u = next_pair(acc_step, L * ACC + half + 1)
                    pe.wait_ge(gT_ready, 2 * L + 1 + half)
                    for k in range(NT // 2):
                        t = half * NT // 2 + k
                        last = mm(u[:, k // 4, (k % 4) * C:(k % 4 + 1) * C], gT[:, t * P:(t + 1) * P],
                                  b2[:, L, :], start=True, stop=True)
                    last.then_inc(pair_full, 1)

                def hidden(n):
                    e, b = divmod(n, B)
                    for f in range(FC[L]):
                        dst = next_bank()
                        mm(dst[:], w1_view(L)[:, e, f * P:(f + 1) * P], hT[:, b * T:(b + 1) * T],
                           start=True, stop=True).then_inc(bank_full, 1)

                def outputs(n, hid_base):
                    e, b = divmod(n, B)
                    u = next_pair(acc_step, L * ACC + 2 + NI * (n + 1))
                    pe.wait_ge(bank_free, hid_base + (n + 1) * FC[L])
                    for i in range(NI):
                        for f in range(FC[L]):
                            last = mm(u[:, 0, i * C:(i + 1) * C],
                                      pw[:, (n % 4) * FC[L] + f, i * P:(i + 1) * P],
                                      w2_view(L)[:, e, f, :], start=(f == 0), stop=(f == FC[L] - 1))
                    last.then_inc(pair_full, 1)

                pe.wait_ge(ld_moe, 16 * (NE + 1) * (L + 1))
                hid_base = nb[0]
                hidden(0)
                for n in range(NE * B):
                    if n + 1 < NE * B:
                        hidden(n + 1)
                    outputs(n, hid_base)

        @block.vector
        def _(v):
            V = nc.vector
            npair = [0]

            def next_pair():
                n = npair[0]
                npair[0] += 1
                v.wait_ge(pair_full, n + 1)
                return pair[n % 2]

            v.wait_ge(act_silu, 1)
            V.tensor_scalar(silu[:, 1, :], silu[:, 0, :], 1.0, None, ALU.add).then_inc(dve_silu, 1)
            v.wait_ge(dve_silu, 1)
            V.reciprocal(silu[:, 0, :], silu[:, 1, :]).then_inc(dve_silu, 1)
            v.wait_ge(dve_silu, 2)
            V.tensor_tensor(silu[:, 2, :], cT[:], silu[:, 0, :], ALU.mult).then_inc(dve_silu, 1)
            v.wait_ge(dve_silu, 3)
            V.tensor_copy(silu_bc[:], silu[:, 2, :].unsqueeze(2).to_broadcast([P, LAYERS * B, P]))\
                .then_inc(dve_silu, 1)
            ns = [0]

            def step(ins):
                ns[0] += 1
                ins.then_inc(setup, 1)

            u = next_pair()
            step(V.tensor_copy(modT[:], u[:, 0, 0:48].rearrange("p (l j b) -> p l j b", l=LAYERS, j=6)))
            v.wait_ge(setup, 1)
            step(V.tensor_scalar(modT[:, :, 1::3, :], modT[:, :, 1::3, :], 1.0, None, ALU.add))
            for L in range(LAYERS):
                u = next_pair()
                uv = u[:].rearrange("p a (b j c) -> p (a b) j c", b=2, j=2)
                v.wait_ge(setup, ns[0])
                step(V.tensor_scalar(gsign[:], uv, 0.0, 2.0, ALU.is_ge, ALU.mult))
                v.wait_ge(setup, ns[0])
                step(V.scalar_tensor_tensor(out=gabs[:], in0=gsign[:], scalar=-1.0, in1=uv,
                                            op0=ALU.add, op1=ALU.mult))
                v.wait_ge(setup, ns[0])
                step(V.tensor_scalar(gabs[:], gabs[:], 0.25, None, ALU.max))
                v.wait_ge(setup, ns[0])
                step(V.scalar_tensor_tensor(out=gates[:, L * B:(L + 1) * B], in0=gsign[:], scalar=-1.0,
                                            in1=gabs[:], op0=ALU.add, op1=ALU.mult))
            u = next_pair()
            v.wait_ge(ld_attn, n_attn)
            step(V.scalar_tensor_tensor(out=wqkv[:], in0=u[:, 0, 0:3 * C], scalar=0.5, in1=wqkv[:],
                                        op0=ALU.mult, op1=ALU.add))
            step(V.scalar_tensor_tensor(out=wo[:, 1, :], in0=u[:, 1, 0:C], scalar=0.5, in1=wo[:, 1, :],
                                        op0=ALU.mult, op1=ALU.add))
            for w in (wq, wuk):
                half = HD // 2
                wv = w[:].rearrange("p v (h s k) -> p v h s k", s=2, k=half)
                for s_ in range(2):
                    step(V.tensor_copy(wv[:, 1, :, s_, :], wv[:, 0, :, 1 - s_, :]))
            v.wait_ge(setup, ns[0])
            assert ns[0] == SETUP

            nstat, nxn, nlat = [0], [0], [0]

            def statistics(src, b, width):
                n = nstat[0]
                nstat[0] += 1
                if n >= B:
                    v.wait_ge(ln_mv, NI * (n - B + 1))
                    v.wait_ge(ln_xn, nxn[0])
                    if nlat[0]:
                        v.wait_ge(lat_ready, nlat[0])
                for i in range(NI):
                    V.bn_stats(stats[:, b, i, :], src(i)).then_inc(ln_stat, 1)
                v.wait_ge(ln_stat, NI * (n + 1))
                for i in range(NI):
                    V.bn_aggr(mv[:, b, i, :], stats[:, b, i, :]).then_inc(ln_mv, 1)
                return n + 1

            def norm_rows(n, b):
                for i in range(NI):
                    t = b * NI + i
                    V.tensor_scalar(xn[:, t, :], x[:, t, :], mv[:, b, i, 0:1], rstd[:, b, i:i + 1],
                                    ALU.subtract, ALU.mult).then_inc(ln_xn, 1)
                nxn[0] += NI

            def modulate(n, L, half, b):
                u = next_pair()
                V.tensor_scalar(hT[:, b * T:(b + 1) * T], u[:, 0, :], modT[:, L, 3 * half + 1, b:b + 1],
                                modT[:, L, 3 * half, b:b + 1], ALU.mult, ALU.add).then_inc(h_ready, 1)

            def layer_norm(L, half):
                base = (2 * L + half) * B
                done = []
                for b in range(B):
                    if base == 0:
                        v.wait_ge(ld_x[b], 16)
                    else:
                        v.wait_ge(x_done, base - B + b + 1)
                    done.append(statistics(lambda i: x[:, b * NI + i, :], b, C))
                for b in range(B):
                    v.wait_ge(ln_rstd, done[b])
                    norm_rows(base + b, b)
                for b in range(B):
                    modulate(base + b, L, half, b)

            nsplit = [0]

            def split_parts(L, b, n):
                base = 8 * (L * B + b) + 4 * n
                if L * B + b:
                    pb = (b - 1) % B
                    v.wait_ge(scr_done[n][pb], 96 * (L + (b > 0)))
                src = full[:, n, :]
                V.tensor_copy(parts[:, n, 0, :], src).then_inc(split, 1)
                v.wait_ge(split, base + 1)
                V.tensor_tensor(rot[:, n, :], src, parts[:, n, 0, :], ALU.subtract).then_inc(split, 1)
                v.wait_ge(split, base + 2)
                V.tensor_copy(parts[:, n, 1, :], rot[:, n, :]).then_inc(split, 1)
                v.wait_ge(split, base + 3)
                V.tensor_tensor(parts[:, n, 2, :], rot[:, n, :], parts[:, n, 1, :], ALU.subtract).then_inc(split, 1)

            def rotate(b, n):
                u = next_pair()
                done = 6 * b + 3 * n
                if b or n:
                    v.wait_ge(split, 8 * b + 4 * n)
                V.tensor_tensor(rot[:, 0, :], u[:, 0, :], cosT[:], ALU.mult).then_inc(rotated, 1)
                V.tensor_tensor(rot[:, 1, :], u[:, 1, :], sinT[:], ALU.mult).then_inc(rotated, 1)
                v.wait_ge(rotated, done + 2)
                V.tensor_tensor(full[:, n, :], rot[:, 0, :], rot[:, 1, :], ALU.add).then_inc(rotated, 1)
                v.wait_ge(rotated, done + 3)

            def values(b, bias):
                u = next_pair()
                dst = vaug[:, b * NI:(b + 1) * NI, 0:NH * VW].rearrange("p i (h k) -> p i h k", k=VW)[:, :, :, 0:HD]
                src = u[:, 0, :].rearrange("p (i h k) -> p i h k", i=NI, h=NH)
                for i in range(NI):
                    if bias is None:
                        V.tensor_copy(dst[:, i], src[:, i]).then_inc(v_ready, 1)
                    else:
                        V.tensor_tensor(dst[:, i], src[:, i], bias.rearrange("p (h k) -> p h k", k=HD), ALU.add)\
                            .then_inc(v_ready, 1)

            for L in range(LAYERS):
                layer_norm(L, 0)
                if L == 0:
                    v.wait_ge(pool_init, 5)
                for b in range(B):
                    if L == 0:
                        rotate(b, 0)
                        split_parts(L, b, 0)
                        u = next_pair()
                        n = statistics(lambda i: u[:, 0, i * LAT:(i + 1) * LAT], b, LAT)
                        v.wait_ge(ln_rstd, n)
                        for i in range(NI):
                            V.tensor_scalar(latn[:, i, :], u[:, 0, i * LAT:(i + 1) * LAT], mv[:, b, i, 0:1],
                                            rstd[:, b, i:i + 1], ALU.subtract, ALU.mult).then_inc(lat_ready, 1)
                        nlat[0] += NI
                        u = next_pair()
                        V.tensor_scalar(latT[:], u[0:LAT, 0, :], lnlat[:, 0:1], lnlat[:, 1:2],
                                        ALU.mult, ALU.add).then_inc(lat_ready, 1)
                        nlat[0] += 1
                        rotate(b, 1)
                        split_parts(L, b, 1)
                        values(b, None)
                    else:
                        u = next_pair()
                        v.wait_ge(split, 8 * (L * B + b))
                        for n in range(2):
                            V.tensor_scalar(full[:, n, :], u[:, n, :], bqk[:, n:n + 1], None, ALU.add)\
                                .then_inc(biased, 1)
                        v.wait_ge(biased, 2 * (b + 1))
                        split_parts(L, b, 0)
                        split_parts(L, b, 1)
                        values(b, bv[:])

                def maxima(s, k):
                    u = next_pair()
                    nm = negmax[:, s % 2].rearrange("p (i r) j -> p i r j", r=2)
                    if k == 0 and L * STEPS + s >= 2:
                        v.wait_ge(msplit, 4 * (L * STEPS + s - 1))
                    pr = k // 2
                    if k == 4:
                        V.tensor_reduce(nm[:, 1].rearrange("p r j -> p j r"),
                                        u[:].rearrange("p j (r n) -> p j r n", r=2), AX, ALU.max, negate=True)\
                            .then_inc(reduced, 1)
                    elif k % 2 == 0:
                        V.tensor_reduce(nm[:, 3, :, pr], u[:], AX, ALU.max, negate=True).then_inc(reduced, 1)
                    else:
                        V.tensor_reduce(nm[:, 2, :, pr], u[:, :, 0:384], AX, ALU.max, negate=True)\
                            .then_inc(reduced, 1)
                        V.tensor_reduce(nm[:, 0, :, pr], u[:, :, 384:512], AX, ALU.max, negate=True)\
                            .then_inc(reduced, 1)

                def split_max(s):
                    gs = L * STEPS + s
                    v.wait_ge(reduced, 7 * (gs + 1))
                    if gs:
                        v.wait_ge(msplit, 4 * gs)
                    src, dst = negmax[:, s % 2], mparts[:, s % 2]
                    V.tensor_copy(dst[:, :, 0, :], src).then_inc(msplit, 1)
                    v.wait_ge(msplit, 4 * gs + 1)
                    V.tensor_tensor(mres[:], src, dst[:, :, 0, :], ALU.subtract).then_inc(msplit, 1)
                    v.wait_ge(msplit, 4 * gs + 2)
                    V.tensor_copy(dst[:, :, 1, :], mres[:]).then_inc(msplit, 1)
                    v.wait_ge(msplit, 4 * gs + 3)
                    V.tensor_tensor(dst[:, :, 2, :], mres[:], dst[:, :, 1, :], ALU.subtract).then_inc(msplit, 1)

                def copy_max(s):
                    gs = L * STEPS + s
                    u = next_pair()
                    if gs >= 2:
                        gp = gs - 2
                        v.wait_ge(m_out[gp % NG], 16 * (gp // NG + 1))
                    V.tensor_copy(mT[:, s % 2, :], u[0:48, 0, :].bitcast(BF16)[:, 0:P]).then_inc(m_copied, 1)

                def normalise(s):
                    gs = L * STEPS + s
                    b, g = divmod(s, NG)
                    u = next_pair()
                    uv = u[:, 0, :].rearrange("p (i h k) -> p i h k", i=NI, h=GH)
                    if gs:
                        v.wait_ge(o_step, 2 * gs)
                    V.reciprocal(rec[:], uv[:, :, :, HD]).then_inc(o_step, 1)
                    v.wait_ge(o_step, 2 * gs + 1)
                    dst = o_nat[:, b % 2, :, g * GH * HD:(g + 1) * GH * HD].rearrange("p i (h k) -> p i h k", h=GH)
                    V.tensor_tensor(dst, uv[:, :, :, 0:HD], rec[:].unsqueeze(3).to_broadcast([P, NI, GH, HD]),
                                    ALU.mult).then_inc(o_step, 1)

                def copy_output(b):
                    u = next_pair()
                    V.tensor_copy(oT[:], u[:, 0, :]).then_inc(oT_ready, 1)

                def residual(src, half, b):
                    n = (2 * L + half) * B + b + 1
                    gb = gates[:, L * B + b, half, :].unsqueeze(1).to_broadcast([P, NI, C])
                    if n > 1:
                        v.wait_ge(x_done, n - 1)
                    V.tensor_tensor(upd[:], src, gb, ALU.mult).then_inc(gated, 1)
                    v.wait_ge(gated, n)
                    xb = x[:, b * NI:(b + 1) * NI, :]
                    V.tensor_tensor(xb, xb, upd[:], ALU.add).then_inc(x_done, 1)

                def attn_residual(b):
                    u = next_pair()
                    residual(u[:, 0, :].rearrange("p (i c) -> p i c", i=NI), 0, b)

                for s in range(NG):
                    for k in range(5):
                        maxima(s, k)
                    split_max(s)
                    if s:
                        copy_max(s - 1)
                for s in range(STEPS):
                    if s + NG < STEPS:
                        for k in range(5):
                            maxima(s + NG, k)
                        split_max(s + NG)
                    if s + NG - 1 < STEPS:
                        copy_max(s + NG - 1)
                    if s:
                        normalise(s - 1)
                    if s % NG == 1 and s > NG:
                        copy_output(s // NG - 1)
                    if s % NG == 2 and s > NG:
                        attn_residual(s // NG - 1)
                normalise(STEPS - 1)
                copy_output(B - 1)
                attn_residual(B - 1)

                layer_norm(L, 1)

                def r(ins):
                    nroute[0] += 1
                    ins.then_inc(route, 1)
                    v.wait_ge(route, nroute[0])

                if L == 0:
                    nroute = [0]
                u = next_pair()
                lgp = u[:, 0, 0:NT * NE].rearrange("p (t e) -> p t e", e=NE)
                if L == 0:
                    V.tensor_tensor(lg[:], lgp, br[:].unsqueeze(1).to_broadcast([P, NT, NE]), ALU.add)\
                        .then_inc(logits_read, 1)
                else:
                    V.tensor_copy(lg[:], lgp).then_inc(logits_read, 1)
                v.wait_ge(logits_read, L + 1)

                def bc(col):
                    return col.unsqueeze(2).to_broadcast([P, NT, NE])

                if L == 1:
                    r(V.tensor_reduce(wk[:, 0, :], lg[:], AX, ALU.max))
                    V.tensor_tensor(lgs[:], lg[:], bc(wk[:, 0, :]), ALU.subtract).then_inc(exp_in, 1)
                    v.wait_ge(exp_out, 2)
                    r(V.tensor_reduce(wk[:, 1, :], ex[:], AX, ALU.add))
                    r(V.reciprocal(wk[:, 2, :], wk[:, 1, :]))
                    r(V.tensor_tensor(lg[:], ex[:], bc(wk[:, 2, :]), ALU.mult))
                for t in range(NT):
                    V.max(top[:, t, :], lg[:, t, :]).then_inc(route, 1)
                nroute[0] += NT
                v.wait_ge(route, nroute[0])
                for t in range(NT):
                    V.max_index(topi[:, t, :], top[:, t, :], lg[:, t, :]).then_inc(route, 1)
                nroute[0] += NT
                v.wait_ge(route, nroute[0])
                r(V.tensor_copy(topf[:], topi[:, :, 0:2]))
                if L == 0:
                    V.tensor_tensor(wk[:, 0, :], top[:, :, 1], top[:, :, 0], ALU.subtract).then_inc(exp_in, 1)
                    v.wait_ge(exp_out, 1)
                    r(V.tensor_scalar(wk[:, 0, :], wk[:, 1, :], 1.0, None, ALU.add))
                    r(V.reciprocal(wk[:, 2, :], wk[:, 0, :]))
                    r(V.tensor_tensor(wk[:, 3, :], wk[:, 1, :], wk[:, 2, :], ALU.mult))
                    wts = (wk[:, 2, :], wk[:, 3, :])
                else:
                    wts = (top[:, :, 0], top[:, :, 1])
                for k in range(2):
                    r(V.tensor_tensor(oh[:, k], iota8[:].unsqueeze(1).to_broadcast([P, NT, NE]), bc(topf[:, :, k]),
                                      ALU.is_equal))
                if L == 1:
                    V.tensor_tensor(sel[:], oh[:, 0], oh[:, 1], ALU.add).then_inc(chosen, 1)
                for k in range(2):
                    r(V.tensor_tensor(oh[:, k], oh[:, k], bc(wts[k]), ALU.mult))
                if L == 0:
                    V.tensor_tensor(gate[:], oh[:, 0], oh[:, 1], ALU.add).then_inc(gate_ready, 1)
                else:
                    r(V.tensor_tensor(gate[:], oh[:, 0], oh[:, 1], ALU.add))
                    u = next_pair()
                    V.scalar_tensor_tensor(out=gate[:], in0=u[:, 0, 0:NT * NE].rearrange("p (t e) -> p t e", e=NE),
                                           scalar=float(CAPACITY), in1=gate[:], op0=ALU.is_lt,
                                           op1=ALU.mult).then_inc(gate_ready, 1)
                for half in range(2):
                    u = next_pair()
                    V.tensor_copy(gT[:, half * 1024:(half + 1) * 1024].rearrange("p (a n) -> p a n", a=2),
                                  u[0:NE]).then_inc(gT_ready, 1)
                for half in range(2):
                    u = next_pair()
                    V.tensor_copy(acc[:, half * 8:(half + 1) * 8, :], u[:].rearrange("p a (t c) -> p (a t) c", t=4))\
                        .then_inc(acc_step, 1)

                v.wait_ge(gate_ready, L + 1)
                v.wait_ge(acc_step, L * ACC + 2)
                for n in range(NE * B):
                    e, b = divmod(n, B)
                    u = next_pair()
                    if e:
                        v.wait_ge(acc_step, L * ACC + 2 + NI * (n - B + 1))
                    for i in range(NI):
                        t = b * NI + i
                        V.scalar_tensor_tensor(out=acc[:, t, :], in0=u[:, 0, i * C:(i + 1) * C],
                                               scalar=gate[:, t, e:e + 1], in1=acc[:, t, :],
                                               op0=ALU.mult, op1=ALU.add).then_inc(acc_step, 1)
                v.wait_ge(acc_step, (L + 1) * ACC)
                for b in range(B):
                    residual(acc[:, b * NI:(b + 1) * NI, :], 1, b)


SETUP = 16


def kernel(**inputs):
    import ml_dtypes
    import concourse.bacc as bacc
    from concourse.bass_utils import run_bass_kernel_spmd

    f32, bf = np.float32, ml_dtypes.bfloat16
    ins = {k: np.ascontiguousarray(inputs[k]) for k in inputs}

    as_is = ["L0_attn_x", "L0_attn_W_q", "L0_attn_W_dkv", "L0_attn_W_uk", "L0_attn_W_uv", "L0_attn_W_o",
             "L0_ffn_Wr", "L0_ffn_W1", "L0_ffn_W2", "L0_ffn_b2", "L0_wmod", "L1_attn_la_attn", "L1_attn_la_proj",
             "L1_ffn_Wr", "L1_ffn_W1", "L1_ffn_W2", "L1_ffn_b2", "L1_wmod"]
    arrays = {k: ins[k] for k in as_is}
    arrays["cT"] = np.concatenate([ins["L0_c"], ins["L1_c"]]).T
    arrays["lnlat"] = np.stack([ins["L0_attn_ln_gamma"], ins["L0_attn_ln_beta"]], 1)
    arrays["w_attnT"] = ins["L1_attn_w_attn"].T
    arrays["lb_attnT"] = ins["L1_attn_lb_attn"].T
    arrays["w_projT"] = ins["L1_attn_w_proj"].T
    arrays["lb_projT"] = ins["L1_attn_lb_proj"].T
    arrays["bqk"] = ins["L1_attn_b_attn"][:2 * C].reshape(2, C).T
    arrays["bv"] = np.broadcast_to(ins["L1_attn_b_attn"][2 * C:], (P, C))
    arrays["bproj"] = ins["L1_attn_b_proj"].reshape(1, C)
    arrays["br"] = np.broadcast_to(ins["L0_ffn_br"], (P, NE))
    for L in range(LAYERS):
        arrays[f"b1_{L}"] = ins[f"L{L}_ffn_b1"].reshape(NE, FC[L], P).transpose(2, 0, 1)

    row, col = np.arange(P)[:, None], np.arange(P)[None, :]
    arrays["ident"] = np.eye(P, dtype=f32)
    arrays["identb"] = np.eye(P, dtype=f32).astype(bf)
    arrays["mask_q"] = np.where(col > row, MASKED, 0).astype(bf)
    arrays["mask_k"] = np.where(row > col, MASKED, 0).astype(bf)
    arrays["before"] = (row < col).astype(bf)
    arrays["ones"] = np.ones((P, P), bf)
    arrays["tail_q"] = np.zeros((P, T), bf)
    arrays["tail_k"] = np.repeat((np.arange(P) % 16 < 3)[:, None], T, 1).astype(bf)
    arrays["iota8"] = np.repeat(np.arange(NE, dtype=f32)[None], P, 0)
    half = HD // 2
    inv_freq = (f32(1.0) / f32(10000.0) ** (np.arange(half, dtype=f32) / f32(half))).astype(f32)
    angles = (inv_freq[:, None] * np.arange(T, dtype=f32)[None]).astype(f32)
    cos, sin = np.cos(angles), np.sin(angles)
    arrays["cosT"] = np.tile(cos, (C // half, 1)).astype(f32)
    arrays["sinT"] = np.tile(np.concatenate([-sin, sin]), (NH, 1)).astype(f32)

    nc = bacc.Bacc("TRN2", target_bir_lowering=False, num_devices=1)
    arrays = {k: np.ascontiguousarray(x) for k, x in arrays.items()}
    aps = {k: nc.dram_tensor(f"in_{k}", x.shape, mybir.dt.from_np(x.dtype), kind="ExternalInput").ap()
           for k, x in arrays.items()}
    out = nc.dram_tensor("out_0", (B, T, C), F32, kind="ExternalOutput").ap()
    build(nc, aps, out)
    r = run_bass_kernel_spmd(nc, [{f"in_{k}": x for k, x in arrays.items()}], core_ids=[0])
    return r.results[0]["out_0"]
```

```python
from contextlib import ExitStack

import numpy as np
import concourse.bass as bass
from concourse import mybir

ALU = mybir.AluOpType
ACT = mybir.ActivationFunctionType
AX = mybir.AxisListType.X
F32 = mybir.dt.float32
BF16 = mybir.dt.bfloat16
U32 = mybir.dt.uint32

LAYERS = 2
B, T, C = 4, 512, 128
P = 128
NI = T // P
NT = B * NI
NH, HD = 16, 8
GH = 4
NG = NH // GH
STEPS = B * NG
LAT = 32
RANK = 32
NE = 8
FC = (2, 4)
CAPACITY = int(T / NE * 1.25)
EPS = 1e-5
SCALE = 1.0 / float(np.sqrt(HD))
FAR = 1e4
MASKED = -1e30
VW = HD + 1
VROW = NH * VW + 32 - VW
Q_PARTS = (0, 1, 0, 1, 0, 2)
K_PARTS = (0, 1, 1, 0, 2, 0)
MAX_ROW = HD * len(Q_PARTS)
HALF = 64
P_SLOTS = 20
W_SLOTS = 4
ST_UNITS = 10
PAIR_UNITS = (((0, 0, 0),), ((0, 1, 0), (0, 3, 384)), ((1, 0, 0),), ((1, 1, 0), (1, 3, 384)),
              ((0, 2, 0), (1, 2, 256)))


def build(nc, a, out):
    with ExitStack() as ctx:
        def sb(name, shape, dt=F32):
            return ctx.enter_context(nc.sbuf_tensor(name, shape, dt))

        def sem(name):
            return ctx.enter_context(nc.semaphore(name))

        x = sb("x", [P, NT, C])
        xn = sb("xn", [P, NT, C])
        acc = xn
        hT = sb("hT", [P, B * T])
        ident = sb("ident", [P, P])
        identb = sb("identb", [P, P], BF16)
        mask_q = sb("mask_q", [P, P], BF16)
        mask_k = sb("mask_k", [P, P], BF16)
        before = sb("before", [P, P], BF16)
        ones = sb("ones", [P, P], BF16)
        onesf = sb("onesf", [1, P])
        tail_q = sb("tail_q", [P, T], BF16)
        tail_k = sb("tail_k", [P, T], BF16)
        cosT = sb("cosT", [P, T])
        sinT = sb("sinT", [P, T])
        cT = sb("cT", [P, LAYERS * B])
        silu = sb("silu", [P, 3, LAYERS * B])
        modT = sb("modT", [P, LAYERS, 6, B])
        gates = sb("gates", [P, LAYERS * B, 2, C])
        wq = sb("wq", [P, 2, C])
        wuk = sb("wuk", [LAT, 2, C])
        wuv = sb("wuv", [LAT, C])
        wdkv = sb("wdkv", [P, LAT])
        lnlat = sb("lnlat", [LAT, 2])
        wqkv = sb("wqkv", [P, 3 * C])
        la_attn = sb("la_attn", [RANK, C])
        lb_attn = sb("lb_attn", [RANK, 3 * C])
        la_proj = sb("la_proj", [RANK, C])
        lb_proj = sb("lb_proj", [RANK, C])
        bqk = sb("bqk", [P, 2])
        bv = sb("bv", [P, C])
        bproj = sb("bproj", [1, C])
        wo = sb("wo", [P, LAYERS, C])
        wr = sb("wr", [P, LAYERS, NE])
        br = sb("br", [P, NE])
        w1 = sb("w1", [P, NE * FC[0] * P])
        w2 = sb("w2", [P, NE * FC[0] * C])
        b1 = [sb(f"b1_{L}", [P, NE, FC[L]]) for L in range(LAYERS)]
        b2_0 = sb("b2_0", [NE, C])
        b2_1 = sb("b2_1", [P, NE])
        negh = sb("negh", [P, NI])
        iota8 = sb("iota8", [P, NE])
        stats = sb("stats", [P, B, NI, 6])
        mv = sb("mv", [P, B, NI, 2])
        ve = sb("ve", [P, B, NI])
        rstd = sb("rstd", [P, B, NI])
        latc = sb("latc", [P, NI, LAT])
        lstats = sb("lstats", [P, NI, 6])
        lmv = sb("lmv", [P, NI, 2])
        lve = sb("lve", [P, NI])
        lrstd = sb("lrstd", [P, NI])
        parts = sb("parts", [P, 2, 3, T], BF16)
        latn = sb("latn", [P, NI, LAT])
        vaug = sb("vaug", [P, NT, VROW])
        qop = sb("qop", [P, 2, NH // 2, T], BF16)
        kop = sb("kop", [P, 2, NH, T], BF16)
        negmax = sb("negmax", [P, 2, 2, 2, NI])
        mres = sb("mres", [P, 2, 2 * NI])
        mparts = sb("mparts", [P, 2, 2, 3, 2 * NI], BF16)
        mT = sb("mT", [48, 2, P], BF16)
        latT = sb("latT", [LAT, T])
        rot = sb("rot", [P, 2, T])
        full = sb("full", [P, 2, T])
        gT = sb("gT", [NE, T])
        pw = sb("pw", [P, P_SLOTS, T])
        wmod = pw[:, 0:3, :].rearrange("p a (b n) -> p (a b n)", b=1).rearrange("p (l n) -> p l n", l=LAYERS)
        silu_bc = pw[:, 3:5, :].rearrange("p a (m n) -> p (a m) n", n=P)
        oT4 = sb("oT4", [P, 2, T])
        rec = sb("rec", [P, NI, GH])
        o_nat = sb("o_nat", [P, 2, NI, C])
        oT = sb("oT", [P, T])
        gsign = o_nat[:].rearrange("p a (b j) c -> p (a b) j c", j=2)
        gabs = oT4[:].rearrange("p a (m j c) -> p (a m) j c", m=2, j=2)
        upd = sb("upd", [P, NI, C])
        lg = sb("lg", [P, NT, NE])
        lgs = sb("lgs", [P, NT, NE])
        ex = sb("ex", [P, NT, NE])
        top = sb("top", [P, NT, 8])
        topi = sb("topi", [P, NT, 8], U32)
        topf = sb("topf", [P, NT, 2])
        wk = sb("wk", [P, 4, NT])
        oh = sb("oh", [P, 2, NT, NE])
        gate = sb("gate", [P, NT, NE])
        sel = sb("sel", [P, NT, NE], BF16)
        away = sb("away", [P, NT, NE])
        pos = sb("pos", [P, NT, NE])
        iota_s = sb("iota_s", [P, CAPACITY])
        gres = sb("gres", [P, NI, NE])
        gparts = sb("gparts", [P, NT, NE, 3], BF16)
        slot_w = sb("slot_w", [P, NE, B])
        kflat = kop[:].rearrange("p a h t -> p a (h t)")
        qflat = qop[:].rearrange("p a h t -> p a (h t)")
        NS = NE * CAPACITY
        slots = [kflat[:, 0, k * NI * NS:(k + 1) * NI * NS].rearrange("p (i e n) -> p i e n", i=NI, e=NE)
                 for k in range(2)]
        slotsT = [kflat[0:CAPACITY, 1, 0:NE * T], kflat[0:CAPACITY, 1, NE * T:2 * NE * T],
                  qflat[0:CAPACITY, 0, :], qflat[0:CAPACITY, 1, :]]
        slotsT = [t.rearrange("p (e t) -> p e t", e=NE) for t in slotsT]
        bufT = pw[:, 0:5, :].rearrange("p a n -> p (a n)").rearrange("p (e b n) -> p e b n", e=NE, b=B)
        hid1 = pw[:, 5:10, :].rearrange("p a n -> p (a n)").rearrange("p (k f n) -> p k f n", k=2, f=FC[1])

        bank = [ctx.enter_context(nc.psum_tensor(f"bank{i}", [P, 512], F32)) for i in range(3)]
        pair = [ctx.enter_context(nc.psum_tensor(f"pair{i}", [P, 2, 512], F32)) for i in range(2)]
        pvb = ctx.enter_context(nc.psum_tensor("pvb", [P, 512], F32))

        scr_q = nc.dram_tensor("scr_q", (B, NH, HALF, T), BF16, kind="Internal").ap()
        scr_k = nc.dram_tensor("scr_k", (B, NH, HALF, T), BF16, kind="Internal").ap()
        scr_m = nc.dram_tensor("scr_m", (B, NG, 48, P), BF16, kind="Internal").ap()

        ld_x = [sem(f"ld_x{b}") for b in range(B)]
        ld_small, ld_mod, ld_attn, ld_moe = sem("ld_small"), sem("ld_mod"), sem("ld_attn"), sem("ld_moe")
        ld_latent = sem("ld_latent")
        ld_exp = [sem(f"ld_exp{k}") for k in range(W_SLOTS)]
        tails, pool_init = sem("tails"), sem("pool_init")
        act_silu, dve_silu, setup = sem("act_silu"), sem("dve_silu"), sem("setup")
        swapped, factors, updated = sem("swapped"), sem("factors"), sem("updated")
        pair_full = sem("pair_full")
        bank_full = sem("bank_full")
        ln_stat, ln_mv, ln_ve, ln_rstd = sem("ln_stat"), sem("ln_mv"), sem("ln_ve"), sem("ln_rstd")
        lat_stat, lat_mv, lat_ve, lat_rstd = sem("lat_stat"), sem("lat_mv"), sem("lat_ve"), sem("lat_rstd")
        lat_copied = sem("lat_copied")
        ln_xn, h_ready, latn_ready, latT_ready = sem("ln_xn"), sem("h_ready"), sem("latn_ready"), sem("latT_ready")
        rotated, biased, split, v_ready = sem("rotated"), sem("biased"), sem("split"), sem("v_ready")
        scr_done = [[sem(f"scr_{n}{b}") for b in range(B)] for n in "qk"]
        op_loaded = [[sem(f"op_loaded{i}_{g}") for g in range(NG)] for i in range(2)]
        reduced, msplit, m_copied = sem("reduced"), sem("msplit"), sem("m_copied")
        m_out, m_in = [sem(f"m_out{g}") for g in range(NG)], [sem(f"m_in{g}") for g in range(NG)]
        weights, pv_done, pv_copied = sem("weights"), sem("pv_done"), sem("pv_copied")
        o_step, oT_ready, gated, x_done = sem("o_step"), sem("oT_ready"), sem("gated"), sem("x_done")
        logits_read, route_step, exp_in, exp_out = sem("logits_read"), sem("route_step"), sem("exp_in"), sem("exp_out")
        gate_ready, gT_ready, acc_step, hidden0 = sem("gate_ready"), sem("gT_ready"), sem("acc_step"), sem("hidden0")
        acc_started = sem("acc_started")
        chosen, pos_ready, gsplit, xsplit = sem("chosen"), sem("pos_ready"), sem("gsplit"), sem("xsplit")
        slots_ready, slotsT_ready = sem("slots_ready"), sem("slotsT_ready")
        buf_ready, slot_w_ready = sem("buf_ready"), sem("slot_w_ready")
        hidden1, yT_ready, y_turned, y_split = sem("hidden1"), sem("yT_ready"), sem("y_turned"), sem("y_split")
        summed, stored = sem("summed"), sem("stored")

        REDUCTIONS = (1, 3, 4, 6, 7)

        SMALL = ["cT", "ident", "identb", "mask_q", "mask_k", "before", "ones", "tail_q", "tail_k", "cosT", "sinT",
                 "iota8", "iota_s"]
        smalls = dict(ident=ident, identb=identb, mask_q=mask_q, mask_k=mask_k, before=before, ones=ones,
                      tail_q=tail_q, tail_k=tail_k, cosT=cosT, sinT=sinT, cT=cT, iota8=iota8, iota_s=iota_s)
        n_mod = 16 * (2 + LAYERS)
        n_small = 16 * (len(SMALL) - 2)

        wq_in = a["L0_attn_W_q"]
        attn_loads = [
            (wq[:, 0, :], wq_in), (wuk[:, 0, :], a["L0_attn_W_uk"]), (wuv[:], a["L0_attn_W_uv"]),
            (wdkv[:], a["L0_attn_W_dkv"]), (lnlat[:], a["lnlat"]), (wqkv[:], a["w_attnT"]),
            (la_attn[:], a["L1_attn_la_attn"]), (lb_attn[:], a["lb_attnT"]), (la_proj[:], a["L1_attn_la_proj"]),
            (lb_proj[:], a["lb_projT"]), (bqk[:], a["bqk"]), (bv[:], a["bv"]), (bproj[:], a["bproj"]),
            (wo[:, 0, :], a["L0_attn_W_o"]), (wo[:, 1, :], a["w_projT"]), (wr[:, 0, :], a["L0_ffn_Wr"]),
            (wr[:, 1, :], a["L1_ffn_Wr"]), (br[:], a["br"]), (b1[0][:], a["b1_0"]), (b1[1][:], a["b1_1"]),
            (b2_0[:], a["L0_ffn_b2"]), (b2_1[:], a["b2_1"]),
        ]
        n_latent = 16 * 5
        n_attn = 16 * (len(attn_loads) - 5)

        w1_0 = w1[:].rearrange("p (e n) -> p e n", e=NE)
        w2_0 = w2[:].rearrange("p (e k n) -> p e k n", e=NE, k=FC[0])
        w1_1 = w1[:].rearrange("p (e n) -> p e n", e=W_SLOTS)
        w2_1 = w2[:].rearrange("p (e k n) -> p e k n", e=W_SLOTS, k=FC[1])

        block = ctx.enter_context(nc.Block())

        @block.sync
        def _(sp):
            xv = a["L0_attn_x"].rearrange("b (i p) c -> b p i c", p=P)
            for n in SMALL[:2]:
                sp.dma_start(smalls[n][:], a[n]).then_inc(ld_mod, 16)
            for L in range(LAYERS):
                sp.dma_start(wmod[:, L, :], a[f"L{L}_wmod"]).then_inc(ld_mod, 16)
            for b in range(B):
                sp.dma_start(x[:, b * NI:(b + 1) * NI, :], xv[b]).then_inc(ld_x[b], 16)
            for dst, src in attn_loads[:5]:
                sp.dma_start(dst, src).then_inc(ld_latent, 16)
            for n in SMALL[2:]:
                sp.dma_start(smalls[n][:], a[n]).then_inc(ld_small, 16)
            for dst, src in attn_loads[5:]:
                sp.dma_start(dst, src).then_inc(ld_attn, 16)
            sp.wait_ge(ld_small, n_small)
            for b in range(B):
                for tile_, scr in ((tail_q, scr_q), (tail_k, scr_k)):
                    for h0 in (0, NH // 2):
                        sp.dma_start(scr[b, h0:h0 + NH // 2, MAX_ROW:HALF, :], tile_[:]).then_inc(tails, 16)
            sp.dma_start(w1_0, a["L0_ffn_W1"].rearrange("e p n -> p e n")).then_inc(ld_moe, 16)
            for e in range(NE):
                sp.dma_start(w2_0[:, e], a["L0_ffn_W2"][e].rearrange("(k p) n -> p k n", p=P)).then_inc(ld_moe, 16)

            def load_expert(e):
                k = e % W_SLOTS
                if e >= W_SLOTS:
                    sp.wait_ge(y_split, 5 * (e - W_SLOTS + 1))
                sp.dma_start(w1_1[:, k, :], a["L1_ffn_W1"][e]).then_inc(ld_exp[k], 16)
                sp.dma_start(w2_1[:, k], a["L1_ffn_W2"][e].rearrange("(k p) n -> p k n", p=P))\
                  .then_inc(ld_exp[k], 16)

            def write_parts(L, b):
                for n, (scr, order_) in enumerate(((scr_q, Q_PARTS), (scr_k, K_PARTS))):
                    sp.wait_ge(split, 8 * (L * B + b) + 4 * (n + 1))
                    for r, part in enumerate(order_):
                        sp.dma_start(scr[b, :, r * HD:(r + 1) * HD, :], parts[:, n, part, :])\
                          .then_inc(scr_done[n][b], 16)

            def load_operands(L, b):
                sp.wait_ge(scr_done[0][b], 96 * (L + 1))
                sp.wait_ge(scr_done[1][b], 96 * (L + 1))
                for g in range(NG):
                    gs = L * STEPS + b * NG + g
                    if gs >= 2 * NG:
                        sp.wait_ge(pv_done, gs - 2 * NG + 1)
                    for par in range(2):
                        heads = slice(g * GH + par, (g + 1) * GH, 2)
                        rows = slice(par * HALF, (par + 1) * HALF)
                        sp.dma_start(qop[rows, b % 2, 2 * g:2 * g + 2, :],
                                     scr_q[b, heads].rearrange("h r t -> r h t")).then_inc(op_loaded[b % 2][g], 16)
                        sp.dma_start(kop[rows, b % 2, heads, :],
                                     scr_k[b, heads].rearrange("h r t -> r h t")).then_inc(op_loaded[b % 2][g], 16)

            for L in range(LAYERS):
                write_parts(L, 0)
                if L == 0:
                    sp.wait_ge(tails, 16 * 4 * B)
                    sp.wait_ge(pool_init, 4)
                load_operands(L, 0)
                write_parts(L, 1)
                load_operands(L, 1)
                write_parts(L, 2)
                if L == 1:
                    sp.wait_ge(acc_step, B * NE * NI)
                    for e in range(W_SLOTS):
                        load_expert(e)
                load_operands(L, 2)
                write_parts(L, 3)
                load_operands(L, 3)
            for e in range(W_SLOTS, NE):
                load_expert(e)
            ov = out.rearrange("b (i p) c -> b p i c", p=P)
            for b in range(B):
                sp.wait_ge(x_done, (2 * LAYERS - 1) * B + b + 1)
                sp.dma_start(ov[b], x[:, b * NI:(b + 1) * NI, :]).then_inc(stored, 16)
            sp.wait_ge(stored, 16 * B)

        @block.gpsimd
        def _(pool):
            nc.gpsimd.memset(negh[:], -0.5).then_inc(pool_init, 1)
            nc.gpsimd.memset(kop[:, 0, :, :], 0.0).then_inc(pool_init, 1)
            nc.gpsimd.memset(kop[:, 1, :, :], 0.0).then_inc(pool_init, 1)
            nc.gpsimd.memset(vaug[:], 1.0).then_inc(pool_init, 1)
            nc.gpsimd.memset(onesf[:], 1.0).then_inc(pool_init, 1)
            pool.wait_ge(pool_init, 5)

            def stat(L, half, b):
                n = (2 * L + half) * B + b
                pool.wait_ge(ln_mv, NI * (n + 1))
                nc.gpsimd.tensor_scalar(ve[:, b, :], mv[:, b, :, 1], EPS, None, ALU.add).then_inc(ln_ve, 1)
                pool.wait_ge(ln_ve, n + 1)
                nc.gpsimd.tensor_tensor(rstd[:, b, :], ve[:, b, :], negh[:], ALU.pow).then_inc(ln_rstd, 1)

            def lat(b):
                pool.wait_ge(lat_mv, NI * (b + 1))
                nc.gpsimd.tensor_scalar(lve[:], lmv[:, :, 1], EPS, None, ALU.add).then_inc(lat_ve, 1)
                pool.wait_ge(lat_ve, b + 1)
                nc.gpsimd.tensor_tensor(lrstd[:], lve[:], negh[:], ALU.pow).then_inc(lat_rstd, 1)

            def max_turn(L, s):
                b, g = divmod(s, NG)
                gs = L * STEPS + s
                pool.wait_ge(m_copied, gs + 1)
                pool.dma_start(scr_m[b, g], mT[:, s % 2, :]).then_inc(m_out[g], 16)
                pool.wait_ge(m_out[g], 16 * (L * B + b + 1))
                src = scr_m[b, g].rearrange("(r part k) q -> r part k q", r=2, part=3)
                for par in range(2):
                    row = par * HALF + MAX_ROW
                    pool.dma_start(qop[row:row + 3, b % 2, 2 * g:2 * g + 2, :].rearrange("p j (i q) -> p (j i) q", i=NI),
                                   src[par]).then_inc(m_in[g], 16)

            work = dict(stat=stat, lat=lat, max_turn=max_turn)
            for name, *at in ORDER:
                if name in work:
                    work[name](*at)

        @block.scalar
        def _(act):
            nb = [0]

            def next_bank():
                nb[0] += 1
                act.wait_ge(bank_full, nb[0])
                return bank[(nb[0] - 1) % 3]

            def modulation():
                act.wait_ge(ld_mod, n_mod)
                nc.scalar.activation(silu[:, 0, :], cT[:], ACT.Exp, scale=-1.0).then_inc(act_silu, 1)

            def turn(L, half, b):
                src = next_bank()
                act.wait_ge(setup, 2)
                nc.scalar.activation(hT[:, b * T:(b + 1) * T], src[:], ACT.Identity,
                                     scale=modT[:, L, 3 * half + 1, b:b + 1],
                                     bias=modT[:, L, 3 * half, b:b + 1]).then_inc(h_ready, 1)

            def lat_turn(b):
                src = next_bank()
                act.wait_ge(ld_latent, n_latent)
                nc.scalar.activation(latT[:], src[0:LAT, :], ACT.Identity, scale=lnlat[:, 0:1],
                                     bias=lnlat[:, 1:2]).then_inc(latT_ready, 1)

            def scores_k(L, s, u):
                src = next_bank()
                gs = L * STEPS + s
                if u == 0 and gs >= 2:
                    act.wait_ge(pv_done, gs - 1)
                nc.scalar.activation(pw[:, (s % 2) * ST_UNITS + u, :], src[:], ACT.Exp, scale=SCALE)\
                    .then_inc(weights, 1)

            def weigh_copy(L, s):
                gs = L * STEPS + s
                act.wait_ge(pv_done, gs + 1)
                if gs == 0:
                    act.wait_ge(factors, 4 * LAYERS)
                if gs >= 2:
                    act.wait_ge(o_step, 2 * (gs - 1))
                nc.scalar.activation(oT4[:, gs % 2, :], pvb[:], ACT.Copy).then_inc(pv_copied, 1)

            def route_exp(L, b):
                ts = slice(b * NI, (b + 1) * NI)
                act.wait_ge(exp_in, L * B + b + 1)
                if L == 0:
                    nc.scalar.activation(wk[:, 1, ts], wk[:, 0, ts], ACT.Exp).then_inc(exp_out, 1)
                else:
                    nc.scalar.activation(ex[:, ts, :], lgs[:, ts, :], ACT.Exp).then_inc(exp_out, 1)

            def hidden(n):
                if n == 0:
                    act.wait_ge(ld_attn, n_attn)
                b, e = divmod(n, NE)
                for f in range(FC[0]):
                    src = next_bank()
                    nc.scalar.activation(pw[:, (n % 3) * FC[0] + f, :], src[:], ACT.Relu,
                                         bias=b1[0][:, e, f:f + 1]).then_inc(hidden0, 1)

            def dispatch(b, k):
                src = next_bank()
                nc.scalar.activation(bufT[:, k * 4:(k + 1) * 4, b, :],
                                     src[:, 0:4 * CAPACITY].rearrange("p (e n) -> p e n", e=4), ACT.Identity,
                                     scale=modT[:, 1, 4, b:b + 1], bias=modT[:, 1, 3, b:b + 1])\
                    .then_inc(buf_ready, 1)

            def slots_turn(b, i):
                src = next_bank()
                nc.scalar.activation(slotsT[b][:, :, i * P:(i + 1) * P],
                                     src[0:CAPACITY, :].bitcast(BF16).rearrange("p (e n) -> p e n", e=NE),
                                     ACT.Copy).then_inc(slotsT_ready, 1)

            def expert_hidden(e):
                for f in range(FC[1]):
                    src = next_bank()
                    nc.scalar.activation(hid1[:, e % 2, f, :], src[:, 0:B * CAPACITY], ACT.Relu,
                                         bias=b1[1][:, e, f:f + 1]).then_inc(hidden1, 1)

            def expert_out(e):
                src = next_bank()
                nc.scalar.activation(oT4[:, e % 2, 0:B * CAPACITY], src[:, 0:B * CAPACITY], ACT.Identity,
                                     bias=b2_1[:, e:e + 1]).then_inc(yT_ready, 1)

            work = dict(modulation=modulation, turn=turn, lat_turn=lat_turn, scores_k=scores_k,
                        weigh_copy=weigh_copy, route_exp=route_exp, hidden=hidden, dispatch=dispatch,
                        slots_turn=slots_turn, expert_hidden=expert_hidden, expert_out=expert_out)
            for name, *at in ORDER:
                if name in work:
                    work[name](*at)

        @block.tensor
        def _(pe):
            mm = nc.tensor.matmul
            np_, nb = [0], [0]
            pair_read, bank_read = [None, None], [None, None, None]

            def next_pair(*reader):
                n = np_[0] % 2
                np_[0] += 1
                if pair_read[n]:
                    pe.wait_ge(*pair_read[n])
                pair_read[n] = reader
                return pair[n]

            def next_bank(*reader):
                n = nb[0] % 3
                nb[0] += 1
                if bank_read[n]:
                    pe.wait_ge(*bank_read[n])
                bank_read[n] = reader
                return bank[n]

            def modulation():
                pe.wait_ge(ld_mod, n_mod)
                pe.wait_ge(dve_silu, 4)
                u = next_pair(setup, 1)
                for L in range(LAYERS):
                    for j in range(6):
                        last = mm(u[:, 0, L * 24 + j * B:L * 24 + (j + 1) * B], wmod[:, L, j * C:(j + 1) * C],
                                  silu[:, 2, L * B:(L + 1) * B], start=True, stop=True)
                last.then_inc(pair_full, 1)

            def gate_factors(L):
                u = next_pair(factors, 4 * L + 4)
                gw = wmod[:, L, :].rearrange("p (j k c) -> p k j c", j=2, k=3)[:, 2]
                for b in range(B):
                    last = mm(u[:, b // 2, (b % 2) * 256:(b % 2 + 1) * 256], silu_bc[:, L * B + b, :], gw,
                              start=True, stop=True)
                last.then_inc(pair_full, 1)

            def low_rank():
                pe.wait_ge(ld_attn, n_attn)
                u = next_pair(updated, 2)
                mm(u[:, 0, 0:3 * C], la_attn[:], lb_attn[:], start=True, stop=True)
                mm(u[:, 1, 0:C], la_proj[:], lb_proj[:], start=True, stop=True).then_inc(pair_full, 1)

            def turn(L, half, b):
                n = (2 * L + half) * B + b
                if n == 0:
                    pe.wait_ge(ld_small, n_small)
                dst = next_bank(h_ready, n + 1)
                pe.wait_ge(ln_xn, NI * (n + 1))
                for i in range(NI):
                    last = nc.tensor.transpose(dst[:, i * P:(i + 1) * P], xn[:, b * NI + i, :], ident[:])
                last.then_inc(bank_full, 1)

            def lat(b):
                if b == 0:
                    pe.wait_ge(ld_latent, n_latent)
                    pe.wait_ge(swapped, 4)
                u = next_pair(lat_copied, b + 1)
                pe.wait_ge(h_ready, b + 1)
                for i in range(NI):
                    last = mm(u[:, 0, i * LAT:(i + 1) * LAT], hT[:, b * T + i * P:b * T + (i + 1) * P], wdkv[:],
                              start=True, stop=True)
                last.then_inc(pair_full, 1)

            def rotate_q(b):
                u = next_pair(rotated, 6 * b + 2)
                for v in range(2):
                    last = mm(u[:, v, :], wq[:, v, :], hT[:, b * T:(b + 1) * T], start=True, stop=True)
                last.then_inc(pair_full, 1)

            def lat_turn(b):
                dst = next_bank(latT_ready, b + 1)
                pe.wait_ge(latn_ready, NI * (b + 1))
                for i in range(NI):
                    last = nc.tensor.transpose(dst[0:LAT, i * P:(i + 1) * P], latn[:, i, :], ident[:])
                last.then_inc(bank_full, 1)

            def rotate_k(b):
                u = next_pair(rotated, 6 * b + 5)
                pe.wait_ge(latT_ready, b + 1)
                for v in range(2):
                    last = mm(u[:, v, :], wuk[:, v, :], latT[:], start=True, stop=True)
                last.then_inc(pair_full, 1)

            def bias_qk(b):
                if b == 0:
                    pe.wait_ge(updated, 2)
                u = next_pair(biased, 2 * (b + 1))
                pe.wait_ge(h_ready, 2 * B + b + 1)
                for v in range(2):
                    last = mm(u[:, v, :], wqkv[:, v * C:(v + 1) * C], hT[:, b * T:(b + 1) * T],
                              start=True, stop=True)
                last.then_inc(pair_full, 1)

            def values(L, b):
                u = next_pair(v_ready, NI * (L * B + b + 1))
                for i in range(NI):
                    dst = u[:, 0, i * C:(i + 1) * C]
                    if L == 0:
                        last = mm(dst, latT[:, i * P:(i + 1) * P], wuv[:], start=True, stop=True)
                    else:
                        last = mm(dst, hT[:, b * T + i * P:b * T + (i + 1) * P], wqkv[:, 2 * C:3 * C],
                                  start=True, stop=True)
                last.then_inc(pair_full, 1)

            def scores_q(L, s, k):
                b, g = divmod(s, NG)
                if k == 0:
                    pe.wait_ge(op_loaded[b % 2][g], 64 * (L * 2 + b // 2 + 1))
                u = next_pair(reduced, 7 * (L * STEPS + s) + REDUCTIONS[k])
                if k < 4:
                    pr, tiles = k // 2, ((3, 0),) if k % 2 == 0 else ((2, 0), (0, 384))
                    jobs = [(2 * pr + v, v, i, c0) for v in range(2) for i, c0 in tiles]
                else:
                    jobs = [(h, h // 2, 1, (h % 2) * 256) for h in range(GH)]
                for h, v, i, c0 in jobs:
                    head = g * GH + h
                    n = (i + 1) * P
                    mm(u[:, v, c0:c0 + n], qop[:, b % 2, head // 2, i * P:(i + 1) * P],
                       kop[:, b % 2, head, 0:n], start=True, stop=False)
                    last = mm(u[:, v, c0 + i * P:c0 + n], identb[:], mask_q[:], start=False, stop=True)
                last.then_inc(pair_full, 1)

            def max_turn(L, s):
                u = next_pair(m_copied, L * STEPS + s + 1)
                pe.wait_ge(msplit, 4 * (L * STEPS + s + 1))
                tb = u[0:48, 0, :].bitcast(BF16)[:, 0:P]
                nc.tensor.transpose(tb, mparts[:, s % 2].rearrange("p a b c -> p (a b c)"), identb[:])\
                    .then_inc(pair_full, 1)

            def scores_k(L, s, k):
                b, g = divmod(s, NG)
                if k == 0:
                    pe.wait_ge(m_in[g], 32 * (L * B + b + 1))
                dst = next_bank(weights, ST_UNITS * (L * STEPS + s) + k + 1)
                pr, k2 = divmod(k, 5)
                for hh, j, c0 in PAIR_UNITS[k2]:
                    head = g * GH + 2 * pr + hh
                    n = T - j * P
                    mm(dst[:, c0:c0 + n], kop[:, b % 2, head, j * P:(j + 1) * P],
                       qop[:, b % 2, head // 2, j * P:T], start=True, stop=False)
                    last = mm(dst[:, c0:c0 + P], identb[:], mask_k[:], start=False, stop=True)
                last.then_inc(bank_full, 1)

            def weigh(L, s):
                b, g = divmod(s, NG)
                gs = L * STEPS + s
                if g == 0:
                    pe.wait_ge(v_ready, NI * (L * B + b + 1))
                if gs >= 1:
                    pe.wait_ge(pv_copied, gs)
                pe.wait_ge(weights, ST_UNITS * (gs + 1))
                where = {}
                for pr in range(2):
                    for k2, unit in enumerate(PAIR_UNITS):
                        for hh, j, c0 in unit:
                            where[2 * pr + hh, j] = ((s % 2) * ST_UNITS + 5 * pr + k2, c0)
                for j in range(NI):
                    for h in range(GH):
                        slot, c0 = where[h, j]
                        col = (g * GH + h) * VW
                        last = mm(pvb[32 * h:32 * h + 32, j * P:T], vaug[:, b * NI + j, col:col + 32],
                                  pw[:, slot, c0:c0 + T - j * P], start=(j == 0), stop=(j == NI - 1))
                last.then_inc(pv_done, 1)

            def normalise(L, s):
                gs = L * STEPS + s
                u = next_pair(o_step, 2 * (gs + 1))
                pe.wait_ge(pv_copied, gs + 1)
                for i in range(NI):
                    last = nc.tensor.transpose(u[:, 0, i * P:(i + 1) * P], oT4[:, gs % 2, i * P:(i + 1) * P],
                                               ident[:])
                last.then_inc(pair_full, 1)

            def out_turn(L, b):
                u = next_pair(oT_ready, L * B + b + 1)
                pe.wait_ge(o_step, 2 * (L * STEPS + (b + 1) * NG))
                for i in range(NI):
                    last = nc.tensor.transpose(u[:, 0, i * P:(i + 1) * P], o_nat[:, b % 2, i, :], ident[:])
                last.then_inc(pair_full, 1)

            def project(L, b):
                u = next_pair(gated, 2 * L * B + b + 1)
                pe.wait_ge(oT_ready, L * B + b + 1)
                for i in range(NI):
                    dst = u[:, 0, i * C:(i + 1) * C]
                    last = mm(dst, oT[:, i * P:(i + 1) * P], wo[:, L, :], start=True, stop=(L == 0))
                    if L == 1:
                        last = mm(dst, onesf[:], bproj[:], start=False, stop=True)
                last.then_inc(pair_full, 1)

            def logits(L, b):
                if L * B + b == 0:
                    pe.wait_ge(ld_attn, n_attn)
                u = next_pair(logits_read, L * B + b + 1)
                pe.wait_ge(h_ready, (2 * L + 1) * B + b + 1)
                for i in range(NI):
                    last = mm(u[:, 0, i * NE:(i + 1) * NE], hT[:, b * T + i * P:b * T + (i + 1) * P], wr[:, L, :],
                              start=True, stop=True)
                last.then_inc(pair_full, 1)

            def gate_turn(b):
                u = next_pair(gT_ready, b + 1)
                pe.wait_ge(gate_ready, b + 1)
                for i in range(NI):
                    last = nc.tensor.transpose(u[0:NE, 0, i * P:(i + 1) * P], gate[:, b * NI + i, :], ident[:])
                last.then_inc(pair_full, 1)

            def acc_start(b):
                u = next_pair(acc_started, b + 1)
                pe.wait_ge(gT_ready, b + 1)
                for i in range(NI):
                    last = mm(u[:, 0, i * C:(i + 1) * C], gT[:, i * P:(i + 1) * P], b2_0[:], start=True, stop=True)
                last.then_inc(pair_full, 1)

            def position(b):
                u = next_pair(pos_ready, b + 1)
                pe.wait_ge(chosen, 2 * (b + 1))
                for i in range(NI):
                    dst = u[:, 0, i * NE:(i + 1) * NE]
                    last = mm(dst, before[:], sel[:, b * NI + i, :], start=True, stop=(i == 0))
                    for k in range(i):
                        last = mm(dst, ones[:], sel[:, b * NI + k, :], start=False, stop=(k == i - 1))
                last.then_inc(pair_full, 1)

            def hidden(n):
                if n == 0:
                    pe.wait_ge(ld_moe, 16 * (NE + 1))
                b, e = divmod(n, NE)
                for f in range(FC[0]):
                    dst = next_bank(hidden0, FC[0] * n + f + 1)
                    mm(dst[:], w1_0[:, e, f * P:(f + 1) * P], hT[:, b * T:(b + 1) * T],
                       start=True, stop=True).then_inc(bank_full, 1)

            def outputs(n):
                b, e = divmod(n, NE)
                u = next_pair(acc_step, NI * (n + 1))
                pe.wait_ge(hidden0, FC[0] * (n + 1))
                for i in range(NI):
                    for f in range(FC[0]):
                        last = mm(u[:, 0, i * C:(i + 1) * C], pw[:, (n % 3) * FC[0] + f, i * P:(i + 1) * P],
                                  w2_0[:, e, f, :], start=(f == 0), stop=(f == FC[0] - 1))
                last.then_inc(pair_full, 1)

            def dispatch(b, k):
                dst = next_bank(buf_ready, 2 * b + k + 1)
                pe.wait_ge(xsplit, 4 * (b + 1))
                pe.wait_ge(slots_ready, NI * (b + 1))
                rows = parts[:, b % 2].rearrange("p n (i c) -> p n i c", i=NI)
                for i in range(NI):
                    for part in range(3):
                        last = mm(dst[:, 0:4 * CAPACITY], rows[:, part, i, :], slots[b % 2][:, i, 4 * k:4 * k + 4, :],
                                  start=(i + part == 0), stop=(i == NI - 1 and part == 2))
                last.then_inc(bank_full, 1)

            def slots_turn(b, i):
                dst = next_bank(slotsT_ready, NI * b + i + 1)
                tb = dst[0:CAPACITY, :].bitcast(BF16)
                for e in range(NE):
                    last = nc.tensor.transpose(tb[:, e * P:(e + 1) * P], slots[b % 2][:, i, e, :], identb[:])
                last.then_inc(bank_full, 1)

            def slot_weights(b):
                u = next_pair(slot_w_ready, b + 1)
                pe.wait_ge(gsplit, 4 * (b + 1))
                for e in range(NE):
                    for i in range(NI):
                        last = mm(u[0:CAPACITY, 0, 3 * e:3 * e + 3], slots[b % 2][:, i, e, :],
                                  gparts[:, b * NI + i, e, :], start=(i == 0), stop=(i == NI - 1))
                last.then_inc(pair_full, 1)

            def expert_hidden(e):
                pe.wait_ge(ld_exp[e % W_SLOTS], 32 * (e // W_SLOTS + 1))
                if e == 0:
                    pe.wait_ge(buf_ready, 2 * B)
                for f in range(FC[1]):
                    dst = next_bank(hidden1, FC[1] * e + f + 1)
                    mm(dst[:, 0:B * CAPACITY], w1_1[:, e % W_SLOTS, f * P:(f + 1) * P],
                       bufT[:, e].rearrange("p b n -> p (b n)"), start=True, stop=True).then_inc(bank_full, 1)

            def expert_out(e):
                dst = next_bank(yT_ready, e + 1)
                pe.wait_ge(hidden1, FC[1] * (e + 1))
                for f in range(FC[1]):
                    last = mm(dst[:, 0:B * CAPACITY], w2_1[:, e % W_SLOTS, f, :], hid1[:, e % 2, f, :],
                              start=(f == 0), stop=(f == FC[1] - 1))
                last.then_inc(bank_full, 1)

            def expert_turn(e):
                if e == 0:
                    pe.wait_ge(pv_copied, LAYERS * STEPS)
                else:
                    pe.wait_ge(y_split, 5 * (e - 1) + 1)
                pe.wait_ge(yT_ready, e + 1)
                for b in range(B):
                    last = nc.tensor.transpose(pvb[0:CAPACITY, b * C:(b + 1) * C],
                                               oT4[:, e % 2, b * CAPACITY:(b + 1) * CAPACITY], ident[:])
                last.then_inc(y_turned, 1)

            def combine(e):
                if e == 0:
                    for reader in pair_read:
                        pe.wait_ge(*reader)
                    pe.wait_ge(slotsT_ready, NI * B)
                pe.wait_ge(y_split, 5 * (e + 1))
                for b in range(B):
                    for i in range(NI):
                        for part in range(3):
                            last = mm(pair[b // 2][:, b % 2, i * C:(i + 1) * C], slotsT[b][:, e, i * P:(i + 1) * P],
                                      parts[0:CAPACITY, e % 2, part, b * C:(b + 1) * C],
                                      start=(e + i + part == 0), stop=(e == NE - 1 and part == 2),
                                      skip_group_check=True)
                    if e == NE - 1:
                        last.then_inc(summed, 1)

            work = dict(modulation=modulation, gate_factors=gate_factors, low_rank=low_rank, turn=turn, lat=lat,
                        rotate_q=rotate_q, lat_turn=lat_turn, rotate_k=rotate_k, bias_qk=bias_qk, values=values,
                        scores_q=scores_q, max_turn=max_turn, scores_k=scores_k, weigh=weigh, normalise=normalise,
                        out_turn=out_turn, project=project, logits=logits, gate_turn=gate_turn,
                        acc_start=acc_start, position=position, hidden=hidden, outputs=outputs,
                        dispatch=dispatch, slots_turn=slots_turn, slot_weights=slot_weights,
                        expert_hidden=expert_hidden, expert_out=expert_out, expert_turn=expert_turn, combine=combine)
            for name, *at in ORDER:
                if name in work:
                    work[name](*at)

        @block.vector
        def _(v):
            V = nc.vector
            npair = [0]

            def next_pair():
                n = npair[0]
                npair[0] += 1
                v.wait_ge(pair_full, n + 1)
                return pair[n % 2]

            def tiles_of(b):
                return slice(b * NI, (b + 1) * NI)

            def modulation():
                v.wait_ge(act_silu, 1)
                V.tensor_scalar(silu[:, 1, :], silu[:, 0, :], 1.0, None, ALU.add).then_inc(dve_silu, 1)
                v.wait_ge(dve_silu, 1)
                V.reciprocal(silu[:, 0, :], silu[:, 1, :]).then_inc(dve_silu, 1)
                v.wait_ge(dve_silu, 2)
                V.tensor_tensor(silu[:, 2, :], cT[:], silu[:, 0, :], ALU.mult).then_inc(dve_silu, 1)
                v.wait_ge(dve_silu, 3)
                V.tensor_copy(silu_bc[:], silu[:, 2, :].unsqueeze(2).to_broadcast([P, LAYERS * B, P]))\
                    .then_inc(dve_silu, 1)
                u = next_pair()
                V.tensor_copy(modT[:], u[:, 0, 0:48].rearrange("p (l j b) -> p l j b", l=LAYERS, j=6))\
                    .then_inc(setup, 1)
                v.wait_ge(setup, 1)
                V.tensor_scalar(modT[:, :, 1::3, :], modT[:, :, 1::3, :], 1.0, None, ALU.add).then_inc(setup, 1)

            def swap_halves():
                v.wait_ge(ld_latent, n_latent)
                for w in (wq, wuk):
                    wv = w[:].rearrange("p v (h s k) -> p v h s k", s=2, k=HD // 2)
                    for s_ in range(2):
                        V.tensor_copy(wv[:, 1, :, s_, :], wv[:, 0, :, 1 - s_, :]).then_inc(swapped, 1)

            def gate_factors(L):
                u = next_pair()
                uv = u[:].rearrange("p a (b j c) -> p (a b) j c", b=2, j=2)
                if L:
                    v.wait_ge(factors, 4 * L)
                V.tensor_scalar(gsign, uv, 0.0, 2.0, ALU.is_ge, ALU.mult).then_inc(factors, 1)
                v.wait_ge(factors, 4 * L + 1)
                V.scalar_tensor_tensor(out=gabs, in0=gsign, scalar=-1.0, in1=uv,
                                       op0=ALU.add, op1=ALU.mult).then_inc(factors, 1)
                v.wait_ge(factors, 4 * L + 2)
                V.tensor_scalar(gabs, gabs, 0.25, None, ALU.max).then_inc(factors, 1)
                v.wait_ge(factors, 4 * L + 3)
                V.scalar_tensor_tensor(out=gates[:, L * B:(L + 1) * B], in0=gsign, scalar=-1.0,
                                       in1=gabs, op0=ALU.add, op1=ALU.mult).then_inc(factors, 1)

            def low_rank():
                u = next_pair()
                v.wait_ge(ld_attn, n_attn)
                V.scalar_tensor_tensor(out=wqkv[:], in0=u[:, 0, 0:3 * C], scalar=0.5, in1=wqkv[:],
                                       op0=ALU.mult, op1=ALU.add).then_inc(updated, 1)
                V.scalar_tensor_tensor(out=wo[:, 1, :], in0=u[:, 1, 0:C], scalar=0.5, in1=wo[:, 1, :],
                                       op0=ALU.mult, op1=ALU.add).then_inc(updated, 1)

            def stat(L, half, b):
                n = (2 * L + half) * B + b
                if n < B:
                    v.wait_ge(ld_x[b], 16)
                else:
                    v.wait_ge(x_done, n - B + 1)
                    v.wait_ge(ln_xn, NI * (n - B + 1))
                for i in range(NI):
                    V.bn_stats(stats[:, b, i, :], x[:, b * NI + i, :]).then_inc(ln_stat, 1)
                for i in range(NI):
                    v.wait_ge(ln_stat, NI * n + i + 1)
                    V.bn_aggr(mv[:, b, i, :], stats[:, b, i, :]).then_inc(ln_mv, 1)

            def norm(L, half, b):
                n = (2 * L + half) * B + b
                v.wait_ge(ln_mv, NI * (n + 1))
                v.wait_ge(ln_rstd, n + 1)
                for i in range(NI):
                    t = b * NI + i
                    V.tensor_scalar(xn[:, t, :], x[:, t, :], mv[:, b, i, 0:1], rstd[:, b, i:i + 1],
                                    ALU.subtract, ALU.mult).then_inc(ln_xn, 1)

            def lat(b):
                u = next_pair()
                if b:
                    v.wait_ge(latn_ready, NI * b)
                V.tensor_copy(latc[:], u[:, 0, 0:NI * LAT].rearrange("p (i c) -> p i c", i=NI))\
                    .then_inc(lat_copied, 1)
                v.wait_ge(lat_copied, b + 1)
                for i in range(NI):
                    V.bn_stats(lstats[:, i, :], latc[:, i, :]).then_inc(lat_stat, 1)
                for i in range(NI):
                    v.wait_ge(lat_stat, NI * b + i + 1)
                    V.bn_aggr(lmv[:, i, :], lstats[:, i, :]).then_inc(lat_mv, 1)

            def lat_norm(b):
                v.wait_ge(lat_mv, NI * (b + 1))
                v.wait_ge(lat_rstd, b + 1)
                if b:
                    v.wait_ge(latT_ready, b)
                for i in range(NI):
                    V.tensor_scalar(latn[:, i, :], latc[:, i, :], lmv[:, i, 0:1], lrstd[:, i:i + 1],
                                    ALU.subtract, ALU.mult).then_inc(latn_ready, 1)

            def split_parts(L, b, n):
                base = 8 * (L * B + b) + 4 * n
                if L * B + b:
                    pb = (b - 1) % B
                    v.wait_ge(scr_done[n][pb], 96 * (L + (b > 0)))
                src = full[:, n, :]
                V.tensor_copy(parts[:, n, 0, :], src).then_inc(split, 1)
                v.wait_ge(split, base + 1)
                V.tensor_tensor(rot[:, n, :], src, parts[:, n, 0, :], ALU.subtract).then_inc(split, 1)
                v.wait_ge(split, base + 2)
                V.tensor_copy(parts[:, n, 1, :], rot[:, n, :]).then_inc(split, 1)
                v.wait_ge(split, base + 3)
                V.tensor_tensor(parts[:, n, 2, :], rot[:, n, :], parts[:, n, 1, :], ALU.subtract).then_inc(split, 1)

            def rotate(b, n):
                u = next_pair()
                done = 6 * b + 3 * n
                if b or n:
                    v.wait_ge(split, 8 * b + 4 * n)
                V.tensor_tensor(rot[:, 0, :], u[:, 0, :], cosT[:], ALU.mult).then_inc(rotated, 1)
                V.tensor_tensor(rot[:, 1, :], u[:, 1, :], sinT[:], ALU.mult).then_inc(rotated, 1)
                v.wait_ge(rotated, done + 2)
                V.tensor_tensor(full[:, n, :], rot[:, 0, :], rot[:, 1, :], ALU.add).then_inc(rotated, 1)
                v.wait_ge(rotated, done + 3)
                split_parts(0, b, n)

            def rotate_q(b):
                rotate(b, 0)

            def rotate_k(b):
                rotate(b, 1)

            def bias_qk(b):
                u = next_pair()
                v.wait_ge(split, 8 * (B + b))
                for n in range(2):
                    V.tensor_scalar(full[:, n, :], u[:, n, :], bqk[:, n:n + 1], None, ALU.add).then_inc(biased, 1)
                for n in range(2):
                    v.wait_ge(biased, 2 * b + n + 1)
                    split_parts(1, b, n)

            def values(L, b):
                u = next_pair()
                if L * B + b == 0:
                    v.wait_ge(pool_init, 5)
                dst = vaug[:, tiles_of(b), 0:NH * VW].rearrange("p i (h k) -> p i h k", k=VW)[:, :, :, 0:HD]
                src = u[:, 0, :].rearrange("p (i h k) -> p i h k", i=NI, h=NH)
                for i in range(NI):
                    if L == 0:
                        V.tensor_copy(dst[:, i], src[:, i]).then_inc(v_ready, 1)
                    else:
                        V.tensor_tensor(dst[:, i], src[:, i], bv[:].rearrange("p (h k) -> p h k", k=HD), ALU.add)\
                            .then_inc(v_ready, 1)

            def scores_q(L, s, k):
                u = next_pair()
                gs = L * STEPS + s
                nm = negmax[:, s % 2]
                if k == 0 and gs >= 2:
                    v.wait_ge(msplit, 4 * (gs - 1))
                pr = k // 2
                if k == 4:
                    V.tensor_reduce(nm[:, :, :, 1], u[:].rearrange("p j (r n) -> p r j n", r=2), AX, ALU.max,
                                    negate=True).then_inc(reduced, 1)
                    split_max(gs)
                elif k % 2 == 0:
                    V.tensor_reduce(nm[:, :, pr, 3], u[:], AX, ALU.max, negate=True).then_inc(reduced, 1)
                else:
                    V.tensor_reduce(nm[:, :, pr, 2], u[:, :, 0:384], AX, ALU.max, negate=True)\
                        .then_inc(reduced, 1)
                    V.tensor_reduce(nm[:, :, pr, 0], u[:, :, 384:512], AX, ALU.max, negate=True)\
                        .then_inc(reduced, 1)

            def split_max(gs):
                v.wait_ge(reduced, 7 * (gs + 1))
                src, dst = negmax[:, gs % 2].rearrange("p r j i -> p r (j i)"), mparts[:, gs % 2]
                V.tensor_copy(dst[:, :, 0, :], src).then_inc(msplit, 1)
                v.wait_ge(msplit, 4 * gs + 1)
                V.tensor_tensor(mres[:], src, dst[:, :, 0, :], ALU.subtract).then_inc(msplit, 1)
                v.wait_ge(msplit, 4 * gs + 2)
                V.tensor_copy(dst[:, :, 1, :], mres[:]).then_inc(msplit, 1)
                v.wait_ge(msplit, 4 * gs + 3)
                V.tensor_tensor(dst[:, :, 2, :], mres[:], dst[:, :, 1, :], ALU.subtract).then_inc(msplit, 1)

            def max_turn(L, s):
                gs = L * STEPS + s
                u = next_pair()
                if gs >= 2:
                    gp = gs - 2
                    v.wait_ge(m_out[gp % NG], 16 * (gp // NG + 1))
                V.tensor_copy(mT[:, s % 2, :], u[0:48, 0, :].bitcast(BF16)[:, 0:P]).then_inc(m_copied, 1)

            def normalise(L, s):
                gs = L * STEPS + s
                b, g = divmod(s, NG)
                u = next_pair()
                uv = u[:, 0, :].rearrange("p (i h k) -> p i h k", i=NI, h=GH)
                if gs:
                    v.wait_ge(o_step, 2 * gs)
                V.reciprocal(rec[:], uv[:, :, :, HD]).then_inc(o_step, 1)
                v.wait_ge(o_step, 2 * gs + 1)
                dst = o_nat[:, b % 2, :, g * GH * HD:(g + 1) * GH * HD].rearrange("p i (h k) -> p i h k", h=GH)
                V.tensor_tensor(dst, uv[:, :, :, 0:HD], rec[:].unsqueeze(3).to_broadcast([P, NI, GH, HD]),
                                ALU.mult).then_inc(o_step, 1)

            def out_turn(L, b):
                u = next_pair()
                V.tensor_copy(oT[:], u[:, 0, :]).then_inc(oT_ready, 1)

            def residual(src, L, half, b):
                n = (2 * L + half) * B + b + 1
                gb = gates[:, L * B + b, half, :].unsqueeze(1).to_broadcast([P, NI, C])
                if n == 1:
                    v.wait_ge(factors, 4 * LAYERS)
                else:
                    v.wait_ge(x_done, n - 1)
                V.tensor_tensor(upd[:], src, gb, ALU.mult).then_inc(gated, 1)
                v.wait_ge(gated, n)
                xb = x[:, tiles_of(b), :]
                V.tensor_tensor(xb, xb, upd[:], ALU.add).then_inc(x_done, 1)

            def project(L, b):
                residual(next_pair()[:, 0, :].rearrange("p (i c) -> p i c", i=NI), L, 0, b)

            def logits(L, b):
                ts = tiles_of(b)
                u = next_pair()
                lgp = u[:, 0, 0:NI * NE].rearrange("p (t e) -> p t e", e=NE)
                if L == 0:
                    if b == 0:
                        v.wait_ge(ld_attn, n_attn)
                    V.tensor_tensor(lg[:, ts, :], lgp, br[:].unsqueeze(1).to_broadcast([P, NI, NE]), ALU.add)\
                        .then_inc(logits_read, 1)
                    v.wait_ge(logits_read, b + 1)
                    top_two(b)
                    V.tensor_tensor(wk[:, 0, ts], top[:, ts, 1], top[:, ts, 0], ALU.subtract).then_inc(exp_in, 1)
                else:
                    V.tensor_copy(lg[:, ts, :], lgp).then_inc(logits_read, 1)
                    v.wait_ge(logits_read, B + b + 1)
                    r(V.tensor_reduce(wk[:, 0, ts], lg[:, ts, :], AX, ALU.max))
                    V.tensor_tensor(lgs[:, ts, :], lg[:, ts, :], bc(wk[:, 0, ts]), ALU.subtract)\
                        .then_inc(exp_in, 1)

            nroute = [0]

            def r(ins):
                nroute[0] += 1
                ins.then_inc(route_step, 1)
                v.wait_ge(route_step, nroute[0])

            def bc(col):
                return col.unsqueeze(2).to_broadcast([P, NI, NE])

            def top_two(b):
                for t in range(b * NI, (b + 1) * NI):
                    V.max(top[:, t, :], lg[:, t, :]).then_inc(route_step, 1)
                for t in range(b * NI, (b + 1) * NI):
                    nroute[0] += 1
                    v.wait_ge(route_step, nroute[0])
                    V.max_index(topi[:, t, :], top[:, t, :], lg[:, t, :]).then_inc(route_step, 1)
                nroute[0] += NI
                v.wait_ge(route_step, nroute[0])
                r(V.tensor_copy(topf[:, tiles_of(b)], topi[:, tiles_of(b), 0:2]))

            def route(L, b):
                ts = tiles_of(b)
                v.wait_ge(exp_out, L * B + b + 1)
                if L == 0:
                    r(V.tensor_scalar(wk[:, 0, ts], wk[:, 1, ts], 1.0, None, ALU.add))
                    r(V.reciprocal(wk[:, 2, ts], wk[:, 0, ts]))
                    r(V.tensor_tensor(wk[:, 3, ts], wk[:, 1, ts], wk[:, 2, ts], ALU.mult))
                    wts = (wk[:, 2, ts], wk[:, 3, ts])
                else:
                    r(V.tensor_reduce(wk[:, 1, ts], ex[:, ts, :], AX, ALU.add))
                    r(V.reciprocal(wk[:, 2, ts], wk[:, 1, ts]))
                    r(V.tensor_tensor(lg[:, ts, :], ex[:, ts, :], bc(wk[:, 2, ts]), ALU.mult))
                    top_two(b)
                    wts = (top[:, ts, 0], top[:, ts, 1])
                for k in range(2):
                    r(V.tensor_tensor(oh[:, k, ts], iota8[:].unsqueeze(1).to_broadcast([P, NI, NE]),
                                      bc(topf[:, ts, k]), ALU.is_equal))
                if L == 1:
                    V.tensor_tensor(sel[:, ts], oh[:, 0, ts], oh[:, 1, ts], ALU.add).then_inc(chosen, 1)
                    v.wait_ge(chosen, 2 * b + 1)
                    V.tensor_scalar(away[:, ts], sel[:, ts], -FAR, FAR, ALU.mult, ALU.add).then_inc(chosen, 1)
                for k in range(2):
                    r(V.tensor_tensor(oh[:, k, ts], oh[:, k, ts], bc(wts[k]), ALU.mult))
                V.tensor_tensor(gate[:, ts], oh[:, 0, ts], oh[:, 1, ts], ALU.add).then_inc(gate_ready, 1)

            def gate_turn(b):
                u = next_pair()
                if b:
                    v.wait_ge(acc_started, b)
                V.tensor_copy(gT[:], u[0:NE, 0, :]).then_inc(gT_ready, 1)

            def acc_start(b):
                u = next_pair()
                V.tensor_copy(acc[:, tiles_of(b), :], u[:, 0, :].rearrange("p (t c) -> p t c", t=NI))\
                    .then_inc(acc_started, 1)

            def position(b):
                u = next_pair()
                v.wait_ge(chosen, 2 * (b + 1))
                V.tensor_tensor(pos[:, tiles_of(b)], u[:, 0, 0:NI * NE].rearrange("p (t e) -> p t e", e=NE),
                                away[:, tiles_of(b)], ALU.add).then_inc(pos_ready, 1)

            def outputs(n):
                b, e = divmod(n, NE)
                u = next_pair()
                if e == 0:
                    v.wait_ge(gate_ready, b + 1)
                    v.wait_ge(acc_started, b + 1)
                for i in range(NI):
                    t = b * NI + i
                    if e:
                        v.wait_ge(acc_step, NI * (n - 1) + i + 1)
                    V.scalar_tensor_tensor(out=acc[:, t, :], in0=u[:, 0, i * C:(i + 1) * C],
                                           scalar=gate[:, t, e:e + 1], in1=acc[:, t, :],
                                           op0=ALU.mult, op1=ALU.add).then_inc(acc_step, 1)

            def gate_residual(b):
                v.wait_ge(acc_step, NI * NE * (b + 1))
                residual(acc[:, tiles_of(b), :], 0, 1, b)

            def split_gates(b):
                ts = tiles_of(b)
                v.wait_ge(gate_ready, B + b + 1)
                if b:
                    v.wait_ge(gsplit, 4 * b)
                V.tensor_copy(gparts[:, ts, :, 0], gate[:, ts]).then_inc(gsplit, 1)
                v.wait_ge(gsplit, 4 * b + 1)
                V.tensor_tensor(gres[:], gate[:, ts], gparts[:, ts, :, 0], ALU.subtract).then_inc(gsplit, 1)
                v.wait_ge(gsplit, 4 * b + 2)
                V.tensor_copy(gparts[:, ts, :, 1], gres[:]).then_inc(gsplit, 1)
                v.wait_ge(gsplit, 4 * b + 3)
                V.tensor_tensor(gparts[:, ts, :, 2], gres[:], gparts[:, ts, :, 1], ALU.subtract)\
                    .then_inc(gsplit, 1)

            def split_rows(b):
                v.wait_ge(ln_xn, NI * (3 * B + b + 1))
                if b < 2:
                    v.wait_ge(scr_done[b][B - 1], 96 * LAYERS)
                    v.wait_ge(split, 8 * LAYERS * B)
                else:
                    v.wait_ge(buf_ready, 2 * (b - 1))
                    v.wait_ge(xsplit, 4 * (b - 1))
                src = xn[:, tiles_of(b), :].rearrange("p i c -> p (i c)")
                dst, res = parts[:, b % 2], rot[:, b % 2, :]
                V.tensor_copy(dst[:, 0, :], src).then_inc(xsplit, 1)
                v.wait_ge(xsplit, 4 * b + 1)
                V.tensor_tensor(res, src, dst[:, 0, :], ALU.subtract).then_inc(xsplit, 1)
                v.wait_ge(xsplit, 4 * b + 2)
                V.tensor_copy(dst[:, 1, :], res).then_inc(xsplit, 1)
                v.wait_ge(xsplit, 4 * b + 3)
                V.tensor_tensor(dst[:, 2, :], res, dst[:, 1, :], ALU.subtract).then_inc(xsplit, 1)

            def fill_slots(b):
                v.wait_ge(pos_ready, b + 1)
                if b == 0:
                    v.wait_ge(pv_done, LAYERS * STEPS)
                elif b > 1:
                    v.wait_ge(slot_w_ready, b - 1)
                for i in range(NI):
                    V.tensor_tensor(slots[b % 2][:, i], iota_s[:].unsqueeze(1).to_broadcast([P, NE, CAPACITY]),
                                    pos[:, b * NI + i, :].unsqueeze(2).to_broadcast([P, NE, CAPACITY]),
                                    ALU.is_equal).then_inc(slots_ready, 1)

            def slot_weights(b):
                u = next_pair()
                V.tensor_reduce(slot_w[0:CAPACITY, :, b], u[0:CAPACITY, 0, 0:3 * NE].rearrange("p (e k) -> p e k", e=NE),
                                AX, ALU.add).then_inc(slot_w_ready, 1)

            def expert_turn(e):
                v.wait_ge(y_turned, e + 1)
                if e == 0:
                    v.wait_ge(slot_w_ready, B)
                    v.wait_ge(xsplit, 4 * B)
                else:
                    v.wait_ge(y_split, 5 * e)
                y, res, dst = full[0:CAPACITY, 0, :], rot[0:CAPACITY, 0, :], parts[0:CAPACITY, e % 2]
                V.tensor_tensor(y.rearrange("p (b c) -> p b c", b=B),
                                pvb[0:CAPACITY, :].rearrange("p (b c) -> p b c", b=B),
                                slot_w[0:CAPACITY, e, :].unsqueeze(2).to_broadcast([CAPACITY, B, C]), ALU.mult)\
                    .then_inc(y_split, 1)
                v.wait_ge(y_split, 5 * e + 1)
                V.tensor_copy(dst[:, 0, :], y).then_inc(y_split, 1)
                v.wait_ge(y_split, 5 * e + 2)
                V.tensor_tensor(res, y, dst[:, 0, :], ALU.subtract).then_inc(y_split, 1)
                v.wait_ge(y_split, 5 * e + 3)
                V.tensor_copy(dst[:, 1, :], res).then_inc(y_split, 1)
                v.wait_ge(y_split, 5 * e + 4)
                V.tensor_tensor(dst[:, 2, :], res, dst[:, 1, :], ALU.subtract).then_inc(y_split, 1)

            def finish(b):
                v.wait_ge(summed, b + 1)
                residual(pair[b // 2][:, b % 2, :].rearrange("p (i c) -> p i c", i=NI), 1, 1, b)

            work = dict(modulation=modulation, swap_halves=swap_halves, gate_factors=gate_factors,
                        low_rank=low_rank, stat=stat, norm=norm, lat=lat, rotate_q=rotate_q, lat_norm=lat_norm,
                        rotate_k=rotate_k, bias_qk=bias_qk, values=values, scores_q=scores_q, max_turn=max_turn,
                        normalise=normalise, out_turn=out_turn, project=project, logits=logits, route=route,
                        gate_turn=gate_turn, acc_start=acc_start, position=position, outputs=outputs,
                        gate_residual=gate_residual, split_gates=split_gates, split_rows=split_rows,
                        fill_slots=fill_slots, slot_weights=slot_weights, expert_turn=expert_turn, finish=finish)
            for name, *at in ORDER:
                if name in work:
                    work[name](*at)


def with_extras(base, extras):
    out, k = [], 0
    for n, stage in enumerate(base):
        out.append(stage)
        upto = len(extras) * (n + 1) // len(base)
        out += extras[k:upto]
        k = upto
    return out


def norm_stages(L, half, b):
    return [("stat", L, half, b), ("norm", L, half, b), ("turn", L, half, b)]


def input_stages(L, b):
    if L == 0:
        return [("lat", b), ("rotate_q", b), ("lat_norm", b), ("lat_turn", b), ("rotate_k", b), ("values", L, b)]
    return [("bias_qk", b), ("values", L, b)]


def routing_stages(L, b):
    out = norm_stages(L, 1, b) + [("logits", L, b), ("route_exp", L, b), ("route", L, b)]
    return out + ([("gate_turn", b), ("acc_start", b)] if L == 0 else [("position", b)])


def attention_step(L, s, extras):
    base = []
    for u in range(ST_UNITS):
        base.append(("scores_k", L, s, u))
        if u % 2 and s + NG < STEPS:
            base.append(("scores_q", L, s + NG, u // 2))
        if s and u == 4:
            base.append(("weigh", L, s - 1))
        if s and u == 6:
            base.append(("weigh_copy", L, s - 1))
    if s + NG - 1 < STEPS:
        base.append(("max_turn", L, s + NG - 1))
    if s:
        base.append(("normalise", L, s - 1))
    return with_extras(base, extras)


def first_scores(L):
    out = []
    for s in range(NG):
        out += [("scores_q", L, s, k) for k in range(5)]
        if s:
            out.append(("max_turn", L, s - 1))
    return out


def attention_stages(L, more):
    out = []
    pending = []
    for s in range(STEPS):
        extras = list(more.get(s, []))
        b, r = divmod(s, NG)
        if b:
            done = routing_stages(L, b - 1)
            extras += {0: [], 1: [("out_turn", L, b - 1)], 2: [("project", L, b - 1)] + done[:1],
                       3: done[1:4]}[r]
        if r == 0 and b > 1:
            extras = routing_stages(L, b - 2)[4:] + extras
        out += attention_step(L, s, extras)
    return out


def tail_stages(L):
    last = routing_stages(L, B - 1)
    return ([("weigh", L, STEPS - 1), ("weigh_copy", L, STEPS - 1)],
            routing_stages(L, B - 2)[4:] + [("normalise", L, STEPS - 1), ("out_turn", L, B - 1),
                                            ("project", L, B - 1)] + last)


def order():
    out = [("modulation",)]
    n = [norm_stages(0, 0, b) for b in range(B)]
    out += n[0][:1] + n[1][:1] + n[0][1:] + [("swap_halves",)] + input_stages(0, 0) + n[1][1:] + n[2][:1] + input_stages(0, 1)
    out += with_extras(first_scores(0), n[3][:1] + n[2][1:] + n[3][1:] +
                        [("gate_factors", 0), ("gate_factors", 1), ("low_rank",)])
    out += attention_stages(0, {0: input_stages(0, 2)[:3], 1: input_stages(0, 2)[3:],
                                4: input_stages(0, 3)[:3], 5: input_stages(0, 3)[3:]})
    now, tail = tail_stages(0)
    out += now
    groups = []
    for b in range(B):
        for e in range(NE):
            nth = b * NE + e
            if nth == 0:
                groups.append([("hidden", 0)])
            groups.append(([("hidden", nth + 1)] if nth + 1 < B * NE else []) + [("outputs", nth)])
    flat = groups[0]
    g = groups[1:]
    later = [[("gate_residual", b)] + norm_stages(1, 0, b) + input_stages(1, b) for b in range(B)]
    flat += sum(with_extras(g[0:NE], [[t] for t in tail]), [])
    flat += sum(with_extras(g[NE:2 * NE], [[t] for t in later[0]]), [])
    first = first_scores(1)
    cut = len(first) // 2
    flat += sum(with_extras(g[2 * NE:3 * NE], [[t] for t in later[1] + first[:cut]]), [])
    flat += sum(with_extras(g[3 * NE:], [[t] for t in later[2] + first[cut:]]), [])
    out += flat
    out += attention_stages(1, {0: later[3][:3], 1: later[3][3:5], 2: later[3][5:]})
    now, tail = tail_stages(1)

    def dispatch(b):
        return [("split_gates", b), ("split_rows", b), ("fill_slots", b), ("dispatch", b, 0), ("dispatch", b, 1)] + \
               [("slots_turn", b, i) for i in range(NI)] + [("slot_weights", b)]

    out += with_extras(now + dispatch(0) + dispatch(1), tail[:-len(routing_stages(1, B - 1)) + 3])
    out += with_extras(dispatch(2), tail[-len(routing_stages(1, B - 1)) + 3:])
    out += dispatch(3)
    out += [("expert_hidden", 0), ("expert_out", 0), ("expert_hidden", 1)]
    for e in range(NE):
        out.append(("expert_turn", e))
        if e + 1 < NE:
            out.append(("expert_out", e + 1))
        if e + 2 < NE:
            out.append(("expert_hidden", e + 2))
        out.append(("combine", e))
    return out + [("finish", b) for b in range(B)]


ORDER = order()


def kernel(**inputs):
    import ml_dtypes
    import concourse.bacc as bacc
    from concourse.bass_utils import run_bass_kernel_spmd

    f32, bf = np.float32, ml_dtypes.bfloat16
    ins = {k: np.ascontiguousarray(inputs[k]) for k in inputs}

    as_is = ["L0_attn_x", "L0_attn_W_q", "L0_attn_W_dkv", "L0_attn_W_uk", "L0_attn_W_uv", "L0_attn_W_o",
             "L0_ffn_Wr", "L0_ffn_W1", "L0_ffn_W2", "L0_ffn_b2", "L0_wmod", "L1_attn_la_attn", "L1_attn_la_proj",
             "L1_ffn_Wr", "L1_ffn_W1", "L1_ffn_W2", "L1_wmod"]
    arrays = {k: ins[k] for k in as_is}
    arrays["cT"] = np.concatenate([ins["L0_c"], ins["L1_c"]]).T
    arrays["lnlat"] = np.stack([ins["L0_attn_ln_gamma"], ins["L0_attn_ln_beta"]], 1)
    arrays["w_attnT"] = ins["L1_attn_w_attn"].T
    arrays["lb_attnT"] = ins["L1_attn_lb_attn"].T
    arrays["w_projT"] = ins["L1_attn_w_proj"].T
    arrays["lb_projT"] = ins["L1_attn_lb_proj"].T
    arrays["bqk"] = ins["L1_attn_b_attn"][:2 * C].reshape(2, C).T
    arrays["bv"] = np.broadcast_to(ins["L1_attn_b_attn"][2 * C:], (P, C))
    arrays["bproj"] = ins["L1_attn_b_proj"].reshape(1, C)
    arrays["br"] = np.broadcast_to(ins["L0_ffn_br"], (P, NE))
    for L in range(LAYERS):
        arrays[f"b1_{L}"] = ins[f"L{L}_ffn_b1"].reshape(NE, FC[L], P).transpose(2, 0, 1)

    arrays["b2_1"] = ins["L1_ffn_b2"].T

    row, col = np.arange(P)[:, None], np.arange(P)[None, :]
    arrays["ident"] = np.eye(P, dtype=f32)
    arrays["identb"] = np.eye(P, dtype=f32).astype(bf)
    arrays["mask_q"] = np.where(col > row, MASKED, 0).astype(bf)
    arrays["mask_k"] = np.where(row > col, MASKED, 0).astype(bf)
    arrays["before"] = (row < col).astype(bf)
    arrays["ones"] = np.ones((P, P), bf)
    arrays["tail_q"] = np.zeros((P, T), bf)
    arrays["tail_k"] = np.repeat((np.arange(P) % 16 < 3)[:, None], T, 1).astype(bf)
    arrays["iota8"] = np.repeat(np.arange(NE, dtype=f32)[None], P, 0)
    arrays["iota_s"] = np.repeat(np.arange(CAPACITY, dtype=f32)[None], P, 0)
    half = HD // 2
    inv_freq = (f32(1.0) / f32(10000.0) ** (np.arange(half, dtype=f32) / f32(half))).astype(f32)
    angles = (inv_freq[:, None] * np.arange(T, dtype=f32)[None]).astype(f32)
    cos, sin = np.cos(angles), np.sin(angles)
    arrays["cosT"] = np.tile(cos, (C // half, 1)).astype(f32)
    arrays["sinT"] = np.tile(np.concatenate([-sin, sin]), (NH, 1)).astype(f32)

    nc = bacc.Bacc("TRN2", target_bir_lowering=False, num_devices=1)
    arrays = {k: np.ascontiguousarray(x) for k, x in arrays.items()}
    aps = {k: nc.dram_tensor(f"in_{k}", x.shape, mybir.dt.from_np(x.dtype), kind="ExternalInput").ap()
           for k, x in arrays.items()}
    out = nc.dram_tensor("out_0", (B, T, C), F32, kind="ExternalOutput").ap()
    build(nc, aps, out)
    r = run_bass_kernel_spmd(nc, [{f"in_{k}": x for k, x in arrays.items()}], core_ids=[0])
    return r.results[0]["out_0"]
```

```python
from contextlib import ExitStack

import numpy as np
import concourse.bass as bass
from concourse import mybir

ALU = mybir.AluOpType
ACT = mybir.ActivationFunctionType
AX = mybir.AxisListType.X
F32 = mybir.dt.float32
BF16 = mybir.dt.bfloat16
U32 = mybir.dt.uint32

LAYERS = 2
B, T, C = 4, 512, 128
P = 128
NI = T // P
NT = B * NI
NH, HD = 16, 8
GH = 4
NG = NH // GH
STEPS = B * NG
LAT = 32
RANK = 32
NE = 8
FC = (2, 4)
CAPACITY = int(T / NE * 1.25)
EPS = 1e-5
SCALE = 1.0 / float(np.sqrt(HD))
FAR = 1e4
MASKED = -1e30
VW = HD + 1
VROW = NH * VW + 32 - VW
Q_PARTS = (0, 1, 0, 1, 0, 2)
K_PARTS = (0, 1, 1, 0, 2, 0)
MAX_ROW = HD * len(Q_PARTS)
HALF = 64
P_SLOTS = 20
W_SLOTS = 4
ST_UNITS = 10
PAIR_UNITS = (((0, 0, 0),), ((0, 1, 0), (0, 3, 384)), ((1, 0, 0),), ((1, 1, 0), (1, 3, 384)),
              ((0, 2, 0), (1, 2, 256)))


PACKS = dict(
    first=(("cT", LAYERS * B, P), ("ident", P, P), ("wmod_first", 2 * C, P)),
    latent=(("wq", 2 * C, P), ("wdkv", LAT, P), ("wuk", 2 * C, LAT), ("wuv", C, LAT), ("lnlat", 2, LAT)),
    rope=(("cosT", T, P), ("sinT", T, P)),
    bits=(("identb", P, P), ("mask_q", P, P), ("mask_k", P, P), ("before", P, P), ("ones", P, P)),
    rest=(("wqkv", 3 * C, P), ("la_attn", C, RANK), ("lb_attn", 3 * C, RANK), ("la_proj", C, RANK),
          ("lb_proj", C, RANK), ("bqk", 2, P), ("bv", C, P), ("bproj", C, 1), ("wo", LAYERS * C, P),
          ("wr", LAYERS * NE, P), ("br", NE, P), ("b1_0", NE * FC[0], P), ("b1_1", NE * FC[1], P),
          ("b2_0", C, NE), ("b2_1", NE, P), ("iota8", NE, P), ("iota_s", CAPACITY, P)))


def build(nc, a, out):
    with ExitStack() as ctx:
        def sb(name, shape, dt=F32):
            return ctx.enter_context(nc.sbuf_tensor(name, shape, dt))

        def sem(name):
            return ctx.enter_context(nc.semaphore(name))

        x = sb("x", [P, NT, C])
        xn = sb("xn", [P, NT, C])
        acc = xn
        hT = sb("hT", [P, B * T])
        packs, loaded = {}, {}
        for pack, items in PACKS.items():
            packs[pack] = sb(pack, [P, sum(n for _, n, _ in items)], BF16 if pack == "bits" else F32)
            at = 0
            for name, n, rows in items:
                loaded[name] = packs[pack][0:rows, at:at + n]
                at += n
        cT, ident, identb = loaded["cT"], loaded["ident"], loaded["identb"]
        mask_q, mask_k = loaded["mask_q"], loaded["mask_k"]
        before, ones = loaded["before"], loaded["ones"]
        cosT, sinT = loaded["cosT"], loaded["sinT"]
        wmod_first = loaded["wmod_first"]
        wq, wuk = (loaded[n].rearrange("p (v c) -> p v c", v=2) for n in ("wq", "wuk"))
        wuv, wdkv, lnlat = loaded["wuv"], loaded["wdkv"], loaded["lnlat"]
        wqkv, bqk, bv, bproj = loaded["wqkv"], loaded["bqk"], loaded["bv"], loaded["bproj"]
        la_attn, lb_attn, la_proj, lb_proj = (loaded[n] for n in ("la_attn", "lb_attn", "la_proj", "lb_proj"))
        wo, wr = (loaded[n].rearrange("p (l c) -> p l c", l=LAYERS) for n in ("wo", "wr"))
        br, iota8, iota_s = loaded["br"], loaded["iota8"], loaded["iota_s"]
        b1 = [loaded[f"b1_{L}"].rearrange("p (e f) -> p e f", e=NE) for L in range(LAYERS)]
        b2_0, b2_1 = loaded["b2_0"], loaded["b2_1"]
        onesf = sb("onesf", [1, P])
        silu = sb("silu", [P, 3, LAYERS * B])
        modT = sb("modT", [P, LAYERS, 6, B])
        gates = sb("gates", [P, LAYERS * B, 2, C])
        w1 = sb("w1", [P, NE * FC[0] * P])
        w2 = sb("w2", [P, NE * FC[0] * C])
        negh = sb("negh", [P, NI])
        stats = sb("stats", [P, B, NI, 6])
        mv = sb("mv", [P, B, NI, 2])
        ve = sb("ve", [P, B, NI])
        rstd = sb("rstd", [P, B, NI])
        latc = sb("latc", [P, NI, LAT])
        lstats = sb("lstats", [P, NI, 6])
        lmv = sb("lmv", [P, NI, 2])
        lve = sb("lve", [P, NI])
        lrstd = sb("lrstd", [P, NI])
        parts = sb("parts", [P, 2, 3, T], BF16)
        latn = sb("latn", [P, NI, LAT])
        vaug = sb("vaug", [P, NT, VROW])
        qop = sb("qop", [P, 2, NH // 2, T], BF16)
        kop = sb("kop", [P, 2, NH, T], BF16)
        negmax = sb("negmax", [P, 2, 2, 2, NI])
        mres = sb("mres", [P, 2, 2 * NI])
        mparts = sb("mparts", [P, 2, 2, 3, 2 * NI], BF16)
        mT = sb("mT", [48, 2, P], BF16)
        latT = sb("latT", [LAT, T])
        rot = sb("rot", [P, 2, T])
        full = sb("full", [P, 2, T])
        gT = sb("gT", [NE, T])
        pw = sb("pw", [P, P_SLOTS, T])
        wmod = pw[:, 0:3,:].rearrange("p a n -> p (a n)").rearrange("p (l n) -> p l n", l=LAYERS)
        oT4 = sb("oT4", [P, 2, T])
        rec = sb("rec", [P, NI, GH])
        o_nat = sb("o_nat", [P, 2, NI, C])
        oT = sb("oT", [P, T])
        gsign = sb("gsign", [P, LAYERS, 2, B])
        gsize = sb("gsize", [P, LAYERS, 2, B])
        upd = sb("upd", [P, NI, C])
        lg = sb("lg", [P, NT, NE])
        lgs = sb("lgs", [P, NT, NE])
        ex = sb("ex", [P, NT, NE])
        top = sb("top", [P, NT, 8])
        topi = sb("topi", [P, NT, 8], U32)
        topf = sb("topf", [P, NT, 2])
        wk = sb("wk", [P, 4, NT])
        oh = sb("oh", [P, 2, NT, NE])
        gate = sb("gate", [P, NT, NE])
        sel = sb("sel", [P, NT, NE], BF16)
        away = sb("away", [P, NT, NE])
        pos = sb("pos", [P, NT, NE])
        gres = sb("gres", [P, NI, NE])
        gparts = sb("gparts", [P, NT, NE, 3], BF16)
        slot_w = sb("slot_w", [P, NE, B])
        kflat = kop[:].rearrange("p a h t -> p a (h t)")
        qflat = qop[:].rearrange("p a h t -> p a (h t)")
        NS = NE * CAPACITY
        slots = [kflat[:, 0, k * NI * NS:(k + 1) * NI * NS].rearrange("p (i e n) -> p i e n", i=NI, e=NE)
                 for k in range(2)]
        slotsT = [kflat[0:CAPACITY, 1, 0:NE * T], kflat[0:CAPACITY, 1, NE * T:2 * NE * T],
                  qflat[0:CAPACITY, 0,:], qflat[0:CAPACITY, 1,:]]
        slotsT = [t.rearrange("p (e t) -> p e t", e=NE) for t in slotsT]
        bufT = pw[:, 0:5,:].rearrange("p a n -> p (a n)").rearrange("p (e b n) -> p e b n", e=NE, b=B)
        hid1 = pw[:, 5:10,:].rearrange("p a n -> p (a n)").rearrange("p (k f n) -> p k f n", k=2, f=FC[1])

        bank = [ctx.enter_context(nc.psum_tensor(f"bank{i}", [P, 512], F32)) for i in range(3)]
        pair = [ctx.enter_context(nc.psum_tensor(f"pair{i}", [P, 2, 512], F32)) for i in range(2)]
        pvb = ctx.enter_context(nc.psum_tensor("pvb", [P, 512], F32))

        scr_q = nc.dram_tensor("scr_q", (B, NH, MAX_ROW + 3, T), BF16, kind="Internal").ap()
        scr_k = nc.dram_tensor("scr_k", (B, NH, MAX_ROW, T), BF16, kind="Internal").ap()
        scr_m = nc.dram_tensor("scr_m", (B, NG, 48, P), BF16, kind="Internal").ap()

        ld_x = [sem(f"ld_x{b}") for b in range(B)]
        ld = {pack: sem(f"ld_{pack}") for pack in PACKS}
        ld_mod, ld_moe, copied = sem("ld_mod"), sem("ld_moe"), sem("copied")
        ld_exp = [sem(f"ld_exp{k}") for k in range(W_SLOTS)]
        tail_q, tail_k = sem("tail_q"), [sem(f"tail_k{i}") for i in range(2)]
        pool_init = sem("pool_init")
        act_silu, dve_silu, setup = sem("act_silu"), sem("dve_silu"), sem("setup")
        factored, factors, updated = sem("factored"), sem("factors"), sem("updated")
        cleared = sem("cleared")
        pair_full = sem("pair_full")
        bank_full = sem("bank_full")
        ln_stat, ln_mv, ln_ve, ln_rstd = sem("ln_stat"), sem("ln_mv"), sem("ln_ve"), sem("ln_rstd")
        lat_stat, lat_mv, lat_ve, lat_rstd = sem("lat_stat"), sem("lat_mv"), sem("lat_ve"), sem("lat_rstd")
        lat_copied = sem("lat_copied")
        ln_xn, h_ready, latn_ready, latT_ready = sem("ln_xn"), sem("h_ready"), sem("latn_ready"), sem("latT_ready")
        rotated, biased, split, v_ready = sem("rotated"), sem("biased"), [sem(f"split_{n}") for n in "qk"], sem("v_ready")
        scr_done = [[sem(f"scr_{n}{b}") for b in range(B)] for n in "qk"]
        op_loaded = [[sem(f"op_loaded{i}_{g}") for g in range(NG)] for i in range(2)]
        reduced, msplit, m_copied = sem("reduced"), sem("msplit"), sem("m_copied")
        m_out, m_in = [sem(f"m_out{g}") for g in range(NG)], [sem(f"m_in{g}") for g in range(NG)]
        weights, pv_done, pv_copied = sem("weights"), sem("pv_done"), sem("pv_copied")
        o_step, oT_ready, gated, x_done = sem("o_step"), sem("oT_ready"), sem("gated"), sem("x_done")
        logits_read, route_step, exp_in, exp_out = sem("logits_read"), sem("route_step"), sem("exp_in"), sem("exp_out")
        gate_ready, gT_ready, acc_step, hidden0 = sem("gate_ready"), sem("gT_ready"), sem("acc_step"), sem("hidden0")
        acc_started = sem("acc_started")
        chosen, pos_ready, gsplit, xsplit = sem("chosen"), sem("pos_ready"), sem("gsplit"), sem("xsplit")
        slots_ready, slotsT_ready = sem("slots_ready"), sem("slotsT_ready")
        buf_ready, slot_w_ready = sem("buf_ready"), sem("slot_w_ready")
        hidden1, yT_ready, y_turned, y_split = sem("hidden1"), sem("yT_ready"), sem("y_turned"), sem("y_split")
        summed, stored = sem("summed"), sem("stored")

        REDUCTIONS = (1, 3, 4, 6, 7)

        FIRST_MOD = [(0, 0), (0, 1)]
        OTHER_MOD = [(L, j) for L in range(LAYERS) for j in range(6) if (L, j) not in FIRST_MOD]

        w1_0 = w1[:].rearrange("p (e n) -> p e n", e=NE)
        w2_0 = w2[:].rearrange("p (e k n) -> p e k n", e=NE, k=FC[0])
        w1_1 = w1[:].rearrange("p (e n) -> p e n", e=W_SLOTS)
        w2_1 = w2[:].rearrange("p (e k n) -> p e k n", e=W_SLOTS, k=FC[1])

        block = ctx.enter_context(nc.Block())

        @block.sync
        def _(sp):
            xv = a["L0_attn_x"].rearrange("b (i p) c -> b p i c", p=P)
            def load(pack):
                sp.dma_start(packs[pack][:], a[pack]).then_inc(ld[pack], 16)

            load("first")
            sp.dma_start(x[:, 0:NI,:], xv[0]).then_inc(ld_x[0], 16)
            load("latent")
            load("rope")
            sp.dma_start(x[:, NI:2 * NI,:], xv[1]).then_inc(ld_x[1], 16)
            load("bits")
            sp.dma_start(scr_q[:,:, MAX_ROW:,:], a["zeros"]).then_inc(tail_q, 16)
            for par in range(2):
                rows = slice(par * HALF + MAX_ROW, (par + 1) * HALF)
                sp.dma_start(qop[rows], a["tail_q"]).then_inc(tail_q, 16)

            def key_tails(i):
                for par in range(2):
                    rows = slice(par * HALF + MAX_ROW, (par + 1) * HALF)
                    sp.dma_start(kop[rows, i, par::2,:], a["tail_k"]).then_inc(tail_k[i], 16)

            sp.dma_start(wmod, a["wmod"]).then_inc(ld_mod, 16)
            sp.wait_ge(cleared, 1)
            key_tails(0)
            for b in range(2, B):
                sp.dma_start(x[:, b * NI:(b + 1) * NI,:], xv[b]).then_inc(ld_x[b], 16)

            def load_expert(e):
                k = e % W_SLOTS
                if e >= W_SLOTS:
                    sp.wait_ge(y_split, 5 * (e - W_SLOTS + 1))
                sp.dma_start(w1_1[:, k,:], a["L1_ffn_W1"][e]).then_inc(ld_exp[k], 16)
                sp.dma_start(w2_1[:, k], a["L1_ffn_W2"][e].rearrange("(k p) n -> p k n", p=P))\
                  .then_inc(ld_exp[k], 16)

            def write_parts(L, b):
                for n, (scr, blocks) in enumerate(((scr_q, Q_PARTS), (scr_k, K_PARTS))):
                    for part, ready in enumerate((1, 3, 4)):
                        sp.wait_ge(split[n], 4 * (L * B + b) + ready)
                        for r in range(len(blocks)):
                            if blocks[r] == part:
                                sp.dma_start(scr[b,:, r * HD:(r + 1) * HD,:], parts[:, n, part,:])\
                                  .then_inc(scr_done[n][b], 16)

            def load_operands(L, b):
                if L == 0 and b < 2:
                    sp.wait_ge(tail_q, 48)
                    sp.wait_ge(tail_k[b], 32)
                sp.wait_ge(scr_done[0][b], 96 * (L + 1))
                sp.wait_ge(scr_done[1][b], 96 * (L + 1))
                for g in range(NG):
                    gs = L * STEPS + b * NG + g
                    if gs >= 2 * NG:
                        sp.wait_ge(pv_done, gs - 2 * NG + 1)
                    for par in range(2):
                        heads = slice(g * GH + par, (g + 1) * GH, 2)
                        row = par * HALF
                        sp.dma_start(qop[row:row + MAX_ROW + 3, b % 2, 2 * g:2 * g + 2,:],
                                     scr_q[b, heads].rearrange("h r t -> r h t")).then_inc(op_loaded[b % 2][g], 16)
                        sp.dma_start(kop[row:row + MAX_ROW, b % 2, heads,:],
                                     scr_k[b, heads].rearrange("h r t -> r h t")).then_inc(op_loaded[b % 2][g], 16)

            for L in range(LAYERS):
                write_parts(L, 0)
                load_operands(L, 0)
                if L == 0:
                    load("rest")
                    sp.wait_ge(pool_init, 5)
                    key_tails(1)
                write_parts(L, 1)
                load_operands(L, 1)
                if L == 0:
                    sp.dma_start(w1_0, a["L0_ffn_W1"].rearrange("e p n -> p e n")).then_inc(ld_moe, 16)
                    sp.dma_start(w2_0.rearrange("p e k n -> p (e k) n"),
                                 a["L0_ffn_W2"].rearrange("e (k p) n -> p (e k) n", p=P)).then_inc(ld_moe, 16)
                write_parts(L, 2)
                if L == 1:
                    sp.wait_ge(acc_step, B * NE * NI)
                    for e in range(W_SLOTS):
                        load_expert(e)
                load_operands(L, 2)
                write_parts(L, 3)
                load_operands(L, 3)
            for e in range(W_SLOTS, NE):
                load_expert(e)
            ov = out.rearrange("b (i p) c -> b p i c", p=P)
            for b in range(B):
                sp.wait_ge(x_done, (2 * LAYERS - 1) * B + b + 1)
                sp.dma_start(ov[b], x[:, b * NI:(b + 1) * NI,:]).then_inc(stored, 16)
            sp.wait_ge(stored, 16 * B)

        @block.gpsimd
        def _(pool):
            nc.gpsimd.memset(negh[:], -0.5).then_inc(pool_init, 1)
            nc.gpsimd.memset(onesf[:], 1.0).then_inc(pool_init, 1)
            pool.wait_ge(pool_init, 2)

            def clear(k):
                if k == 0:
                    nc.gpsimd.memset(vaug[:], 1.0).then_inc(pool_init, 1)
                else:
                    nc.gpsimd.memset(kop[:, 1, (k - 1) * 8:k * 8,:], 0.0).then_inc(pool_init, 1)

            def stat(L, half, b):
                n = (2 * L + half) * B + b
                pool.wait_ge(ln_mv, NI * (n + 1))
                nc.gpsimd.tensor_scalar(ve[:, b,:], mv[:, b,:, 1], EPS, None, ALU.add).then_inc(ln_ve, 1)
                pool.wait_ge(ln_ve, n + 1)
                nc.gpsimd.tensor_tensor(rstd[:, b,:], ve[:, b,:], negh[:], ALU.pow).then_inc(ln_rstd, 1)

            def lat(b):
                pool.wait_ge(lat_mv, NI * (b + 1))
                nc.gpsimd.tensor_scalar(lve[:], lmv[:,:, 1], EPS, None, ALU.add).then_inc(lat_ve, 1)
                pool.wait_ge(lat_ve, b + 1)
                nc.gpsimd.tensor_tensor(lrstd[:], lve[:], negh[:], ALU.pow).then_inc(lat_rstd, 1)

            def max_turn(L, s):
                b, g = divmod(s, NG)
                gs = L * STEPS + s
                pool.wait_ge(m_copied, gs + 1)
                pool.dma_start(scr_m[b, g], mT[:, s % 2,:]).then_inc(m_out[g], 16)
                pool.wait_ge(m_out[g], 16 * (L * B + b + 1))
                src = scr_m[b, g].rearrange("(r part k) q -> r part k q", r=2, part=3)
                for par in range(2):
                    row = par * HALF + MAX_ROW
                    pool.dma_start(qop[row:row + 3, b % 2, 2 * g:2 * g + 2,:].rearrange("p j (i q) -> p (j i) q", i=NI),
                                   src[par]).then_inc(m_in[g], 16)

            def split_part(L, b, n, k):
                if k % 2 == 0 or n == 0 or b == 0:
                    return
                base = 4 * (L * B + b)
                pool.wait_ge(split[n], base + k)
                if k == 1:
                    nc.gpsimd.tensor_tensor(rot[:, n,:], full[:, n,:], parts[:, n, 0,:], ALU.subtract)\
                        .then_inc(split[n], 1)
                else:
                    nc.gpsimd.tensor_tensor(parts[:, n, 2,:], rot[:, n,:], parts[:, n, 1,:], ALU.subtract)\
                        .then_inc(split[n], 1)

            work = dict(clear=clear, stat=stat, lat=lat, max_turn=max_turn, split_part=split_part)
            for name, *at in ORDER:
                if name in work:
                    work[name](*at)

        @block.scalar
        def _(act):
            nb = [0]

            def next_bank():
                nb[0] += 1
                act.wait_ge(bank_full, nb[0])
                return bank[(nb[0] - 1) % 3]

            def silus():
                act.wait_ge(ld["first"], 16)
                nc.scalar.activation(silu[:, 0,:], cT[:], ACT.Exp, scale=-1.0).then_inc(act_silu, 1)

            def turn(L, half, b):
                src = next_bank()
                if L == half == b == 0:
                    act.wait_ge(setup, 1)
                elif L == b == 0:
                    act.wait_ge(setup, 3)
                nc.scalar.activation(hT[:, b * T:(b + 1) * T], src[:], ACT.Identity,
                                     scale=modT[:, L, 3 * half + 1, b:b + 1],
                                     bias=modT[:, L, 3 * half, b:b + 1]).then_inc(h_ready, 1)

            def gate_factors(L, half):
                src = next_bank()
                nc.scalar.activation(gates[:, L * B:(L + 1) * B, half,:],
                                     src[:].rearrange("p (b c) -> p b c", b=B), ACT.Copy).then_inc(factors, 1)

            def lat_turn(b):
                src = next_bank()
                act.wait_ge(ld["latent"], 16)
                nc.scalar.activation(latT[:], src[0:LAT,:], ACT.Identity, scale=lnlat[:, 0:1],
                                     bias=lnlat[:, 1:2]).then_inc(latT_ready, 1)

            def bias_qk(b):
                for n in range(2):
                    src = next_bank()
                    act.wait_ge(split[n], 4 * (B + b))
                    nc.scalar.activation(full[:, n,:], src[:], ACT.Identity, bias=bqk[:, n:n + 1])\
                        .then_inc(biased, 1)

            def split_part(L, b, n, k):
                if k % 2:
                    return
                base = 4 * (L * B + b)
                if k == 0:
                    if L == 0:
                        act.wait_ge(rotated, 6 * b + 3 * n + 3)
                    else:
                        act.wait_ge(biased, 2 * b + n + 1)
                    if L * B + b:
                        act.wait_ge(scr_done[n][(b - 1) % B], 96 * (L + (b > 0)))
                    nc.scalar.activation(parts[:, n, 0,:], full[:, n,:], ACT.Copy).then_inc(split[n], 1)
                else:
                    act.wait_ge(split[n], base + 2)
                    nc.scalar.activation(parts[:, n, 1,:], rot[:, n,:], ACT.Copy).then_inc(split[n], 1)

            def scores_k(L, s, u):
                src = next_bank()
                gs = L * STEPS + s
                if u == 0 and gs >= 2:
                    act.wait_ge(pv_done, gs - 1)
                nc.scalar.activation(pw[:, (s % 2) * ST_UNITS + u,:], src[:], ACT.Exp, scale=SCALE)\
                    .then_inc(weights, 1)

            def max_turn(L, s):
                src = next_bank()
                gs = L * STEPS + s
                if gs >= 2:
                    gp = gs - 2
                    act.wait_ge(m_out[gp % NG], 16 * (gp // NG + 1))
                nc.scalar.activation(mT[:, s % 2,:], src[0:48,:].bitcast(BF16)[:, 0:P], ACT.Copy)\
                    .then_inc(m_copied, 1)

            def out_turn(L, b):
                src = next_bank()
                nc.scalar.activation(oT[:], src[:], ACT.Copy).then_inc(oT_ready, 1)

            def weigh_copy(L, s):
                gs = L * STEPS + s
                act.wait_ge(pv_done, gs + 1)
                if gs >= 2:
                    act.wait_ge(o_step, 2 * (gs - 1))
                nc.scalar.activation(oT4[:, gs % 2,:], pvb[:], ACT.Copy).then_inc(pv_copied, 1)

            def route_exp(L, b):
                ts = slice(b * NI, (b + 1) * NI)
                act.wait_ge(exp_in, L * B + b + 1)
                if L == 0:
                    nc.scalar.activation(wk[:, 1, ts], wk[:, 0, ts], ACT.Exp).then_inc(exp_out, 1)
                else:
                    nc.scalar.activation(ex[:, ts,:], lgs[:, ts,:], ACT.Exp).then_inc(exp_out, 1)

            def hidden(n):
                if n == 0:
                    act.wait_ge(ld["rest"], 16)
                b, e = divmod(n, NE)
                for f in range(FC[0]):
                    src = next_bank()
                    nc.scalar.activation(pw[:, (n % 3) * FC[0] + f,:], src[:], ACT.Relu,
                                         bias=b1[0][:, e, f:f + 1]).then_inc(hidden0, 1)

            def dispatch(b, k):
                src = next_bank()
                nc.scalar.activation(bufT[:, k * 4:(k + 1) * 4, b,:],
                                     src[:, 0:4 * CAPACITY].rearrange("p (e n) -> p e n", e=4), ACT.Identity,
                                     scale=modT[:, 1, 4, b:b + 1], bias=modT[:, 1, 3, b:b + 1])\
                    .then_inc(buf_ready, 1)

            def slots_turn(b, i):
                src = next_bank()
                nc.scalar.activation(slotsT[b][:,:, i * P:(i + 1) * P],
                                     src[0:CAPACITY,:].bitcast(BF16).rearrange("p (e n) -> p e n", e=NE),
                                     ACT.Copy).then_inc(slotsT_ready, 1)

            def expert_hidden(e):
                for f in range(FC[1]):
                    src = next_bank()
                    nc.scalar.activation(hid1[:, e % 2, f,:], src[:, 0:B * CAPACITY], ACT.Relu,
                                         bias=b1[1][:, e, f:f + 1]).then_inc(hidden1, 1)

            def expert_out(e):
                src = next_bank()
                nc.scalar.activation(oT4[:, e % 2, 0:B * CAPACITY], src[:, 0:B * CAPACITY], ACT.Identity,
                                     bias=b2_1[:, e:e + 1]).then_inc(yT_ready, 1)

            work = dict(silus=silus, gate_factors=gate_factors, turn=turn, lat_turn=lat_turn, scores_k=scores_k,
                        bias_qk=bias_qk, split_part=split_part, max_turn=max_turn, out_turn=out_turn, weigh_copy=weigh_copy, route_exp=route_exp, hidden=hidden, dispatch=dispatch,
                        slots_turn=slots_turn, expert_hidden=expert_hidden, expert_out=expert_out)
            for name, *at in ORDER:
                if name in work:
                    work[name](*at)

        @block.tensor
        def _(pe):
            mm = nc.tensor.matmul
            np_, nb = [0], [0]
            pair_read, bank_read = [None, None], [None, None, None]

            def next_pair(*reader):
                n = np_[0] % 2
                np_[0] += 1
                if pair_read[n]:
                    pe.wait_ge(*pair_read[n])
                pair_read[n] = reader
                return pair[n]

            def next_bank(*reader):
                n = nb[0] % 3
                nb[0] += 1
                if bank_read[n]:
                    pe.wait_ge(*bank_read[n])
                bank_read[n] = reader
                return bank[n]

            def modulation(which):
                pe.wait_ge(dve_silu, 3)
                if which == 0:
                    pe.wait_ge(ld["first"], 16)
                else:
                    pe.wait_ge(ld_mod, 16)
                u = next_pair(setup, 2 * which + 1)
                for L, j in FIRST_MOD if which == 0 else OTHER_MOD:
                    col = (6 * L + j) * B
                    w = wmod_first if which == 0 else wmod[:, L,:]
                    last = mm(u[:, 0, col:col + B], w[:, j * C:(j + 1) * C], silu[:, 2, L * B:(L + 1) * B],
                              start=True, stop=True)
                last.then_inc(pair_full, 1)

            def gate_factors(L, half):
                dst = next_bank(factors, 2 * L + half + 1)
                pe.wait_ge(factored, 4)
                for b in range(B):
                    last = mm(dst[:, b * C:(b + 1) * C], modT[:, L, 3 * half + 2, b:b + 1].to_broadcast([P, P]),
                              ident[:], start=True, stop=True)
                last.then_inc(bank_full, 1)

            def low_rank():
                pe.wait_ge(ld["rest"], 16)
                u = next_pair(updated, 2)
                mm(u[:, 0, 0:3 * C], la_attn[:], lb_attn[:], start=True, stop=True)
                mm(u[:, 1, 0:C], la_proj[:], lb_proj[:], start=True, stop=True).then_inc(pair_full, 1)

            def turn(L, half, b):
                n = (2 * L + half) * B + b
                dst = next_bank(h_ready, n + 1)
                pe.wait_ge(ln_xn, NI * (n + 1))
                for i in range(NI):
                    last = nc.tensor.transpose(dst[:, i * P:(i + 1) * P], xn[:, b * NI + i,:], ident[:])
                last.then_inc(bank_full, 1)

            def lat(b):
                if b == 0:
                    pe.wait_ge(ld["latent"], 16)
                u = next_pair(lat_copied, b + 1)
                pe.wait_ge(h_ready, b + 1)
                for i in range(NI):
                    last = mm(u[:, 0, i * LAT:(i + 1) * LAT], hT[:, b * T + i * P:b * T + (i + 1) * P], wdkv[:],
                              start=True, stop=True)
                last.then_inc(pair_full, 1)

            def rotate_q(b):
                u = next_pair(rotated, 6 * b + 2)
                for v in range(2):
                    last = mm(u[:, v,:], wq[:, v,:], hT[:, b * T:(b + 1) * T], start=True, stop=True)
                last.then_inc(pair_full, 1)

            def lat_turn(b):
                dst = next_bank(latT_ready, b + 1)
                pe.wait_ge(latn_ready, NI * (b + 1))
                for i in range(NI):
                    last = nc.tensor.transpose(dst[0:LAT, i * P:(i + 1) * P], latn[:, i,:], ident[:])
                last.then_inc(bank_full, 1)

            def rotate_k(b):
                u = next_pair(rotated, 6 * b + 5)
                pe.wait_ge(latT_ready, b + 1)
                for v in range(2):
                    last = mm(u[:, v,:], wuk[:, v,:], latT[:], start=True, stop=True)
                last.then_inc(pair_full, 1)

            def bias_qk(b):
                if b == 0:
                    pe.wait_ge(updated, 2)
                pe.wait_ge(h_ready, 2 * B + b + 1)
                for v in range(2):
                    dst = next_bank(biased, 2 * b + v + 1)
                    mm(dst[:], wqkv[:, v * C:(v + 1) * C], hT[:, b * T:(b + 1) * T],
                       start=True, stop=True).then_inc(bank_full, 1)

            def values(L, b):
                u = next_pair(v_ready, NI * (L * B + b + 1))
                for i in range(NI):
                    dst = u[:, 0, i * C:(i + 1) * C]
                    if L == 0:
                        last = mm(dst, latT[:, i * P:(i + 1) * P], wuv[:], start=True, stop=True)
                    else:
                        last = mm(dst, hT[:, b * T + i * P:b * T + (i + 1) * P], wqkv[:, 2 * C:3 * C],
                                  start=True, stop=True)
                last.then_inc(pair_full, 1)

            def scores_q(L, s, k):
                b, g = divmod(s, NG)
                if L == s == k == 0:
                    pe.wait_ge(ld["bits"], 16)
                if k == 0:
                    pe.wait_ge(op_loaded[b % 2][g], 64 * (L * 2 + b // 2 + 1))
                u = next_pair(reduced, 7 * (L * STEPS + s) + REDUCTIONS[k])
                if k < 4:
                    pr, tiles = k // 2, ((3, 0),) if k % 2 == 0 else ((2, 0), (0, 384))
                    jobs = [(2 * pr + v, v, i, c0) for v in range(2) for i, c0 in tiles]
                else:
                    jobs = [(h, h // 2, 1, (h % 2) * 256) for h in range(GH)]
                for h, v, i, c0 in jobs:
                    head = g * GH + h
                    n = (i + 1) * P
                    mm(u[:, v, c0:c0 + n], qop[:, b % 2, head // 2, i * P:(i + 1) * P],
                       kop[:, b % 2, head, 0:n], start=True, stop=False)
                    last = mm(u[:, v, c0 + i * P:c0 + n], identb[:], mask_q[:], start=False, stop=True)
                last.then_inc(pair_full, 1)

            def max_turn(L, s):
                dst = next_bank(m_copied, L * STEPS + s + 1)
                pe.wait_ge(msplit, 4 * (L * STEPS + s + 1))
                tb = dst[0:48,:].bitcast(BF16)[:, 0:P]
                nc.tensor.transpose(tb, mparts[:, s % 2].rearrange("p a b c -> p (a b c)"), identb[:])\
                    .then_inc(bank_full, 1)

            def scores_k(L, s, k):
                b, g = divmod(s, NG)
                if k == 0:
                    pe.wait_ge(m_in[g], 32 * (L * B + b + 1))
                dst = next_bank(weights, ST_UNITS * (L * STEPS + s) + k + 1)
                pr, k2 = divmod(k, 5)
                for hh, j, c0 in PAIR_UNITS[k2]:
                    head = g * GH + 2 * pr + hh
                    n = T - j * P
                    mm(dst[:, c0:c0 + n], kop[:, b % 2, head, j * P:(j + 1) * P],
                       qop[:, b % 2, head // 2, j * P:T], start=True, stop=False)
                    last = mm(dst[:, c0:c0 + P], identb[:], mask_k[:], start=False, stop=True)
                last.then_inc(bank_full, 1)

            def weigh(L, s):
                b, g = divmod(s, NG)
                gs = L * STEPS + s
                if g == 0:
                    pe.wait_ge(v_ready, NI * (L * B + b + 1))
                if gs >= 1:
                    pe.wait_ge(pv_copied, gs)
                pe.wait_ge(weights, ST_UNITS * (gs + 1))
                where = {}
                for pr in range(2):
                    for k2, unit in enumerate(PAIR_UNITS):
                        for hh, j, c0 in unit:
                            where[2 * pr + hh, j] = ((s % 2) * ST_UNITS + 5 * pr + k2, c0)
                for j in range(NI):
                    for h in range(GH):
                        slot, c0 = where[h, j]
                        col = (g * GH + h) * VW
                        last = mm(pvb[32 * h:32 * h + 32, j * P:T], vaug[:, b * NI + j, col:col + 32],
                                  pw[:, slot, c0:c0 + T - j * P], start=(j == 0), stop=(j == NI - 1))
                last.then_inc(pv_done, 1)

            def normalise(L, s):
                gs = L * STEPS + s
                u = next_pair(o_step, 2 * (gs + 1))
                pe.wait_ge(pv_copied, gs + 1)
                for i in range(NI):
                    last = nc.tensor.transpose(u[:, 0, i * P:(i + 1) * P], oT4[:, gs % 2, i * P:(i + 1) * P],
                                               ident[:])
                last.then_inc(pair_full, 1)

            def out_turn(L, b):
                dst = next_bank(oT_ready, L * B + b + 1)
                pe.wait_ge(o_step, 2 * (L * STEPS + (b + 1) * NG))
                for i in range(NI):
                    last = nc.tensor.transpose(dst[:, i * P:(i + 1) * P], o_nat[:, b % 2, i,:], ident[:])
                last.then_inc(bank_full, 1)

            def project(L, b):
                u = next_pair(gated, 2 * L * B + b + 1)
                pe.wait_ge(oT_ready, L * B + b + 1)
                for i in range(NI):
                    dst = u[:, 0, i * C:(i + 1) * C]
                    last = mm(dst, oT[:, i * P:(i + 1) * P], wo[:, L,:], start=True, stop=(L == 0))
                    if L == 1:
                        last = mm(dst, onesf[:], bproj[:], start=False, stop=True)
                last.then_inc(pair_full, 1)

            def logits(L, b):
                if L * B + b == 0:
                    pe.wait_ge(ld["rest"], 16)
                u = next_pair(logits_read, L * B + b + 1)
                pe.wait_ge(h_ready, (2 * L + 1) * B + b + 1)
                for i in range(NI):
                    last = mm(u[:, 0, i * NE:(i + 1) * NE], hT[:, b * T + i * P:b * T + (i + 1) * P], wr[:, L,:],
                              start=True, stop=True)
                last.then_inc(pair_full, 1)

            def gate_turn(b):
                u = next_pair(gT_ready, b + 1)
                pe.wait_ge(gate_ready, b + 1)
                for i in range(NI):
                    last = nc.tensor.transpose(u[0:NE, 0, i * P:(i + 1) * P], gate[:, b * NI + i,:], ident[:])
                last.then_inc(pair_full, 1)

            def acc_start(b):
                u = next_pair(acc_started, b + 1)
                pe.wait_ge(gT_ready, b + 1)
                for i in range(NI):
                    last = mm(u[:, 0, i * C:(i + 1) * C], gT[:, i * P:(i + 1) * P], b2_0[:], start=True, stop=True)
                last.then_inc(pair_full, 1)

            def position(b):
                u = next_pair(pos_ready, b + 1)
                pe.wait_ge(chosen, 2 * (b + 1))
                for i in range(NI):
                    dst = u[:, 0, i * NE:(i + 1) * NE]
                    last = mm(dst, before[:], sel[:, b * NI + i,:], start=True, stop=(i == 0))
                    for k in range(i):
                        last = mm(dst, ones[:], sel[:, b * NI + k,:], start=False, stop=(k == i - 1))
                last.then_inc(pair_full, 1)

            def hidden(n):
                if n == 0:
                    pe.wait_ge(ld_moe, 32)
                b, e = divmod(n, NE)
                for f in range(FC[0]):
                    dst = next_bank(hidden0, FC[0] * n + f + 1)
                    mm(dst[:], w1_0[:, e, f * P:(f + 1) * P], hT[:, b * T:(b + 1) * T],
                       start=True, stop=True).then_inc(bank_full, 1)

            def outputs(n):
                b, e = divmod(n, NE)
                u = next_pair(acc_step, NI * (n + 1))
                pe.wait_ge(hidden0, FC[0] * (n + 1))
                for i in range(NI):
                    for f in range(FC[0]):
                        last = mm(u[:, 0, i * C:(i + 1) * C], pw[:, (n % 3) * FC[0] + f, i * P:(i + 1) * P],
                                  w2_0[:, e, f,:], start=(f == 0), stop=(f == FC[0] - 1))
                last.then_inc(pair_full, 1)

            def dispatch(b, k):
                dst = next_bank(buf_ready, 2 * b + k + 1)
                pe.wait_ge(xsplit, 4 * (b + 1))
                pe.wait_ge(slots_ready, NI * (b + 1))
                rows = parts[:, b % 2].rearrange("p n (i c) -> p n i c", i=NI)
                for i in range(NI):
                    for part in range(3):
                        last = mm(dst[:, 0:4 * CAPACITY], rows[:, part, i,:], slots[b % 2][:, i, 4 * k:4 * k + 4,:],
                                  start=(i + part == 0), stop=(i == NI - 1 and part == 2))
                last.then_inc(bank_full, 1)

            def slots_turn(b, i):
                dst = next_bank(slotsT_ready, NI * b + i + 1)
                tb = dst[0:CAPACITY,:].bitcast(BF16)
                for e in range(NE):
                    last = nc.tensor.transpose(tb[:, e * P:(e + 1) * P], slots[b % 2][:, i, e,:], identb[:])
                last.then_inc(bank_full, 1)

            def slot_weights(b):
                u = next_pair(slot_w_ready, b + 1)
                pe.wait_ge(gsplit, 4 * (b + 1))
                for e in range(NE):
                    for i in range(NI):
                        last = mm(u[0:CAPACITY, 0, 3 * e:3 * e + 3], slots[b % 2][:, i, e,:],
                                  gparts[:, b * NI + i, e,:], start=(i == 0), stop=(i == NI - 1))
                last.then_inc(pair_full, 1)

            def expert_hidden(e):
                pe.wait_ge(ld_exp[e % W_SLOTS], 32 * (e // W_SLOTS + 1))
                if e == 0:
                    pe.wait_ge(buf_ready, 2 * B)
                for f in range(FC[1]):
                    dst = next_bank(hidden1, FC[1] * e + f + 1)
                    mm(dst[:, 0:B * CAPACITY], w1_1[:, e % W_SLOTS, f * P:(f + 1) * P],
                       bufT[:, e].rearrange("p b n -> p (b n)"), start=True, stop=True).then_inc(bank_full, 1)

            def expert_out(e):
                dst = next_bank(yT_ready, e + 1)
                pe.wait_ge(hidden1, FC[1] * (e + 1))
                for f in range(FC[1]):
                    last = mm(dst[:, 0:B * CAPACITY], w2_1[:, e % W_SLOTS, f,:], hid1[:, e % 2, f,:],
                              start=(f == 0), stop=(f == FC[1] - 1))
                last.then_inc(bank_full, 1)

            def expert_turn(e):
                if e == 0:
                    pe.wait_ge(pv_copied, LAYERS * STEPS)
                else:
                    pe.wait_ge(y_split, 5 * (e - 1) + 1)
                pe.wait_ge(yT_ready, e + 1)
                for b in range(B):
                    last = nc.tensor.transpose(pvb[0:CAPACITY, b * C:(b + 1) * C],
                                               oT4[:, e % 2, b * CAPACITY:(b + 1) * CAPACITY], ident[:])
                last.then_inc(y_turned, 1)

            def combine(e):
                if e == 0:
                    for reader in pair_read:
                        pe.wait_ge(*reader)
                    pe.wait_ge(slotsT_ready, NI * B)
                pe.wait_ge(y_split, 5 * (e + 1))
                for b in range(B):
                    for i in range(NI):
                        for part in range(3):
                            last = mm(pair[b // 2][:, b % 2, i * C:(i + 1) * C], slotsT[b][:, e, i * P:(i + 1) * P],
                                      parts[0:CAPACITY, e % 2, part, b * C:(b + 1) * C],
                                      start=(e + i + part == 0), stop=(e == NE - 1 and part == 2),
                                      skip_group_check=True)
                    if e == NE - 1:
                        last.then_inc(summed, 1)

            work = dict(modulation=modulation, gate_factors=gate_factors, low_rank=low_rank, turn=turn, lat=lat,
                        rotate_q=rotate_q, lat_turn=lat_turn, rotate_k=rotate_k, bias_qk=bias_qk, values=values,
                        scores_q=scores_q, max_turn=max_turn, scores_k=scores_k, weigh=weigh, normalise=normalise,
                        out_turn=out_turn, project=project, logits=logits, gate_turn=gate_turn,
                        acc_start=acc_start, position=position, hidden=hidden, outputs=outputs,
                        dispatch=dispatch, slots_turn=slots_turn, slot_weights=slot_weights,
                        expert_hidden=expert_hidden, expert_out=expert_out, expert_turn=expert_turn, combine=combine)
            for name, *at in ORDER:
                if name in work:
                    work[name](*at)

        @block.vector
        def _(v):
            V = nc.vector
            npair = [0]

            def next_pair():
                n = npair[0]
                npair[0] += 1
                v.wait_ge(pair_full, n + 1)
                return pair[n % 2]

            def tiles_of(b):
                return slice(b * NI, (b + 1) * NI)

            def silus():
                v.wait_ge(act_silu, 1)
                V.tensor_scalar(silu[:, 1,:], silu[:, 0,:], 1.0, None, ALU.add).then_inc(dve_silu, 1)
                v.wait_ge(dve_silu, 1)
                V.reciprocal(silu[:, 0,:], silu[:, 1,:]).then_inc(dve_silu, 1)
                v.wait_ge(dve_silu, 2)
                V.tensor_tensor(silu[:, 2,:], cT[:], silu[:, 0,:], ALU.mult).then_inc(dve_silu, 1)

            def modulation(which):
                u = next_pair()
                for L, j0, j1 in ((0, 0, 2),) if which == 0 else ((0, 2, 6), (1, 0, 6)):
                    V.tensor_copy(modT[:, L, j0:j1,:],
                                  u[:, 0, (6 * L + j0) * B:(6 * L + j1) * B].rearrange("p (j b) -> p j b", b=B))\
                        .then_inc(copied, 1)
                if which == 0:
                    v.wait_ge(copied, 1)
                    V.tensor_scalar(modT[:, 0, 1,:], modT[:, 0, 1,:], 1.0, None, ALU.add).then_inc(setup, 1)
                else:
                    v.wait_ge(copied, 3)
                    V.tensor_scalar(modT[:, 0, 4,:], modT[:, 0, 4,:], 1.0, None, ALU.add).then_inc(setup, 1)
                    V.tensor_scalar(modT[:, 1, 1::3,:], modT[:, 1, 1::3,:], 1.0, None, ALU.add).then_inc(setup, 1)
                    g, sign, size = modT[:,:, 2::3,:], gsign[:], gsize[:]
                    V.tensor_scalar(sign, g, 0.0, 2.0, ALU.is_ge, ALU.mult).then_inc(factored, 1)
                    v.wait_ge(factored, 1)
                    V.scalar_tensor_tensor(out=size, in0=sign, scalar=-1.0, in1=g,
                                           op0=ALU.add, op1=ALU.mult).then_inc(factored, 1)
                    v.wait_ge(factored, 2)
                    V.tensor_scalar(size, size, 0.25, None, ALU.max).then_inc(factored, 1)
                    v.wait_ge(factored, 3)
                    V.scalar_tensor_tensor(out=g, in0=sign, scalar=-1.0, in1=size,
                                           op0=ALU.add, op1=ALU.mult).then_inc(factored, 1)

            def clear_first():
                V.memset(kop[:, 0,:,:], 0.0).then_inc(cleared, 1)

            def low_rank():
                u = next_pair()
                v.wait_ge(ld["rest"], 16)
                V.scalar_tensor_tensor(out=wqkv[:], in0=u[:, 0, 0:3 * C], scalar=0.5, in1=wqkv[:],
                                       op0=ALU.mult, op1=ALU.add).then_inc(updated, 1)
                V.scalar_tensor_tensor(out=wo[:, 1,:], in0=u[:, 1, 0:C], scalar=0.5, in1=wo[:, 1,:],
                                       op0=ALU.mult, op1=ALU.add).then_inc(updated, 1)

            def stat(L, half, b):
                n = (2 * L + half) * B + b
                if n < B:
                    v.wait_ge(ld_x[b], 16)
                else:
                    v.wait_ge(x_done, n - B + 1)
                    v.wait_ge(ln_xn, NI * (n - B + 1))
                for i in range(NI):
                    V.bn_stats(stats[:, b, i,:], x[:, b * NI + i,:]).then_inc(ln_stat, 1)
                for i in range(NI):
                    v.wait_ge(ln_stat, NI * n + i + 1)
                    V.bn_aggr(mv[:, b, i,:], stats[:, b, i,:]).then_inc(ln_mv, 1)

            def norm(L, half, b):
                n = (2 * L + half) * B + b
                v.wait_ge(ln_mv, NI * (n + 1))
                v.wait_ge(ln_rstd, n + 1)
                for i in range(NI):
                    t = b * NI + i
                    V.tensor_scalar(xn[:, t,:], x[:, t,:], mv[:, b, i, 0:1], rstd[:, b, i:i + 1],
                                    ALU.subtract, ALU.mult).then_inc(ln_xn, 1)

            def lat(b):
                u = next_pair()
                if b:
                    v.wait_ge(latn_ready, NI * b)
                V.tensor_copy(latc[:], u[:, 0, 0:NI * LAT].rearrange("p (i c) -> p i c", i=NI))\
                    .then_inc(lat_copied, 1)
                v.wait_ge(lat_copied, b + 1)
                for i in range(NI):
                    V.bn_stats(lstats[:, i,:], latc[:, i,:]).then_inc(lat_stat, 1)
                for i in range(NI):
                    v.wait_ge(lat_stat, NI * b + i + 1)
                    V.bn_aggr(lmv[:, i,:], lstats[:, i,:]).then_inc(lat_mv, 1)

            def lat_norm(b):
                v.wait_ge(lat_mv, NI * (b + 1))
                v.wait_ge(lat_rstd, b + 1)
                if b:
                    v.wait_ge(latT_ready, b)
                for i in range(NI):
                    V.tensor_scalar(latn[:, i,:], latc[:, i,:], lmv[:, i, 0:1], lrstd[:, i:i + 1],
                                    ALU.subtract, ALU.mult).then_inc(latn_ready, 1)

            def split_part(L, b, n, k):
                if k % 2 == 0 or n == 1 and b > 0:
                    return
                base = 4 * (L * B + b)
                v.wait_ge(split[n], base + k)
                if k == 1:
                    V.tensor_tensor(rot[:, n,:], full[:, n,:], parts[:, n, 0,:], ALU.subtract).then_inc(split[n], 1)
                else:
                    V.tensor_tensor(parts[:, n, 2,:], rot[:, n,:], parts[:, n, 1,:], ALU.subtract)\
                        .then_inc(split[n], 1)

            def rotate(b, n):
                u = next_pair()
                done = 6 * b + 3 * n
                if b:
                    v.wait_ge(split[n], 4 * b)
                if b == n == 0:
                    v.wait_ge(ld["rope"], 16)
                V.tensor_tensor(full[:, n,:], u[:, 0,:], cosT[:], ALU.mult).then_inc(rotated, 1)
                V.tensor_tensor(rot[:, n,:], u[:, 1,:], sinT[:], ALU.mult).then_inc(rotated, 1)
                v.wait_ge(rotated, done + 2)
                V.tensor_tensor(full[:, n,:], full[:, n,:], rot[:, n,:], ALU.add).then_inc(rotated, 1)

            def rotate_q(b):
                rotate(b, 0)

            def rotate_k(b):
                rotate(b, 1)

            def values(L, b):
                u = next_pair()
                if L * B + b == 0:
                    v.wait_ge(pool_init, 3)
                dst = vaug[:, tiles_of(b), 0:NH * VW].rearrange("p i (h k) -> p i h k", k=VW)[:,:,:, 0:HD]
                src = u[:, 0,:].rearrange("p (i h k) -> p i h k", i=NI, h=NH)
                for i in range(NI):
                    if L == 0:
                        V.tensor_copy(dst[:, i], src[:, i]).then_inc(v_ready, 1)
                    else:
                        V.tensor_tensor(dst[:, i], src[:, i], bv[:].rearrange("p (h k) -> p h k", k=HD), ALU.add)\
                            .then_inc(v_ready, 1)

            def scores_q(L, s, k):
                u = next_pair()
                gs = L * STEPS + s
                nm = negmax[:, s % 2]
                if k == 0 and gs >= 2:
                    v.wait_ge(msplit, 4 * (gs - 1))
                pr = k // 2
                if k == 4:
                    V.tensor_reduce(nm[:,:,:, 1], u[:].rearrange("p j (r n) -> p r j n", r=2), AX, ALU.max,
                                    negate=True).then_inc(reduced, 1)
                    split_max(gs)
                elif k % 2 == 0:
                    V.tensor_reduce(nm[:,:, pr, 3], u[:], AX, ALU.max, negate=True).then_inc(reduced, 1)
                else:
                    V.tensor_reduce(nm[:,:, pr, 2], u[:,:, 0:384], AX, ALU.max, negate=True)\
                        .then_inc(reduced, 1)
                    V.tensor_reduce(nm[:,:, pr, 0], u[:,:, 384:512], AX, ALU.max, negate=True)\
                        .then_inc(reduced, 1)

            def split_max(gs):
                v.wait_ge(reduced, 7 * (gs + 1))
                src, dst = negmax[:, gs % 2].rearrange("p r j i -> p r (j i)"), mparts[:, gs % 2]
                V.tensor_copy(dst[:,:, 0,:], src).then_inc(msplit, 1)
                v.wait_ge(msplit, 4 * gs + 1)
                V.tensor_tensor(mres[:], src, dst[:,:, 0,:], ALU.subtract).then_inc(msplit, 1)
                v.wait_ge(msplit, 4 * gs + 2)
                V.tensor_copy(dst[:,:, 1,:], mres[:]).then_inc(msplit, 1)
                v.wait_ge(msplit, 4 * gs + 3)
                V.tensor_tensor(dst[:,:, 2,:], mres[:], dst[:,:, 1,:], ALU.subtract).then_inc(msplit, 1)

            def normalise(L, s):
                gs = L * STEPS + s
                b, g = divmod(s, NG)
                u = next_pair()
                uv = u[:, 0,:].rearrange("p (i h k) -> p i h k", i=NI, h=GH)
                if gs:
                    v.wait_ge(o_step, 2 * gs)
                V.reciprocal(rec[:], uv[:,:,:, HD]).then_inc(o_step, 1)
                v.wait_ge(o_step, 2 * gs + 1)
                dst = o_nat[:, b % 2,:, g * GH * HD:(g + 1) * GH * HD].rearrange("p i (h k) -> p i h k", h=GH)
                V.tensor_tensor(dst, uv[:,:,:, 0:HD], rec[:].unsqueeze(3).to_broadcast([P, NI, GH, HD]),
                                ALU.mult).then_inc(o_step, 1)

            def residual(src, L, half, b):
                n = (2 * L + half) * B + b + 1
                gb = gates[:, L * B + b, half,:].unsqueeze(1).to_broadcast([P, NI, C])
                if b == 0:
                    v.wait_ge(factors, 2 * L + half + 1)
                if n > 1:
                    v.wait_ge(x_done, n - 1)
                V.tensor_tensor(upd[:], src, gb, ALU.mult).then_inc(gated, 1)
                v.wait_ge(gated, n)
                xb = x[:, tiles_of(b),:]
                V.tensor_tensor(xb, xb, upd[:], ALU.add).then_inc(x_done, 1)

            def project(L, b):
                residual(next_pair()[:, 0,:].rearrange("p (i c) -> p i c", i=NI), L, 0, b)

            def logits(L, b):
                ts = tiles_of(b)
                u = next_pair()
                lgp = u[:, 0, 0:NI * NE].rearrange("p (t e) -> p t e", e=NE)
                if L == 0:
                    if b == 0:
                        v.wait_ge(ld["rest"], 16)
                    V.tensor_tensor(lg[:, ts,:], lgp, br[:].unsqueeze(1).to_broadcast([P, NI, NE]), ALU.add)\
                        .then_inc(logits_read, 1)
                    v.wait_ge(logits_read, b + 1)
                    top_two(b)
                    V.tensor_tensor(wk[:, 0, ts], top[:, ts, 1], top[:, ts, 0], ALU.subtract).then_inc(exp_in, 1)
                else:
                    V.tensor_copy(lg[:, ts,:], lgp).then_inc(logits_read, 1)
                    v.wait_ge(logits_read, B + b + 1)
                    r(V.tensor_reduce(wk[:, 0, ts], lg[:, ts,:], AX, ALU.max))
                    V.tensor_tensor(lgs[:, ts,:], lg[:, ts,:], bc(wk[:, 0, ts]), ALU.subtract)\
                        .then_inc(exp_in, 1)

            nroute = [0]

            def r(ins):
                nroute[0] += 1
                ins.then_inc(route_step, 1)
                v.wait_ge(route_step, nroute[0])

            def bc(col):
                return col.unsqueeze(2).to_broadcast([P, NI, NE])

            def top_two(b):
                for t in range(b * NI, (b + 1) * NI):
                    V.max(top[:, t,:], lg[:, t,:]).then_inc(route_step, 1)
                for t in range(b * NI, (b + 1) * NI):
                    nroute[0] += 1
                    v.wait_ge(route_step, nroute[0])
                    V.max_index(topi[:, t,:], top[:, t,:], lg[:, t,:]).then_inc(route_step, 1)
                nroute[0] += NI
                v.wait_ge(route_step, nroute[0])
                r(V.tensor_copy(topf[:, tiles_of(b)], topi[:, tiles_of(b), 0:2]))

            def route(L, b):
                ts = tiles_of(b)
                v.wait_ge(exp_out, L * B + b + 1)
                if L == 0:
                    r(V.tensor_scalar(wk[:, 0, ts], wk[:, 1, ts], 1.0, None, ALU.add))
                    r(V.reciprocal(wk[:, 2, ts], wk[:, 0, ts]))
                    r(V.tensor_tensor(wk[:, 3, ts], wk[:, 1, ts], wk[:, 2, ts], ALU.mult))
                else:
                    r(V.tensor_reduce(wk[:, 1, ts], ex[:, ts,:], AX, ALU.add))
                    r(V.reciprocal(wk[:, 2, ts], wk[:, 1, ts]))
                    r(V.tensor_tensor(lg[:, ts,:], ex[:, ts,:], bc(wk[:, 2, ts]), ALU.mult))
                    top_two(b)

            def gates_of(L, b):
                ts = tiles_of(b)
                wts = (wk[:, 2, ts], wk[:, 3, ts]) if L == 0 else (top[:, ts, 0], top[:, ts, 1])
                for k in range(2):
                    r(V.tensor_tensor(oh[:, k, ts], iota8[:].unsqueeze(1).to_broadcast([P, NI, NE]),
                                      bc(topf[:, ts, k]), ALU.is_equal))
                if L == 1:
                    V.tensor_tensor(sel[:, ts], oh[:, 0, ts], oh[:, 1, ts], ALU.add).then_inc(chosen, 1)
                    v.wait_ge(chosen, 2 * b + 1)
                    V.tensor_scalar(away[:, ts], sel[:, ts], -FAR, FAR, ALU.mult, ALU.add).then_inc(chosen, 1)
                for k in range(2):
                    r(V.tensor_tensor(oh[:, k, ts], oh[:, k, ts], bc(wts[k]), ALU.mult))
                V.tensor_tensor(gate[:, ts], oh[:, 0, ts], oh[:, 1, ts], ALU.add).then_inc(gate_ready, 1)

            def gate_turn(b):
                u = next_pair()
                if b:
                    v.wait_ge(acc_started, b)
                V.tensor_copy(gT[:], u[0:NE, 0,:]).then_inc(gT_ready, 1)

            def acc_start(b):
                u = next_pair()
                V.tensor_copy(acc[:, tiles_of(b),:], u[:, 0,:].rearrange("p (t c) -> p t c", t=NI))\
                    .then_inc(acc_started, 1)

            def position(b):
                u = next_pair()
                v.wait_ge(chosen, 2 * (b + 1))
                V.tensor_tensor(pos[:, tiles_of(b)], u[:, 0, 0:NI * NE].rearrange("p (t e) -> p t e", e=NE),
                                away[:, tiles_of(b)], ALU.add).then_inc(pos_ready, 1)

            def outputs(n):
                b, e = divmod(n, NE)
                u = next_pair()
                if e == 0:
                    v.wait_ge(gate_ready, b + 1)
                    v.wait_ge(acc_started, b + 1)
                for i in range(NI):
                    t = b * NI + i
                    if e:
                        v.wait_ge(acc_step, NI * (n - 1) + i + 1)
                    V.scalar_tensor_tensor(out=acc[:, t,:], in0=u[:, 0, i * C:(i + 1) * C],
                                           scalar=gate[:, t, e:e + 1], in1=acc[:, t,:],
                                           op0=ALU.mult, op1=ALU.add).then_inc(acc_step, 1)

            def gate_residual(b):
                v.wait_ge(acc_step, NI * NE * (b + 1))
                residual(acc[:, tiles_of(b),:], 0, 1, b)

            def split_gates(b):
                ts = tiles_of(b)
                v.wait_ge(gate_ready, B + b + 1)
                if b:
                    v.wait_ge(gsplit, 4 * b)
                V.tensor_copy(gparts[:, ts,:, 0], gate[:, ts]).then_inc(gsplit, 1)
                v.wait_ge(gsplit, 4 * b + 1)
                V.tensor_tensor(gres[:], gate[:, ts], gparts[:, ts,:, 0], ALU.subtract).then_inc(gsplit, 1)
                v.wait_ge(gsplit, 4 * b + 2)
                V.tensor_copy(gparts[:, ts,:, 1], gres[:]).then_inc(gsplit, 1)
                v.wait_ge(gsplit, 4 * b + 3)
                V.tensor_tensor(gparts[:, ts,:, 2], gres[:], gparts[:, ts,:, 1], ALU.subtract)\
                    .then_inc(gsplit, 1)

            def split_rows(b):
                v.wait_ge(ln_xn, NI * (3 * B + b + 1))
                if b < 2:
                    v.wait_ge(scr_done[b][B - 1], 96 * LAYERS)
                    v.wait_ge(split[b], 4 * LAYERS * B)
                else:
                    v.wait_ge(buf_ready, 2 * (b - 1))
                    v.wait_ge(xsplit, 4 * (b - 1))
                src = xn[:, tiles_of(b),:].rearrange("p i c -> p (i c)")
                dst, res = parts[:, b % 2], rot[:, b % 2,:]
                V.tensor_copy(dst[:, 0,:], src).then_inc(xsplit, 1)
                v.wait_ge(xsplit, 4 * b + 1)
                V.tensor_tensor(res, src, dst[:, 0,:], ALU.subtract).then_inc(xsplit, 1)
                v.wait_ge(xsplit, 4 * b + 2)
                V.tensor_copy(dst[:, 1,:], res).then_inc(xsplit, 1)
                v.wait_ge(xsplit, 4 * b + 3)
                V.tensor_tensor(dst[:, 2,:], res, dst[:, 1,:], ALU.subtract).then_inc(xsplit, 1)

            def fill_slots(b):
                v.wait_ge(pos_ready, b + 1)
                if b == 0:
                    v.wait_ge(pv_done, STEPS + (B - 1) * NG)
                elif b > 1:
                    v.wait_ge(slot_w_ready, b - 1)
                for i in range(NI):
                    V.tensor_tensor(slots[b % 2][:, i], iota_s[:].unsqueeze(1).to_broadcast([P, NE, CAPACITY]),
                                    pos[:, b * NI + i,:].unsqueeze(2).to_broadcast([P, NE, CAPACITY]),
                                    ALU.is_equal).then_inc(slots_ready, 1)

            def slot_weights(b):
                u = next_pair()
                V.tensor_reduce(slot_w[0:CAPACITY,:, b], u[0:CAPACITY, 0, 0:3 * NE].rearrange("p (e k) -> p e k", e=NE),
                                AX, ALU.add).then_inc(slot_w_ready, 1)

            def expert_turn(e):
                v.wait_ge(y_turned, e + 1)
                if e == 0:
                    v.wait_ge(slot_w_ready, B)
                    v.wait_ge(xsplit, 4 * B)
                else:
                    v.wait_ge(y_split, 5 * e)
                y, res, dst = full[0:CAPACITY, 0,:], rot[0:CAPACITY, 0,:], parts[0:CAPACITY, e % 2]
                V.tensor_tensor(y.rearrange("p (b c) -> p b c", b=B),
                                pvb[0:CAPACITY,:].rearrange("p (b c) -> p b c", b=B),
                                slot_w[0:CAPACITY, e,:].unsqueeze(2).to_broadcast([CAPACITY, B, C]), ALU.mult)\
                    .then_inc(y_split, 1)
                v.wait_ge(y_split, 5 * e + 1)
                V.tensor_copy(dst[:, 0,:], y).then_inc(y_split, 1)
                v.wait_ge(y_split, 5 * e + 2)
                V.tensor_tensor(res, y, dst[:, 0,:], ALU.subtract).then_inc(y_split, 1)
                v.wait_ge(y_split, 5 * e + 3)
                V.tensor_copy(dst[:, 1,:], res).then_inc(y_split, 1)
                v.wait_ge(y_split, 5 * e + 4)
                V.tensor_tensor(dst[:, 2,:], res, dst[:, 1,:], ALU.subtract).then_inc(y_split, 1)

            def finish(b):
                v.wait_ge(summed, b + 1)
                residual(pair[b // 2][:, b % 2,:].rearrange("p (i c) -> p i c", i=NI), 1, 1, b)

            work = dict(silus=silus, modulation=modulation, clear_first=clear_first, 
                        low_rank=low_rank, stat=stat, norm=norm, lat=lat, rotate_q=rotate_q, lat_norm=lat_norm,
                        rotate_k=rotate_k, split_part=split_part, values=values, scores_q=scores_q, normalise=normalise,
                        project=project, logits=logits, route=route, gates=gates_of,
                        gate_turn=gate_turn, acc_start=acc_start, position=position, outputs=outputs,
                        gate_residual=gate_residual, split_gates=split_gates, split_rows=split_rows,
                        fill_slots=fill_slots, slot_weights=slot_weights, expert_turn=expert_turn, finish=finish)
            for name, *at in ORDER:
                if name in work:
                    work[name](*at)


def with_extras(base, extras):
    out, k = [], 0
    for n, stage in enumerate(base):
        out.append(stage)
        upto = len(extras) * (n + 1) // len(base)
        out += extras[k:upto]
        k = upto
    return out


SPACE = ("space",)


def norm_stages(L, half, b):
    return [("stat", L, half, b), SPACE, ("norm", L, half, b), SPACE, ("turn", L, half, b)]


def split_stages(L, b, n):
    return [("split_part", L, b, n, k) for k in range(4)]


def input_stages(L, b):
    if L == 0:
        queries, keys = split_stages(L, b, 0), split_stages(L, b, 1)
        return [("lat", b), ("lat_norm", b), ("rotate_q", b), ("lat_turn", b)] + queries + \
               [("rotate_k", b)] + keys + [("values", L, b)]
    queries, keys = split_stages(L, b, 0), split_stages(L, b, 1)
    return [("bias_qk", b)] + [stage for two in zip(queries, keys) for stage in two] + [("values", L, b)]


def routing_stages(L, b):
    out = norm_stages(L, 1, b) + [("logits", L, b), ("route_exp", L, b), ("route", L, b), ("gates", L, b)]
    return out + ([("gate_turn", b), ("acc_start", b)] if L == 0 else [("position", b)])


LEAD = 3


def attention_step(L, s, extras):
    base = []
    later = {1: 0, 3: 1, 5: 2, 7: 3, 9: 4}
    for u in range(ST_UNITS):
        base.append(("scores_k", L, s, u))
        if u in later and s + LEAD < STEPS:
            base.append(("scores_q", L, s + LEAD, later[u]))
        if u == 4 and s + LEAD - 1 < STEPS:
            base.append(("max_turn", L, s + LEAD - 1))
        if s and u == 3:
            base.append(("weigh", L, s - 1))
        if s and u == 4:
            base.append(("weigh_copy", L, s - 1))
        if s and u == 6:
            base.append(("normalise", L, s - 1))
    return with_extras(base, extras)


def first_scores(L):
    out = []
    for s in range(LEAD):
        out += [("scores_q", L, s, k) for k in range(5)]
        if s:
            out.append(("max_turn", L, s - 1))
    return out


def attention_stages(L, more):
    out = []
    pending = []
    for s in range(STEPS):
        extras = list(more.get(s, []))
        b, r = divmod(s, NG)
        if b:
            done = routing_stages(L, b - 1)
            extras = {0: [], 1: [("out_turn", L, b - 1), ("project", L, b - 1)] + done[:2], 2: done[2:7],
                      3: done[7:]}[r] + extras
        out += attention_step(L, s, extras)
    return out


def tail_stages(L):
    return ([("weigh", L, STEPS - 1), ("weigh_copy", L, STEPS - 1)],
            [("normalise", L, STEPS - 1), ("out_turn", L, B - 1), ("project", L, B - 1)] + routing_stages(L, B - 1))


def order():
    n = [norm_stages(0, 0, b) for b in range(B)]
    out = [("silus",)] + n[0][:1] + [("modulation", 0), ("clear", 0)] + n[0][1:] + n[1][:1] + [("clear_first",)]
    one, two = input_stages(0, 0), input_stages(0, 1)
    out += one[:9] + n[1][1:3] + one[9:] + n[1][3:] + [("clear", 1)] + two[:3] + [("clear", 2)]
    out += [("modulation", 1)] + with_extras(first_scores(0), two[3:] + [stage for both in zip(n[2], n[3]) for stage in both if stage != SPACE])
    factors = [[("gate_factors", L, half) for half in range(2)] for L in range(LAYERS)]
    two, three = input_stages(0, 2), input_stages(0, 3)
    out += attention_stages(0, {0: two[:5], 1: two[5:10], 2: two[10:], 3: factors[0], 4: three[:5], 5: three[5:10],
                                6: three[10:], 7: factors[1] + [("low_rank",)]})
    now, tail = tail_stages(0)
    out += now
    groups = []
    for b in range(B):
        for e in range(NE):
            nth = b * NE + e
            if nth == 0:
                groups.append([("hidden", 0)])
            groups.append(([("hidden", nth + 1)] if nth + 1 < B * NE else []) + [("outputs", nth)])
    flat = groups[0]
    g = groups[1:]
    later = [[("gate_residual", b)] + norm_stages(1, 0, b) + input_stages(1, b) for b in range(B)]
    flat += sum(with_extras(g[0:NE], [[t] for t in tail]), [])
    flat += sum(with_extras(g[NE:2 * NE], [[t] for t in later[0]]), [])
    first = first_scores(1)
    cut = len(first) // 3
    flat += sum(with_extras(g[2 * NE:3 * NE], [[t] for t in later[1][:8] + with_extras(first[:cut], later[1][8:])]), [])
    flat += sum(with_extras(g[3 * NE:], [[t] for t in with_extras(first[cut:], later[2])]), [])
    out += flat
    def prepare(b):
        return [("split_gates", b), ("split_rows", b), ("fill_slots", b)]

    def dispatch(b):
        return [("dispatch", b, 0), ("dispatch", b, 1)] + [("slots_turn", b, i) for i in range(NI)] + \
               [("slot_weights", b)]

    out += attention_stages(1, {0: later[3][:6], 1: later[3][6:11], 2: later[3][11:],
                                13: prepare(0)[:2], 14: prepare(0)[2:] + prepare(1)[:2], 15: prepare(1)[2:]})
    now, tail = tail_stages(1)
    two, three = prepare(2), prepare(3)
    extras = tail[:4] + two[:1] + tail[4:6] + two[1:2] + tail[6:9] + two[2:] + tail[9:-1]
    out += now + with_extras(dispatch(0) + dispatch(1), extras)
    last = dispatch(2)
    out += last[:1] + tail[-1:] + three + last[1:] + dispatch(3)
    out += [("expert_hidden", 0), ("expert_out", 0), ("expert_hidden", 1)]
    for e in range(NE):
        if e + 1 < NE:
            out += [("expert_turn", e), ("expert_out", e + 1)]
        if e + 2 < NE:
            out.append(("expert_hidden", e + 2))
        if e == NE - 2:
            out.append(("expert_turn", NE - 1))
        out.append(("combine", e))
    return out + [("finish", b) for b in range(B)]


ORDER = order()


def kernel(**inputs):
    import ml_dtypes
    import concourse.bacc as bacc
    from concourse.bass_utils import run_bass_kernel_spmd

    f32, bf = np.float32, ml_dtypes.bfloat16
    ins = {k: np.ascontiguousarray(inputs[k]) for k in inputs}

    arrays = {k: ins[k] for k in ("L0_attn_x", "L0_ffn_W1", "L0_ffn_W2", "L1_ffn_W1", "L1_ffn_W2")}
    arrays["wmod"] = np.stack([ins["L0_wmod"], ins["L1_wmod"]], 1)
    swap = np.arange(C).reshape(NH, 2, HD // 2)[:,::-1].reshape(C)

    def beside(*parts):
        return np.concatenate(parts, 1)

    items = dict(
        cT=np.concatenate([ins["L0_c"], ins["L1_c"]]).T, wmod_first=ins["L0_wmod"][:,:2 * C],
        wq=beside(ins["L0_attn_W_q"], ins["L0_attn_W_q"][:, swap]), wdkv=ins["L0_attn_W_dkv"],
        wuk=beside(ins["L0_attn_W_uk"], ins["L0_attn_W_uk"][:, swap]), wuv=ins["L0_attn_W_uv"],
        lnlat=np.stack([ins["L0_attn_ln_gamma"], ins["L0_attn_ln_beta"]], 1),
        wqkv=ins["L1_attn_w_attn"].T, la_attn=ins["L1_attn_la_attn"], lb_attn=ins["L1_attn_lb_attn"].T,
        la_proj=ins["L1_attn_la_proj"], lb_proj=ins["L1_attn_lb_proj"].T,
        bqk=ins["L1_attn_b_attn"][:2 * C].reshape(2, C).T,
        bv=np.broadcast_to(ins["L1_attn_b_attn"][2 * C:], (P, C)), bproj=ins["L1_attn_b_proj"].reshape(1, C),
        wo=beside(ins["L0_attn_W_o"], ins["L1_attn_w_proj"].T), wr=beside(ins["L0_ffn_Wr"], ins["L1_ffn_Wr"]),
        br=np.broadcast_to(ins["L0_ffn_br"], (P, NE)), b2_0=ins["L0_ffn_b2"], b2_1=ins["L1_ffn_b2"].T)
    for L in range(LAYERS):
        items[f"b1_{L}"] = ins[f"L{L}_ffn_b1"].reshape(NE, FC[L], P).transpose(2, 0, 1).reshape(P, NE * FC[L])

    row, col = np.arange(P)[:, None], np.arange(P)[None,:]
    items["ident"] = np.eye(P, dtype=f32)
    items["identb"] = np.eye(P, dtype=f32).astype(bf)
    items["mask_q"] = np.where(col > row, MASKED, 0).astype(bf)
    items["mask_k"] = np.where(row > col, MASKED, 0).astype(bf)
    items["before"] = (row < col).astype(bf)
    items["ones"] = np.ones((P, P), bf)
    items["iota8"] = np.repeat(np.arange(NE, dtype=f32)[None], P, 0)
    items["iota_s"] = np.repeat(np.arange(CAPACITY, dtype=f32)[None], P, 0)
    half = HD // 2
    inv_freq = (f32(1.0) / f32(10000.0) ** (np.arange(half, dtype=f32) / f32(half))).astype(f32)
    angles = (inv_freq[:, None] * np.arange(T, dtype=f32)[None]).astype(f32)
    cos, sin = np.cos(angles), np.sin(angles)
    items["cosT"] = np.tile(cos, (C // half, 1)).astype(f32)
    items["sinT"] = np.tile(np.concatenate([-sin, sin]), (NH, 1)).astype(f32)

    rows = HALF - MAX_ROW
    arrays["zeros"] = np.zeros((B, NH, 3, T), bf)
    arrays["tail_q"] = np.zeros((rows, 2, NH // 2, T), bf)
    arrays["tail_k"] = np.repeat((np.arange(rows) < 3), NH // 2 * T).reshape(rows, NH // 2, T).astype(bf)

    for pack, names in PACKS.items():
        arrays[pack] = np.zeros((P, sum(n for _, n, _ in names)), bf if pack == "bits" else f32)
        at = 0
        for name, n, used in names:
            arrays[pack][:used, at:at + n] = items[name]
            at += n

    nc = bacc.Bacc("TRN2", target_bir_lowering=False, num_devices=1)
    arrays = {k: np.ascontiguousarray(x) for k, x in arrays.items()}
    aps = {k: nc.dram_tensor(f"in_{k}", x.shape, mybir.dt.from_np(x.dtype), kind="ExternalInput").ap()
           for k, x in arrays.items()}
    out = nc.dram_tensor("out_0", (B, T, C), F32, kind="ExternalOutput").ap()
    build(nc, aps, out)
    r = run_bass_kernel_spmd(nc, [{f"in_{k}": x for k, x in arrays.items()}], core_ids=[0])
    return r.results[0]["out_0"]
```
